# Optimizing a Trainium2 kernel written in Bass

```python
import numpy as np
import jax
import jax.numpy as jnp

def _softmax(x, axis=-1):
    return jax.nn.softmax(x, axis=axis)

def _gelu(x):
    return jax.nn.gelu(x, approximate=True)

def _silu(x):
    return jax.nn.silu(x)

def _sigmoid(x):
    return jax.nn.sigmoid(x)

def _layernorm(x, axis=-1, eps=1e-05):
    m = jnp.mean(x, axis=axis, keepdims=True)
    v = jnp.var(x, axis=axis, keepdims=True)
    return (x - m) / jnp.sqrt(v + eps)

def _scatter_add(tgt, idx, src, axis=0):
    return tgt.at[idx].add(src)

def _segment_sum(src, seg, n):
    return jax.ops.segment_sum(src, seg, n)
kernel_name = 'mk_xattn_ffn_d1_seqx_r4_8a6e81'

def setup_inputs(seed: int=0):
    np.random.seed(seed)
    _w = jnp.asarray

    def _rec_inputs():
        import jax
        import jax.numpy as jnp
        _rk = jax.random.key(seed)
        x = -0.000125 + 0.9999 * jax.random.normal(jax.random.fold_in(_rk, 1), (16, 256, 256), jnp.float32)
        _lenS = 256 - jax.random.randint(jax.random.fold_in(_rk, 7), (16,), 0, max(1, 256 // 4) + 1, jnp.int32)
        _lenS2 = 77 - jax.random.randint(jax.random.fold_in(_rk, 8), (16,), 0, max(1, 77 // 4) + 1, jnp.int32)
        _ctx_768P = jax.random.normal(jax.random.fold_in(_rk, 11), (16, 16, 192), jnp.float32)
        _ctx_768c = jax.random.dirichlet(jax.random.fold_in(_rk, 511), 0.3 * jnp.ones((16,), jnp.float32), (16, 77))
        _ctx_768t = jnp.einsum('bsk,bkd->bsd', _ctx_768c, _ctx_768P)
        _ctx_768t = _ctx_768t * jax.lax.rsqrt(jnp.mean(jnp.square(_ctx_768t)) + 1e-12) * 0.953939
        ctx_768 = 0.00272024 + 0.999456 * (_ctx_768t + 0.3 * jax.random.normal(jax.random.fold_in(_rk, 611), (16, 77, 192), jnp.float32))
        return (x, ctx_768)
    x, ctx_768 = _rec_inputs()

    def _L0_xattn_setup():
        import jax, jax.numpy as jnp
        import numpy as np
        QUERY_DIM = 256
        CONTEXT_DIM = 192
        HEADS = 8
        DIM_HEAD = 64
        INNER = HEADS * DIM_HEAD
        key = jax.random.key(seed)
        ks = jax.random.split(key, 7)
        B, S, L = (8, 1024, 77)
        x = jax.random.normal(ks[0], (B, S, QUERY_DIM), dtype=jnp.float32)
        context = jax.random.normal(ks[1], (B, L, CONTEXT_DIM), dtype=jnp.float32)
        Wq = jax.random.normal(ks[2], (QUERY_DIM, INNER), dtype=jnp.float32) * QUERY_DIM ** (-0.5)
        Wk = jax.random.normal(ks[3], (CONTEXT_DIM, INNER), dtype=jnp.float32) * CONTEXT_DIM ** (-0.5)
        Wv = jax.random.normal(ks[4], (CONTEXT_DIM, INNER), dtype=jnp.float32) * CONTEXT_DIM ** (-0.5)
        Wo = jax.random.normal(ks[5], (INNER, QUERY_DIM), dtype=jnp.float32) * INNER ** (-0.5)
        bo = jax.random.normal(ks[6], (QUERY_DIM,), dtype=jnp.float32) * 0.01
        return {'x': x, 'context': context, 'Wq': Wq, 'Wk': Wk, 'Wv': Wv, 'Wo': Wo, 'bo': bo}
    _L0_xattn_all = _L0_xattn_setup()
    _L0_xattn_in = {k: v for k, v in _L0_xattn_all.items() if k in ('Wq', 'Wk', 'Wv', 'Wo', 'bo')}
    del _L0_xattn_all

    def _L0_ffn_setup():
        import jax, jax.numpy as jnp
        import numpy as np
        DIM = 256
        DEPTH = 2
        HEADS = 8
        DIM_HEAD = 64
        WINDOW = 128
        INNER = HEADS * DIM_HEAD
        HID = int(DIM * 4 * 2 / 3)
        B, N = (2, 2048)
        QK_SCALE = 8.0

        def shift_token(t):
            t1, t2 = jnp.split(t, 2, axis=-1)
            t2 = jnp.pad(t2, ((0, 0), (1, 0), (0, 0)))[:, :-1]
            return jnp.concatenate([t1, t2], axis=-1)

        def l2norm(t):
            return t / jnp.clip(jnp.linalg.norm(t, axis=-1, keepdims=True), 1e-12)

        def rotate_half(x):
            x1, x2 = jnp.split(x, 2, axis=-1)
            return jnp.concatenate([-x2, x1], axis=-1)

        def rotary_xpos(q, k):
            n = q.shape[-2]
            half_idx = jnp.arange(0, DIM_HEAD, 2, dtype=jnp.float32)
            inv_freq = 1.0 / 10000.0 ** (half_idx / DIM_HEAD)
            t = jnp.arange(n, dtype=jnp.float32)
            freqs = t[:, None] * inv_freq[None, :]
            freqs = jnp.concatenate([freqs, freqs], axis=-1)
            base = (half_idx + 0.4 * DIM_HEAD) / (1.4 * DIM_HEAD)
            power = (t - n // 2) / float(WINDOW // 2)
            scale = base[None, :] ** power[:, None]
            scale = jnp.concatenate([scale, scale], axis=-1)
            cos, sin = (jnp.cos(freqs), jnp.sin(freqs))
            q = q * cos * scale + rotate_half(q) * sin * scale
            k = k * cos / scale + rotate_half(k) * sin / scale
            return (q, k)

        def local_attention(q, k, v):
            b, h, n, d = q.shape
            w = n // WINDOW
            bq = q.reshape(b, h, w, WINDOW, d) * QK_SCALE
            bk = k.reshape(b, h, w, WINDOW, d)
            bv = v.reshape(b, h, w, WINDOW, d)

            def look_around(t):
                p = jnp.pad(t, ((0, 0), (0, 0), (1, 0), (0, 0), (0, 0)))
                return jnp.concatenate([p[:, :, :w], p[:, :, 1:]], axis=3)
            bk, bv = (look_around(bk), look_around(bv))
            bt = jnp.arange(n).reshape(w, WINDOW)
            btp = jnp.pad(bt, ((1, 0), (0, 0)), constant_values=-1)
            btk = jnp.concatenate([btp[:w], btp[1:]], axis=1)
            sim = jnp.einsum('bhwid,bhwjd->bhwij', bq, bk)
            i = bt[:, :, None]
            j = btk[:, None, :]
            mask = (i < j) | (i > j + WINDOW) | (j == -1)
            sim = jnp.where(mask, -jnp.finfo(sim.dtype).max, sim)
            attn = jax.nn.softmax(sim, axis=-1)
            out = jnp.einsum('bhwij,bhwjd->bhwid', attn, bv)
            return out.reshape(b, h, n, d)

        def _layer(x, wqkv, qs, ksc, wo, lg, lb, w1, b1, w2, b2):
            b, n, _ = x.shape
            h = shift_token(x)
            qkv = h @ wqkv
            q, k, v = jnp.split(qkv, 3, axis=-1)
            to_heads = lambda t: t.reshape(b, n, HEADS, DIM_HEAD).transpose(0, 2, 1, 3)
            q, k, v = (to_heads(q), to_heads(k), to_heads(v))
            q = l2norm(q) * qs
            k = l2norm(k) * ksc
            q, k = rotary_xpos(q, k)
            o = local_attention(q, k, v)
            o = o.transpose(0, 2, 1, 3).reshape(b, n, INNER)
            x = x + o @ wo
            h = shift_token(x)
            mu = h.mean(-1, keepdims=True)
            var = h.var(-1, keepdims=True)
            h = (h - mu) / jnp.sqrt(var + 1e-05) * lg + lb
            h = h @ w1 + b1
            a, g = jnp.split(h, 2, axis=-1)
            h = a * jax.nn.gelu(g, approximate=False)
            x = x + h @ w2 + b2
            return x
        key = jax.random.key(seed)
        ks = jax.random.split(key, 6)
        return {'x': jax.random.normal(ks[0], (B, N, DIM), jnp.float32), 'wqkv': jax.random.normal(ks[1], (DEPTH, DIM, 3 * INNER), jnp.float32) * 0.02, 'q_scale': jnp.ones((DEPTH, DIM_HEAD), jnp.float32), 'k_scale': jnp.ones((DEPTH, DIM_HEAD), jnp.float32), 'wo': jax.random.normal(ks[2], (DEPTH, INNER, DIM), jnp.float32) * 0.02, 'ln_g': jnp.ones((DEPTH, DIM), jnp.float32), 'ln_b': jnp.zeros((DEPTH, DIM), jnp.float32), 'w1': jax.random.normal(ks[3], (DEPTH, DIM, 2 * HID), jnp.float32) * 0.02, 'b1': jnp.zeros((DEPTH, 2 * HID), jnp.float32), 'w2': jax.random.normal(ks[4], (DEPTH, HID, DIM), jnp.float32) * 0.02, 'b2': jnp.zeros((DEPTH, DIM), jnp.float32)}
    _L0_ffn_all = _L0_ffn_setup()
    _L0_ffn_in = {k: v for k, v in _L0_ffn_all.items() if k in ('wqkv', 'q_scale', 'k_scale', 'wo', 'ln_g', 'ln_b', 'w1', 'b1', 'w2', 'b2')}
    del _L0_ffn_all
    return {'x': x, 'ctx_768': ctx_768, 'L0_xattn_Wq': _L0_xattn_in['Wq'], 'L0_xattn_Wk': _L0_xattn_in['Wk'], 'L0_xattn_Wv': _L0_xattn_in['Wv'], 'L0_xattn_Wo': _L0_xattn_in['Wo'], 'L0_xattn_bo': _L0_xattn_in['bo'], 'L0_ffn_wqkv': _L0_ffn_in['wqkv'], 'L0_ffn_q_scale': _L0_ffn_in['q_scale'], 'L0_ffn_k_scale': _L0_ffn_in['k_scale'], 'L0_ffn_wo': _L0_ffn_in['wo'], 'L0_ffn_ln_g': _L0_ffn_in['ln_g'], 'L0_ffn_ln_b': _L0_ffn_in['ln_b'], 'L0_ffn_w1': _L0_ffn_in['w1'], 'L0_ffn_b1': _L0_ffn_in['b1'], 'L0_ffn_w2': _L0_ffn_in['w2'], 'L0_ffn_b2': _L0_ffn_in['b2']}

def reference(x, ctx_768, L0_xattn_Wq, L0_xattn_Wk, L0_xattn_Wv, L0_xattn_Wo, L0_xattn_bo, L0_ffn_wqkv, L0_ffn_q_scale, L0_ffn_k_scale, L0_ffn_wo, L0_ffn_ln_g, L0_ffn_ln_b, L0_ffn_w1, L0_ffn_b1, L0_ffn_w2, L0_ffn_b2):
    import jax
    import jax.numpy as jnp

    def _L0_xattn_ref(x, context, Wq, Wk, Wv, Wo, bo):
        import jax, jax.numpy as jnp
        import numpy as np
        QUERY_DIM = 256
        CONTEXT_DIM = 192
        HEADS = 8
        DIM_HEAD = 64
        INNER = HEADS * DIM_HEAD
        B, S, _ = x.shape
        L = context.shape[1]
        scale = DIM_HEAD ** (-0.5)
        q = (x @ Wq).reshape(B, S, HEADS, DIM_HEAD).transpose(0, 2, 1, 3)
        k = (context @ Wk).reshape(B, L, HEADS, DIM_HEAD).transpose(0, 2, 1, 3)
        v = (context @ Wv).reshape(B, L, HEADS, DIM_HEAD).transpose(0, 2, 1, 3)
        attn = jnp.einsum('bhsd,bhld->bhsl', q, k) * scale
        attn = jax.nn.softmax(attn, axis=-1)
        out = jnp.einsum('bhsl,bhld->bhsd', attn, v)
        out = out.transpose(0, 2, 1, 3).reshape(B, S, INNER)
        return out @ Wo + bo

    def _L0_ffn_ref(x, wqkv, q_scale, k_scale, wo, ln_g, ln_b, w1, b1, w2, b2):
        import jax, jax.numpy as jnp
        import numpy as np
        DIM = 256
        DEPTH = 2
        HEADS = 8
        DIM_HEAD = 64
        WINDOW = 128
        INNER = HEADS * DIM_HEAD
        HID = int(DIM * 4 * 2 / 3)
        B, N = (2, 2048)
        QK_SCALE = 8.0

        def shift_token(t):
            t1, t2 = jnp.split(t, 2, axis=-1)
            t2 = jnp.pad(t2, ((0, 0), (1, 0), (0, 0)))[:, :-1]
            return jnp.concatenate([t1, t2], axis=-1)

        def l2norm(t):
            return t / jnp.clip(jnp.linalg.norm(t, axis=-1, keepdims=True), 1e-12)

        def rotate_half(x):
            x1, x2 = jnp.split(x, 2, axis=-1)
            return jnp.concatenate([-x2, x1], axis=-1)

        def rotary_xpos(q, k):
            n = q.shape[-2]
            half_idx = jnp.arange(0, DIM_HEAD, 2, dtype=jnp.float32)
            inv_freq = 1.0 / 10000.0 ** (half_idx / DIM_HEAD)
            t = jnp.arange(n, dtype=jnp.float32)
            freqs = t[:, None] * inv_freq[None, :]
            freqs = jnp.concatenate([freqs, freqs], axis=-1)
            base = (half_idx + 0.4 * DIM_HEAD) / (1.4 * DIM_HEAD)
            power = (t - n // 2) / float(WINDOW // 2)
            scale = base[None, :] ** power[:, None]
            scale = jnp.concatenate([scale, scale], axis=-1)
            cos, sin = (jnp.cos(freqs), jnp.sin(freqs))
            q = q * cos * scale + rotate_half(q) * sin * scale
            k = k * cos / scale + rotate_half(k) * sin / scale
            return (q, k)

        def local_attention(q, k, v):
            b, h, n, d = q.shape
            w = n // WINDOW
            bq = q.reshape(b, h, w, WINDOW, d) * QK_SCALE
            bk = k.reshape(b, h, w, WINDOW, d)
            bv = v.reshape(b, h, w, WINDOW, d)

            def look_around(t):
                p = jnp.pad(t, ((0, 0), (0, 0), (1, 0), (0, 0), (0, 0)))
                return jnp.concatenate([p[:, :, :w], p[:, :, 1:]], axis=3)
            bk, bv = (look_around(bk), look_around(bv))
            bt = jnp.arange(n).reshape(w, WINDOW)
            btp = jnp.pad(bt, ((1, 0), (0, 0)), constant_values=-1)
            btk = jnp.concatenate([btp[:w], btp[1:]], axis=1)
            sim = jnp.einsum('bhwid,bhwjd->bhwij', bq, bk)
            i = bt[:, :, None]
            j = btk[:, None, :]
            mask = (i < j) | (i > j + WINDOW) | (j == -1)
            sim = jnp.where(mask, -jnp.finfo(sim.dtype).max, sim)
            attn = jax.nn.softmax(sim, axis=-1)
            out = jnp.einsum('bhwij,bhwjd->bhwid', attn, bv)
            return out.reshape(b, h, n, d)

        def _layer(x, wqkv, qs, ksc, wo, lg, lb, w1, b1, w2, b2):
            b, n, _ = x.shape
            h = shift_token(x)
            qkv = h @ wqkv
            q, k, v = jnp.split(qkv, 3, axis=-1)
            to_heads = lambda t: t.reshape(b, n, HEADS, DIM_HEAD).transpose(0, 2, 1, 3)
            q, k, v = (to_heads(q), to_heads(k), to_heads(v))
            q = l2norm(q) * qs
            k = l2norm(k) * ksc
            q, k = rotary_xpos(q, k)
            o = local_attention(q, k, v)
            o = o.transpose(0, 2, 1, 3).reshape(b, n, INNER)
            x = x + o @ wo
            h = shift_token(x)
            mu = h.mean(-1, keepdims=True)
            var = h.var(-1, keepdims=True)
            h = (h - mu) / jnp.sqrt(var + 1e-05) * lg + lb
            h = h @ w1 + b1
            a, g = jnp.split(h, 2, axis=-1)
            h = a * jax.nn.gelu(g, approximate=False)
            x = x + h @ w2 + b2
            return x
        for l in range(DEPTH):
            x = _layer(x, wqkv[l], q_scale[l], k_scale[l], wo[l], ln_g[l], ln_b[l], w1[l], b1[l], w2[l], b2[l])
        return x
    x = x + _L0_xattn_ref(_layernorm(x, axis=-1), ctx_768, L0_xattn_Wq, L0_xattn_Wk, L0_xattn_Wv, L0_xattn_Wo, L0_xattn_bo)
    x = x + _L0_ffn_ref(_layernorm(x, axis=-1), L0_ffn_wqkv, L0_ffn_q_scale, L0_ffn_k_scale, L0_ffn_wo, L0_ffn_ln_g, L0_ffn_ln_b, L0_ffn_w1, L0_ffn_b1, L0_ffn_w2, L0_ffn_b2)
    return x

_drawn_inputs = setup_inputs


def setup_inputs(seed=0):
    import zlib

    import numpy as np

    out = dict(_drawn_inputs(seed))
    spreads = {'L0_ffn_q_scale': (1.0, 0.6),
     'L0_ffn_k_scale': (1.0, 0.6),
     'L0_ffn_ln_g': (1.0, 0.6),
     'L0_ffn_ln_b': (0.0, 0.8),
     'L0_ffn_b1': (0.0, 0.8),
     'L0_ffn_b2': (0.0, 0.1)}
    factors = {'L0_xattn_bo': 6.165}
    for name, (base, spread) in spreads.items():
        noise = np.random.default_rng([zlib.crc32(name.encode()), seed]).standard_normal(out[name].shape)
        drawn = base * np.exp(spread * noise) if base else spread * noise
        out[name] = jnp.asarray(drawn.astype(out[name].dtype))
    for name, factor in factors.items():
        out[name] = (out[name] * factor).astype(out[name].dtype)
    return out
```

```python
from contextlib import ExitStack

import numpy as np

import concourse.bass as bass
from concourse import mybir

F32 = mybir.dt.float32
F32R = mybir.dt.float32r
BF16 = mybir.dt.bfloat16
ALU = mybir.AluOpType
ACT = mybir.ActivationFunctionType
AX = mybir.AxisListType

P = 128
SEQS, T, D = 16, 256, 256
NT = T // P
KC = D // P
HEADS, DH = 8, 64
INNER = HEADS * DH
IC = INNER // P
CTX, CD = 77, 192
LAYERS = 2
ITEMS = LAYERS * SEQS
HID = int(D * 4 * 2 / 3)
FC = -(-HID // P)
TAIL = HID - (FC - 1) * P
TAIL_G = 64
W1C = 2 * (FC - 1) + 1
QKV = 3 * INNER
EPS = 1e-5
NORM_MIN_SQ = 1e-24
QK_SCALE = 8.0
WINDOW = 128
MASKED = -1e30
UNITS = 6
XUNITS = 4

WEIGHT = {name: n + 1 for n, name in enumerate(
    ["xq", "xo", "wo0", "w20", "qkv0", "w10", "qkv1", "wo1", "w21", "w11"])}


def rope_tables():
    half = np.arange(0, DH, 2, dtype=np.float32)
    freq = np.arange(T, dtype=np.float32)[:, None] * (1.0 / 10000.0 ** (half / DH))[None, :]
    base = (half + 0.4 * DH) / (1.4 * DH)
    power = (np.arange(T, dtype=np.float32) - T // 2) / float(WINDOW // 2)
    scale = (base[None, :] ** power[:, None]).astype(np.float32)
    cos, sin = np.cos(freq.astype(np.float32)), np.sin(freq.astype(np.float32))
    q = scale * np.float32(QK_SCALE)
    k = np.float32(1.0) / scale
    out = np.empty((2, T, 2, DH), np.float32)
    for j, s in enumerate((q, k)):
        out[0, :, j] = np.concatenate([cos * s, cos * s], -1)
        out[1, :, j] = np.concatenate([-sin * s, sin * s], -1)
    return np.ascontiguousarray(out.reshape(2, NT, P, 2, DH).transpose(2, 0, 1, 3, 4))


def masks():
    i, j = np.arange(P)[:, None], np.arange(P)[None, :]
    before = np.where(j < i, MASKED, 0.0)
    own = np.where(j > i, MASKED, 0.0)
    return np.concatenate([before, own, before, own, own, own, own, own], 1).astype(np.float32)


def at(n, per, k):
    if isinstance(n, int):
        return n * per + k
    i, c = n
    return i * (2 * per) + (c * per + k)


def of_parity(n):
    return 16 * (n // 2 + 1) if isinstance(n, int) else n[0] * 16 + 16 * (n[1] // 2 + 1)


def plus(n, d):
    return n + d if isinstance(n, int) else (n[0], n[1] + d)


def index(n):
    return n if isinstance(n, int) else n[0] * 2 + n[1]


def later(n):
    return not (isinstance(n, int) and n == 0)


def build(nc, x, ctx_in, xwq, xwk, xwv, xwo, xbo, wqkv, qsc, ksc, wo, lng, lnb, w1, b1, w2, b2, rope, mask, ident, out):
    ctx = ExitStack()
    with ctx:
        def sb(name, shape, dt=F32, where=ctx):
            return where.enter_context(nc.sbuf_tensor(name, shape, dt))

        def sem(name):
            return ctx.enter_context(nc.semaphore(name))

        y_dram = nc.dram_tensor("y_state", (SEQS, P, NT, D), F32, kind="Internal").ap()
        x1_dram = nc.dram_tensor("x1_state", (SEQS, P, NT, D), F32, kind="Internal").ap()

        pb = ctx.enter_context(nc.psum_tensor("pb", [P, 8, 512], F32))
        id_f = sb("id_f", [P, P])
        id_b = sb("id_b", [P, P], BF16)
        mask_b = sb("mask_b", [P, 2, 512], BF16)
        half_neg = sb("half_neg", [P, 2 * HEADS])
        eps_t = sb("eps_t", [P, NT])
        cos_t = sb("cos_t", [P, LAYERS, NT, 2, DH])
        sin_t = sb("sin_t", [P, LAYERS, NT, 2, DH])
        b2_t = sb("b2_t", [P, LAYERS, D])
        bo_t = sb("bo_t", [P, D])
        b1_t = sb("b1_t", [P, LAYERS, 2, FC])
        lng_t = sb("lng_t", [P, LAYERS, KC])
        lnb_t = sb("lnb_t", [P, LAYERS, KC])
        wqkv_hi = sb("wqkv_hi", [P, KC, QKV], F32R)
        wqkv_lo = sb("wqkv_lo", [P, KC, QKV], F32R)
        wo_hi = sb("wo_hi", [P, IC, D], F32R)
        wo_lo = sb("wo_lo", [P, IC, D], F32R)
        w1_hi = sb("w1_hi", [P, KC, W1C, P], F32R)
        w1_lo = sb("w1_lo", [P, KC, W1C, P], F32R)
        w2_hi = sb("w2_hi", [P, FC, D], F32R)
        w2_lo = sb("w2_lo", [P, FC, D], F32R)
        raw_a = sb("raw_a", [P, KC * QKV])
        raw_b = sb("raw_b", [P, (IC + FC) * D])

        X = ExitStack()
        rope_raw = sb("rope_raw", [P, 2, NT, 2, DH], where=X)
        sc_t = sb("sc_t", [P, LAYERS, 2, 2, DH], where=X)
        mask_raw = sb("mask_raw", [P, 2, 512], where=X)
        xq_hi = sb("xq_hi", [P, KC, INNER], F32R, X)
        xq_lo = sb("xq_lo", [P, KC, INNER], F32R, X)
        xo_hi = sb("xo_hi", [P, IC, D], F32R, X)
        xo_lo = sb("xo_lo", [P, IC, D], F32R, X)
        xk_w = sb("xk_w", [P, 2, INNER], where=X)
        xv_w = sb("xv_w", [P, 2, INNER], where=X)
        x_in = sb("x_in", [P, 2, NT, D], where=X)
        x_b = sb("x_b", [P, 2, NT, D], where=X)
        c_in = sb("c_in", [P, 2, D], where=X)
        xn = sb("xn", [P, NT, D], where=X)
        xn_hi = sb("xn_hi", [P, KC, T], F32R, X)
        xn_lo = sb("xn_lo", [P, KC, T], F32R, X)
        c_t = sb("c_t", [P, 2, CTX], where=X)
        xq_t = sb("xq_t", [P, 2, IC, T], where=X)
        xk_t = sb("xk_t", [P, 2, IC, CTX], where=X)
        x_v = sb("x_v", [P, 2, INNER], where=X)
        x_p = sb("x_p", [P, XUNITS, 4, CTX], where=X)
        x_pt = sb("x_pt", [P, 2, 4, P], where=X)
        xo_hi_t = sb("xo_hi_t", [P, IC, T], F32R, X)
        xo_lo_t = sb("xo_lo_t", [P, IC, T], F32R, X)
        x1_x = sb("x1_x", [P, NT, D], where=X)
        y_x = sb("y_x", [P, NT, D], where=X)
        x_st = sb("x_st", [P, 2, NT, 6], where=X)
        x_mv = sb("x_mv", [P, 2, NT, 2], where=X)
        x_ve = sb("x_ve", [P, 2, NT], where=X)
        x_rs = sb("x_rs", [P, 2, NT], where=X)
        x_nm = sb("x_nm", [P, XUNITS, 4], where=X)
        x_sum = sb("x_sum", [P, XUNITS, 4], where=X)
        x_inv = sb("x_inv", [P, XUNITS, 4], where=X)
        X.close()

        L = ctx.enter_context(ExitStack())
        x_cur = sb("x_cur", [P, NT, D], where=L)
        x_res = sb("x_res", [P, NT, D], where=L)
        x_orig = sb("x_orig", [P, NT, D], where=L)
        xt_hi = sb("xt_hi", [P, 2 * T + 1], F32R, L)
        xt_lo = sb("xt_lo", [P, 2 * T + 1], F32R, L)
        r_cos = sb("r_cos", [P, NT, 2 * INNER], where=L)
        r_sin = sb("r_sin", [P, NT, 2 * INNER], where=L)
        n_sq = sb("n_sq", [P, NT, 2 * HEADS], where=L)
        n_cl = sb("n_cl", [P, NT, 2 * HEADS], where=L)
        n_inv = sb("n_inv", [P, NT, 2 * HEADS], where=L)
        qk_t = sb("qk_t", [P, 2, IC, T], where=L)
        v_t = sb("v_t", [P, 2, NT, INNER], where=L)
        p_t = sb("p_t", [P, 3, 512], where=L)
        pt_t = sb("pt_t", [P, 2, 512], where=L)
        s_nm = sb("s_nm", [P, UNITS, 4], where=L)
        s_sum = sb("s_sum", [P, UNITS, 4], where=L)
        s_inv = sb("s_inv", [P, UNITS, 4], where=L)
        o_hi = sb("o_hi", [P, IC, T], F32R, L)
        o_lo = sb("o_lo", [P, IC, T], F32R, L)
        x1 = sb("x1", [P, NT, 3, P], where=L)
        x1b = sb("x1b", [P, NT, D], where=L)
        l_st = sb("l_st", [P, NT, 6], where=L)
        l_mv = sb("l_mv", [P, NT, 2], where=L)
        l_ve = sb("l_ve", [P, NT], where=L)
        l_rs = sb("l_rs", [P, NT], where=L)
        h_n = sb("h_n", [P, NT, D], where=L)
        h_f = sb("h_f", [P, KC, T], where=L)
        h_hi = sb("h_hi", [P, KC, T], F32R, L)
        h_lo = sb("h_lo", [P, KC, T], F32R, L)
        gl = sb("gl", [P, 2, T], where=L)
        hg = sb("hg", [P, 2, T], where=L)
        hg_hi = sb("hg_hi", [P, FC, T], F32R, L)
        hg_lo = sb("hg_lo", [P, FC, T], F32R, L)
        x2 = sb("x2", [P, 2, NT, D], where=L)

        const_in = sem("const_in")
        raw_a_in, raw_b_in = sem("raw_a_in"), sem("raw_b_in")
        w_hi, w_lo = sem("w_hi"), sem("w_lo")
        const_made = sem("const_made")
        zero_made = sem("zero_made")
        x_load, c_load = [sem(f"x_load{u}") for u in range(2)], [sem(f"c_load{u}") for u in range(2)]
        x_bst, x_bmv = sem("x_bst"), sem("x_bmv")
        x_eps, x_rst = sem("x_eps"), sem("x_rst")
        x_norm = sem("x_norm")
        x_bias = sem("x_bias")
        x_tr, c_tr = sem("x_tr"), sem("c_tr")
        x_thi, x_tlo = sem("x_thi"), sem("x_tlo")
        c_cp = sem("c_cp")
        x_pq, x_pk, x_pv = sem("x_pq"), sem("x_pk"), sem("x_pv")
        x_cq, x_ck, x_cv = sem("x_cq"), sem("x_ck"), sem("x_cv")
        x_s, x_max, x_exp, x_rec, x_pn = sem("x_s"), sem("x_max"), sem("x_exp"), sem("x_rec"), sem("x_pn")
        x_ptr, x_ptc, x_av = sem("x_ptr"), sem("x_ptc"), sem("x_av")
        x_ohi, x_olo, x_wo = sem("x_ohi"), sem("x_olo"), sem("x_wo")
        x_res1, y_bst, y_bmv, y_eps, y_rst, y_norm = [sem(n) for n in (
            "x_res1", "y_bst", "y_bmv", "y_eps", "y_rst", "y_norm")]
        x1_store, y_store = sem("x1_store"), sem("y_store")
        stats_seen = sem("stats_seen")
        stage_l = sem("stage_l")
        cur_load, res_load, orig_load, shift, x2_store = [sem(n) for n in (
            "cur_load", "res_load", "orig_load", "shift", "x2_store")]
        pe_xt, act_xhi, dve_xlo = sem("pe_xt"), sem("act_xhi"), sem("dve_xlo")
        pe_qkv, act_sq, act_v = sem("pe_qkv"), sem("act_sq"), sem("act_v")
        dve_ss, dve_cl, dve_rope = sem("dve_ss"), sem("dve_cl"), sem("dve_rope")
        pool_inv, pool_sum, pool_qk = sem("pool_inv"), sem("pool_sum"), sem("pool_qk")
        pe_qkt, act_qkt = sem("pe_qkt"), sem("act_qkt")
        pe_s, dve_max, act_exp, dve_rec, dve_pn = sem("pe_s"), sem("dve_max"), sem("act_exp"), sem("dve_rec"), sem("dve_pn")
        pe_pt, act_pt, pe_av, act_ohi, dve_olo = sem("pe_pt"), sem("act_pt"), sem("pe_av"), sem("act_ohi"), sem("dve_olo")
        pe_wo, dve_x1, pool_x1b, pool_x1o = sem("pe_wo"), sem("dve_x1"), sem("pool_x1b"), sem("pool_x1o")
        dve_bst, dve_bmv, pool_eps, pool_rst, dve_h = [sem(n) for n in ("dve_bst", "dve_bmv", "pool_eps", "pool_rst", "dve_h")]
        pe_ht, act_h, dve_hhi, dve_hlo = sem("pe_ht"), sem("act_h"), sem("dve_hhi"), sem("dve_hlo")
        pe_w1, act_gelu, dve_hg, dve_hghi, pool_hglo = [sem(n) for n in ("pe_w1", "act_gelu", "dve_hg", "dve_hghi", "pool_hglo")]
        pe_w2, dve_x2 = sem("pe_w2"), sem("dve_x2")

        CONSTS = 0

        x_rows = x.rearrange("s (t p) d -> s p t d", p=P)
        out_rows = out.rearrange("s (t p) d -> s p t d", p=P)

        def one(t, n):
            return t[bass.ds(n, 1)].rearrange("o p t d -> p (o t) d")

        def x_iterations(eng, run):
            for g in range(3):
                run(g)
            with eng.Fori(1, SEQS // 2 - 1) as i:
                for u in range(2):
                    run((i, u + 1))
            run(SEQS - 1)
            run(SEQS)

        def x_roles(g):
            a = None if g == SEQS else g
            b = None if g == 0 else plus(g, -1)
            return a, b, (g if isinstance(g, int) else g[1]) % 2

        def l_iterations(eng, run, between):
            for layer in range(LAYERS):
                first = layer * SEQS
                between(first)
                run(first)
                between(first + 1)
                run(first + 1)
                between(first + 2)
                peeled = 2 if layer else 4
                for g in range(first + 2, first + peeled):
                    run(g)
                ends = first + SEQS - (2 if layer else 0)
                with eng.Fori((first + peeled) // 2, ends // 2) as i:
                    for u in range(2):
                        run((i, u), layer)
            for g in range(ITEMS - 2, ITEMS + 2):
                run(g)

        def l_roles(g):
            a = g if not isinstance(g, int) or g < ITEMS else None
            b = plus(g, -1) if not isinstance(g, int) or 1 <= g <= ITEMS else None
            c = plus(g, -2) if not isinstance(g, int) or g >= 2 else None
            return a, b, c, (g if isinstance(g, int) else g[1]) % 2

        def heads_of(u):
            return range(u // 2 * 4 + u % 2, u // 2 * 4 + 4, 2) if u < 4 else range(u % 2, HEADS, 2)

        def layer_of(n, layer):
            return n // SEQS if isinstance(n, int) else layer

        def seq_of(n, layer):
            return n % SEQS if isinstance(n, int) else n[0] * 2 + (n[1] - layer * SEQS)

        def shifted(t):
            whole = t[:]
            return bass.AP(tensor=whole.tensor, offset=whole.offset, ap=[list(whole.ap[0]), [T + 1, KC], [1, T]])

        block = ctx.enter_context(nc.Block())

        @block.sync
        def _(sp):
            nonlocal CONSTS
            sp.dma_start(id_f[:], ident).then_inc(const_in, 16)
            sp.dma_start(raw_a[:, 0:KC * INNER].rearrange("p (c n) -> p c n", c=KC),
                         xwq.rearrange("(c p) n -> p c n", p=P)).then_inc(raw_a_in, 16)
            sp.dma_start(raw_a[:, KC * INNER:KC * INNER + IC * D].rearrange("p (c n) -> p c n", c=IC),
                         xwo.rearrange("(c p) n -> p c n", p=P)).then_inc(raw_a_in, 16)

            def load_x(n):
                par = (n if isinstance(n, int) else n[1]) % 2
                sp.dma_start(x_in[:, par], one(x_rows, index(n))).then_inc(x_load[par], 16)
                sp.dma_start(c_in[0:CTX, par, 0:CD],
                             ctx_in[bass.ds(index(n), 1)].rearrange("o s d -> s (o d)")).then_inc(c_load[par], 16)

            sp.wait_ge(zero_made, 1)
            load_x(0)
            load_x(1)
            consts = [
                (xk_w[:], xwk.rearrange("(c p) n -> p c n", p=P)),
                (xv_w[:], xwv.rearrange("(c p) n -> p c n", p=P)),
                (bo_t[:], xbo.partition_broadcast(P)),
                (mask_raw[:], mask.rearrange("p (a n) -> p a n", a=2)),
                (rope_raw[:], rope),
            ]
            for layer in range(LAYERS):
                consts.append((b2_t[:, layer], b2[layer].partition_broadcast(P)))
                consts.append((b1_t[:, layer], b1[layer]))
                consts.append((lng_t[:, layer], lng[layer]))
                consts.append((lnb_t[:, layer], lnb[layer]))
                for j, s in enumerate((qsc, ksc)):
                    consts.append((sc_t[:, layer, 0, j], s[layer].partition_broadcast(P)))
                    for half in range(2):
                        consts.append((sc_t[:, layer, 1, j, half * 32:half * 32 + 32],
                                       s[layer, 32 - half * 32:64 - half * 32].partition_broadcast(P)))
            for dst, src in consts:
                sp.dma_start(dst, src).then_inc(const_in, 16)
            CONSTS = 16 * (len(consts) + 1)

            def load_b(layer):
                sp.dma_start(raw_b[:, 0:IC * D].rearrange("p (c n) -> p c n", c=IC),
                             wo[layer].rearrange("(c p) n -> p c n", p=P)).then_inc(raw_b_in, 16)
                sp.dma_start(raw_b[:, IC * D:(IC + FC) * D].rearrange("p (c n) -> p c n", c=FC),
                             w2[layer].rearrange("(c p) n -> p c n", p=P)).then_inc(raw_b_in, 16)

            def load_qkv(layer):
                sp.dma_start(raw_a[:].rearrange("p (c n) -> p c n", c=KC),
                             wqkv[layer].rearrange("(c p) n -> p c n", p=P)).then_inc(raw_a_in, 16)

            def load_w1(layer):
                sp.dma_start(raw_a[:, 0:KC * W1C * P].rearrange("p (c n) -> p c n", c=KC),
                             w1[layer].rearrange("(c p) n -> p c n", p=P)).then_inc(raw_a_in, 16)

            load_b(0)

            def run_x(g):
                a, b, par = x_roles(g)
                if b is not None:
                    sp.wait_ge(x_res1, at(b, 1, 1))
                    sp.dma_start(one(x1_dram, index(b)), x1_x[:]).then_inc(x1_store, 16)
                    sp.wait_ge(y_norm, at(b, 1, 1))
                    sp.dma_start(one(y_dram, index(b)), y_x[:]).then_inc(y_store, 16)
                if not isinstance(g, int) or g < SEQS - 2:
                    sp.wait_ge(x_norm, at(a, 1, 1))
                    sp.wait_ge(x_bias, at(a, 1, 1))
                    sp.wait_ge(c_tr, at(a, 1, 1))
                    load_x(plus(a, 2))
                if isinstance(g, int) and g == 0:
                    sp.wait_ge(w_lo, WEIGHT["xo"])
                    load_qkv(0)
                if isinstance(g, int) and g == SEQS - 1:
                    sp.wait_ge(w_lo, WEIGHT["qkv0"])
                    load_w1(0)
                    load_b(1)

            for g in range(3):
                run_x(g)
            with sp.Fori(1, SEQS // 2 - 2) as i:
                for u in range(2):
                    run_x((i, u + 1))
            for g in range(SEQS - 3, SEQS + 1):
                run_x(g)

            sp.wait_ge(x1_store, 16 * SEQS)
            sp.wait_ge(y_store, 16 * SEQS)
            sp.wait_ge(w_lo, WEIGHT["w10"])
            sp.sem_inc(stage_l, 1)
            sp.dma_start(x_cur[:], one(y_dram, 0)).then_inc(cur_load, 16)
            sp.dma_start(x_res[:], one(y_dram, 0)).then_inc(res_load, 16)
            load_qkv(1)

            def run_l(g, layer=None):
                a, b, c, par = l_roles(g)
                if c is not None:
                    sp.wait_ge(dve_x1, at(c, 1, 1))
                    for t in range(NT):
                        sp.dma_start(x1[1:P, t, 1], x1[0:P - 1, t, 2]).then_inc(shift, 16)
                    sp.dma_start(x1[0:1, 1, 1], x1[P - 1:P, 0, 2]).then_inc(shift, 16)
                    if b is not None:
                        sp.dma_start(x_res[:], one(y_dram, seq_of(b, layer))).then_inc(res_load, 16)
                    if layer_of(c, layer) == LAYERS - 1:
                        sp.dma_start(x_orig[:], one(x1_dram, seq_of(c, layer))).then_inc(orig_load, 16)
                if a is not None and not (isinstance(a, int) and a == ITEMS - 1):
                    sp.wait_ge(pe_xt, at(a, 1, 1))
                    sp.dma_start(x_cur[:], one(y_dram, seq_of(plus(a, 1), layer))).then_inc(cur_load, 16)
                if c is not None:
                    sp.wait_ge(dve_x2, at(c, 1, 1))
                    dst = out_rows if layer_of(c, layer) == LAYERS - 1 else y_dram
                    sp.dma_start(one(dst, seq_of(c, layer)), x2[:, par]).then_inc(x2_store, 16)

            def between(g):
                if g == SEQS:
                    sp.wait_ge(w_lo, WEIGHT["qkv1"])
                    load_w1(1)

            between(0)
            for g in range(4):
                run_l(g)
            with sp.Fori(2, SEQS // 2 - 1) as i:
                for u in range(2):
                    run_l((i, u), 0)
            run_l(SEQS - 2)
            run_l(SEQS - 1)
            between(SEQS)
            run_l(SEQS)
            run_l(SEQS + 1)
            with sp.Fori(SEQS // 2 + 1, SEQS - 1) as i:
                for u in range(2):
                    run_l((i, u), 1)
            for g in range(ITEMS - 2, ITEMS + 2):
                run_l(g)
            sp.wait_ge(x2_store, 16 * ITEMS)

        @block.tensor
        def _(pe):
            def bank(b):
                return pb[:, b]

            def split_product(dst, pairs, done):
                for n, (s_hi, s_lo, m_hi, m_lo) in enumerate(pairs):
                    for k, (s, m) in enumerate(((s_hi, m_hi), (s_hi, m_lo), (s_lo, m_hi))):
                        mm = pe.matmul(dst, s, m, start=(n == 0 and k == 0 and done[0]),
                                       stop=(n == len(pairs) - 1 and k == 2))
                return mm

            pe.wait_ge(const_in, CONSTS)

            def x_turn(a, par):
                pe.wait_ge(x_norm, at(a, 1, 1))
                for c in range(KC):
                    for t in range(NT):
                        mm = pe.transpose(pb[:, 0, c * T + t * P:c * T + t * P + P], xn[:, t, c * P:c * P + P], id_f[:])
                mm.then_inc(x_tr, 1)
                pe.wait_ge(c_load[par], of_parity(a))
                for c in range(2):
                    mm = pe.transpose(pb[:, 1, c * P:c * P + CTX], c_in[0:CTX, par, c * P:c * P + P],
                                      id_f[0:CTX, 0:CTX])
                mm.then_inc(c_tr, 1)

            def x_scores(b, par, u):
                t, odd = u // 2, u % 2
                if u == 0:
                    pe.wait_ge(x_cq, at(b, 2, 2))
                    pe.wait_ge(x_ck, at(b, 1, 1))
                if u >= 2:
                    pe.wait_ge(x_exp, at(b, XUNITS, u - 1))
                for k in range(4):
                    r = odd * DH
                    mm = pe.matmul(pb[:, 2 + u % 2, k * P:k * P + CTX], xq_t[r:r + DH, par, k, t * P:t * P + P],
                                   xk_t[r:r + DH, par, k, :], start=True, stop=True)
                mm.then_inc(x_s, 1)

            def x_probs(b, u):
                pe.wait_ge(x_pn, at(b, XUNITS, u + 1))
                if u >= 2:
                    pe.wait_ge(x_ptc, at(b, XUNITS, u - 1))
                for k in range(4):
                    mm = pe.transpose(pb[0:CTX, u % 2, k * P:k * P + P], x_p[:, u, k, :], id_f[:])
                mm.then_inc(x_ptr, 1)

            def x_values(b, par, u):
                t, odd = u // 2, u % 2
                if u == 0:
                    pe.wait_ge(x_cv, at(b, 1, 1))
                pe.wait_ge(x_ptc, at(b, XUNITS, u + 1))
                for k in range(4):
                    h = 2 * k + odd
                    r, col = odd * DH, (k % 2) * T + t * P
                    mm = pe.matmul(pb[r:r + DH, 6 + k // 2, col:col + P], x_v[0:CTX, par, h * DH:h * DH + DH],
                                   x_pt[0:CTX, u % 2, k, :], start=True, stop=True)
                mm.then_inc(x_av, 1)

            def run_x(g):
                a, b, par = x_roles(g)
                was = 1 - par
                if isinstance(g, int) and g == 0:
                    x_turn(0, 0)
                    pe.wait_ge(w_lo, WEIGHT["xo"])
                if b is not None:
                    x_scores(b, was, 0)
                    x_scores(b, was, 1)
                if a is not None:
                    pe.wait_ge(x_thi, at(a, 1, 1))
                    pe.wait_ge(x_tlo, at(a, 1, 1))
                    if b is not None:
                        pe.wait_ge(x_res1, at(b, 1, 0)) if later(b) else None
                    for c in range(IC):
                        cols = slice(c * P, c * P + P)
                        mm = split_product(pb[:, 4 + c // 2, (c % 2) * T:(c % 2) * T + T],
                                           [(xq_hi[:, k, cols], xq_lo[:, k, cols], xn_hi[:, k], xn_lo[:, k])
                                            for k in range(KC)], (True,))
                        if c % 2:
                            mm.then_inc(x_pq, 1)
                if b is not None:
                    x_probs(b, 0)
                    x_scores(b, was, 2)
                if a is not None:
                    pe.wait_ge(c_cp, at(a, 1, 1))
                    for c in range(IC):
                        for k in range(2):
                            mm = pe.matmul(pb[:, 6, c * P:c * P + CTX], xk_w[:, k, c * P:c * P + P], c_t[:, k, :],
                                           start=(k == 0), stop=(k == 1))
                    mm.then_inc(x_pk, 1)
                if b is not None:
                    x_probs(b, 1)
                    x_scores(b, was, 3)
                if a is not None:
                    for k in range(2):
                        mm = pe.matmul(pb[0:CTX, 7, :], c_t[:, k, :], xv_w[:, k, :], start=(k == 0), stop=(k == 1))
                    mm.then_inc(x_pv, 1)
                if b is not None:
                    if a is not None:
                        pe.wait_ge(x_ck, at(a, 1, 1))
                        pe.wait_ge(x_cv, at(a, 1, 1))
                    x_values(b, was, 0)
                    x_probs(b, 2)
                    x_values(b, was, 1)
                    x_probs(b, 3)
                    x_values(b, was, 2)
                    x_values(b, was, 3)
                if not isinstance(g, int) or g + 1 < SEQS:
                    x_turn(plus(a, 1), 1 - par)
                if b is not None:
                    pe.wait_ge(x_ohi, at(b, 2, 2))
                    pe.wait_ge(x_olo, at(b, 2, 2))
                    if a is not None:
                        pe.wait_ge(x_cq, at(a, 2, 1))
                    for t in range(NT):
                        rows = slice(t * P, t * P + P)
                        mm = split_product(pb[:, 4, t * D:t * D + D],
                                           [(xo_hi_t[:, c, rows], xo_lo_t[:, c, rows], xo_hi[:, c], xo_lo[:, c])
                                            for c in range(IC)], (True,))
                    mm.then_inc(x_wo, 1)

            x_iterations(pe, run_x)

            pe.wait_ge(stage_l, 1)
            QKV_BANK = {(0, 0): 0, (0, 1): 1, (1, 0): 3, (1, 1): 4, (0, 2): 2, (1, 2): 5}
            W1_BANK = [6, 7, 2, 5, 6, 7]

            def turn_x(n):
                pe.wait_ge(cur_load, at(n, 16, 16))
                for c in range(KC):
                    for t in range(NT):
                        mm = pe.transpose(pb[:, 4, c * T + t * P:c * T + t * P + P], x_cur[:, t, c * P:c * P + P], id_f[:])
                mm.then_inc(pe_xt, 1)

            def project(a, t, part):
                b = QKV_BANK[t, part]
                if part < 2 and b < 4 and later(a):
                    pe.wait_ge(act_qkt, at(plus(a, -1), 4, b + 1))
                if part == 2 and b == 2 and later(a):
                    pe.wait_ge(act_qkt, at(plus(a, -1), 4, 3))
                cols = slice(part * INNER, part * INNER + INNER)
                mm = split_product(bank(b), [(xt_hi[:, c * T + t * P:c * T + t * P + P],
                                              xt_lo[:, c * T + t * P:c * T + t * P + P],
                                              wqkv_hi[:, c, cols], wqkv_lo[:, c, cols]) for c in range(KC)], (True,))
                mm.then_inc(pe_qkv, 1)

            def turn_h(c):
                pe.wait_ge(dve_h, at(c, 1, 1))
                for k in range(KC):
                    for t in range(NT):
                        mm = pe.transpose(pb[:, 7, k * T + t * P:k * T + t * P + P], h_n[:, t, k * P:k * P + P], id_f[:])
                mm.then_inc(pe_ht, 1)

            def hidden(a, c, m):
                if m == 0:
                    pe.wait_ge(dve_hhi, at(c, 1, 1))
                    pe.wait_ge(dve_hlo, at(c, 1, 1))
                if m in (2, 3):
                    if a is not None:
                        pe.wait_ge(act_v, at(a, NT, m - 1))
                    elif m == 2:
                        pe.wait_ge(act_qkt, 4 * ITEMS)
                if m >= 4:
                    pe.wait_ge(dve_hg, at(c, FC, m - 3))
                for part in range(2 if m < FC - 1 else 1):
                    n = 2 * m + part
                    mm = split_product(pb[:, W1_BANK[m], part * T:part * T + T],
                                       [(w1_hi[:, k, n], w1_lo[:, k, n], h_hi[:, k], h_lo[:, k]) for k in range(KC)],
                                       (True,))
                mm.then_inc(pe_w1, 1)

            def scores(a, b, c, u):
                if u == 0:
                    pe.wait_ge(act_qkt, at(b, 4, 4))
                    if a is not None:
                        pe.wait_ge(dve_rope, at(a, NT, 1))
                if u == 2:
                    if c is not None:
                        pe.wait_ge(dve_hg, at(c, FC, 3))
                    elif a is not None:
                        pe.wait_ge(act_v, at(a, NT, 1))
                win1 = u < 4
                pe.matmul(bank(u % 3), id_b[:], mask_b[:, 0 if win1 else 1], start=True, stop=False, skip_group_check=True)
                keys = T if win1 else P
                for k, h in enumerate(heads_of(u)):
                    ch, r = h // 2, (h % 2) * DH
                    q_cols = slice(P, T) if win1 else slice(0, P)
                    mm = pe.matmul(pb[:, u % 3, k * keys:k * keys + keys], qk_t[r:r + DH, 0, ch, q_cols],
                                   qk_t[r:r + DH, 1, ch, 0:keys], start=False, stop=True, skip_group_check=True)
                mm.then_inc(pe_s, 1)

            def turn_p(a, b, u):
                pe.wait_ge(dve_pn, at(b, UNITS, u + 1))
                if u == 0 and a is not None:
                    pe.wait_ge(dve_rope, at(a, NT, 2))
                if u >= 2:
                    pe.wait_ge(act_pt, at(b, UNITS, u - 1))
                for k in range(4):
                    mm = pe.transpose(pb[:, 3 + u % 2, k * P:k * P + P], p_t[:, u % 3, k * P:k * P + P], id_f[:])
                mm.then_inc(pe_pt, 1)

            def weigh(a, b, c, par, u):
                pe.wait_ge(act_pt, at(b, UNITS, u + 1))
                if u == 0:
                    pe.wait_ge(act_v, at(b, NT, NT))
                    if c is not None:
                        pe.wait_ge(dve_hg, at(c, FC, 4))
                    elif a is not None:
                        pe.wait_ge(act_v, at(a, NT, NT))
                if u == 2 and c is not None:
                    pe.wait_ge(dve_hg, at(c, FC, 5))
                if u < 4:
                    for k, h in enumerate(heads_of(u)):
                        r, col = (h % 2) * DH, (h // 2 % 2) * T + P
                        for t in range(NT):
                            mm = pe.matmul(pb[r:r + DH, 5 + h // 4, col:col + P],
                                           v_t[:, par, t, h * DH:h * DH + DH],
                                           pt_t[:, u % 2, (2 * k + t) * P:(2 * k + t) * P + P],
                                           start=(t == 0), stop=(t == NT - 1))
                else:
                    for k, h in enumerate(heads_of(u)):
                        r, col = (h % 2) * DH, (h // 2 % 2) * T
                        mm = pe.matmul(pb[r:r + DH, 5 + h // 4, col:col + P], v_t[:, par, 0, h * DH:h * DH + DH],
                                       pt_t[:, u % 2, k * P:k * P + P], start=True, stop=True)
                mm.then_inc(pe_av, 1)

            def feed(c, n):
                t, k = n // FC, n % FC
                if n == 0:
                    pe.wait_ge(dve_hg, at(c, FC, FC))
                if t == 0:
                    pe.wait_ge(dve_hghi, at(c, FC, k + 1))
                    pe.wait_ge(pool_hglo, at(c, FC, k + 1))
                rows = slice(t * P, t * P + P)
                for j, (s, m) in enumerate(((hg_hi, w2_hi), (hg_hi, w2_lo), (hg_lo, w2_hi))):
                    mm = pe.matmul(pb[:, 7, t * D:t * D + D], s[:, k, rows], m[:, k],
                                   start=(k == 0 and j == 0), stop=(k == FC - 1 and j == 2))
                if n == NT * FC - 1:
                    mm.then_inc(pe_w2, 1)

            def run_l(g, layer=None):
                a, b, c, par = l_roles(g)
                if a is not None:
                    pe.wait_ge(act_xhi, at(a, 1, 1))
                    pe.wait_ge(dve_xlo, at(a, 1, 1))
                    for t in range(NT):
                        for part in range(2):
                            project(a, t, part)
                if c is not None:
                    turn_h(c)
                if a is not None:
                    for t in range(NT):
                        project(a, t, 2)
                if c is not None:
                    for m in range(FC):
                        hidden(a, c, m)
                for j in range(UNITS + 3):
                    if b is not None and j < UNITS:
                        scores(a, b, c, j)
                    if b is not None and 2 <= j < UNITS + 2:
                        turn_p(a, b, j - 2)
                    if c is not None and 1 <= j <= 6:
                        feed(c, 2 * j - 2)
                        feed(c, 2 * j - 1)
                    if b is not None and j >= 3:
                        weigh(a, b, c, 1 - par, j - 3)
                if a is not None:
                    for k in range(4):
                        if k == 0:
                            pe.wait_ge(pool_qk, at(a, NT, NT))
                        if k == 2 and b is None:
                            pe.wait_ge(act_v, at(a, NT, 1))
                        for j in range(2):
                            for t in range(NT):
                                col = (2 * k + j) * P
                                mm = pe.transpose(pb[:, k, j * T + t * P:j * T + t * P + P],
                                                  r_cos[:, t, col:col + P], id_f[:])
                        mm.then_inc(pe_qkt, 1)
                    if not (isinstance(a, int) and a == ITEMS - 1):
                        turn_x(plus(a, 1))
                if b is not None:
                    pe.wait_ge(act_ohi, at(b, 2, 2))
                    pe.wait_ge(dve_olo, at(b, 2, 2))
                    if isinstance(b, int) and b == SEQS:
                        pe.wait_ge(w_lo, WEIGHT["wo1"])
                    if c is not None:
                        pe.wait_ge(dve_x2, at(c, 1, 1))
                    for t in range(NT):
                        rows = slice(t * P, t * P + P)
                        mm = split_product(pb[:, 7, t * D:t * D + D],
                                           [(o_hi[:, k, rows], o_lo[:, k, rows], wo_hi[:, k], wo_lo[:, k])
                                            for k in range(IC)], (True,))
                    mm.then_inc(pe_wo, 1)

            def between(g):
                if g == 0:
                    turn_x(0)
                    pe.wait_ge(w_lo, WEIGHT["w10"])
                elif g == SEQS:
                    pe.wait_ge(w_lo, WEIGHT["qkv1"])
                elif g == SEQS + 2:
                    pe.wait_ge(w_lo, WEIGHT["w11"])

            l_iterations(pe, run_l, between)

        @block.scalar
        def _(act):
            def split_hi(name, src, dst):
                nc.scalar.activation(dst, src, ACT.Copy).then_inc(w_hi, 1)

            act.wait_ge(raw_a_in, 32)
            split_hi("xq", raw_a[:, 0:KC * INNER].rearrange("p (c n) -> p c n", c=KC), xq_hi[:])
            split_hi("xo", raw_a[:, KC * INNER:KC * INNER + IC * D].rearrange("p (c n) -> p c n", c=IC), xo_hi[:])

            def x_turned(a):
                act.wait_ge(x_tr, at(a, 1, 1))
                nc.scalar.activation(xn_hi[:].rearrange("p c t -> p (c t)"), pb[:, 0], ACT.Copy).then_inc(x_thi, 1)
                act.wait_ge(c_tr, at(a, 1, 1))
                nc.scalar.activation(c_t[:], pb[:, 1, 0:2 * P].rearrange("p (c n) -> p c n", c=2)[:, :, 0:CTX],
                                     ACT.Copy).then_inc(c_cp, 1)

            def x_exps(b, u):
                act.wait_ge(x_max, at(b, XUNITS, u + 1))
                if later(b):
                    act.wait_ge(x_ptr, at(plus(b, -1), XUNITS, u + 1))
                for k in range(4):
                    e = nc.scalar.activation(x_p[:, u, k, :], pb[:, 2 + u % 2, k * P:k * P + CTX], ACT.Exp,
                                             bias=x_nm[:, u, k:k + 1], scale=1.0, accum_out=x_sum[:, u, k:k + 1])
                e.then_inc(x_exp, 1)

            def x_probs_copy(b, u):
                act.wait_ge(x_ptr, at(b, XUNITS, u + 1))
                if u >= 2 or later(b):
                    act.wait_ge(x_av, at(b, XUNITS, u - 1))
                nc.scalar.activation(x_pt[0:CTX, u % 2].rearrange("p k n -> p (k n)"), pb[0:CTX, u % 2],
                                     ACT.Copy).then_inc(x_ptc, 1)

            def run_x(g):
                a, b, par = x_roles(g)
                if isinstance(g, int) and g == 0:
                    x_turned(0)
                if b is not None:
                    x_exps(b, 0)
                    x_exps(b, 1)
                if a is not None:
                    for k in range(2):
                        act.wait_ge(x_pq, at(a, 2, k + 1))
                        nc.scalar.activation(xq_t[:, par, 2 * k:2 * k + 2].rearrange("p c t -> p (c t)"), pb[:, 4 + k],
                                             ACT.Copy, scale=DH ** -0.5).then_inc(x_cq, 1)
                if b is not None:
                    x_probs_copy(b, 0)
                    x_exps(b, 2)
                if a is not None:
                    act.wait_ge(x_pk, at(a, 1, 1))
                    nc.scalar.activation(xk_t[:, par], pb[:, 6].rearrange("p (c n) -> p c n", c=IC)[:, :, 0:CTX],
                                         ACT.Copy).then_inc(x_ck, 1)
                if b is not None:
                    x_probs_copy(b, 1)
                    x_exps(b, 3)
                if a is not None:
                    act.wait_ge(x_pv, at(a, 1, 1))
                    nc.scalar.activation(x_v[0:CTX, par], pb[0:CTX, 7], ACT.Copy).then_inc(x_cv, 1)
                if b is not None:
                    x_probs_copy(b, 2)
                    x_probs_copy(b, 3)
                    for k in range(2):
                        act.wait_ge(x_av, at(b, XUNITS, XUNITS))
                        nc.scalar.activation(xo_hi_t[:, 2 * k:2 * k + 2].rearrange("p c t -> p (c t)"), pb[:, 6 + k],
                                             ACT.Copy).then_inc(x_ohi, 1)
                if not isinstance(g, int) or g + 1 < SEQS:
                    x_turned(plus(a, 1))
                if isinstance(g, int) and g == 0:
                    act.wait_ge(raw_b_in, 32)
                    split_hi("wo0", raw_b[:, 0:IC * D].rearrange("p (c n) -> p c n", c=IC), wo_hi[:])
                    split_hi("w20", raw_b[:, IC * D:].rearrange("p (c n) -> p c n", c=FC), w2_hi[:])
                if isinstance(g, int) and g == SEQS - 1:
                    act.wait_ge(raw_a_in, 48)
                    split_hi("qkv0", raw_a[:].rearrange("p (c n) -> p c n", c=KC), wqkv_hi[:])
                if isinstance(g, int) and g == SEQS:
                    act.wait_ge(raw_a_in, 64)
                    split_hi("w10", raw_a[:, 0:KC * W1C * P].rearrange("p (c m n) -> p c m n", c=KC, n=P), w1_hi[:])

            x_iterations(act, run_x)

            act.wait_ge(stage_l, 1)
            act.wait_ge(zero_made, 2)

            def x_hi(n):
                act.wait_ge(pe_xt, at(n, 1, 1))
                dst = shifted(xt_hi)
                nc.scalar.activation(dst, pb[:, 4].rearrange("p (c t) -> p c t", c=KC), ACT.Copy).then_inc(act_xhi, 1)

            def run_l(g, layer=None):
                a, b, c, par = l_roles(g)
                if a is not None:
                    for t in range(NT):
                        act.wait_ge(pe_qkv, at(a, 6, 2 * t + 2))
                        if later(a):
                            act.wait_ge(pool_qk, at(plus(a, -1), NT, t + 1))
                        nc.scalar.activation(r_sin[:, t].rearrange("p (j n) -> p j n", j=2), pb[:, 3 * t:3 * t + 2],
                                             ACT.Square).then_inc(act_sq, 1)
                if c is not None:
                    act.wait_ge(pe_ht, at(c, 1, 1))
                    ly = layer_of(c, layer)
                    for k in range(KC):
                        nc.scalar.activation(h_f[:, k], pb[:, 7, k * T:k * T + T], ACT.Identity,
                                             bias=lnb_t[:, ly, k:k + 1], scale=lng_t[:, ly, k:k + 1]).then_inc(act_h, 1)
                if a is not None:
                    for t in range(NT):
                        act.wait_ge(pe_qkv, at(a, 6, 5 + t))
                        nc.scalar.activation(v_t[:, par, t], pb[:, 2 + 3 * t], ACT.Copy).then_inc(act_v, 1)
                if c is not None:
                    ly = layer_of(c, layer)
                    for m in range(FC):
                        act.wait_ge(pe_w1, at(c, FC, m + 1))
                        if m >= 2 or later(c):
                            act.wait_ge(dve_hg, at(c, FC, m - 1))
                        w = [6, 7, 2, 5, 6, 7][m]
                        if m < FC - 1:
                            e = nc.scalar.activation(gl[:, m % 2], pb[:, w, T:2 * T], ACT.Gelu,
                                                     bias=b1_t[:, ly, 1, m:m + 1])
                        else:
                            e = nc.scalar.activation(gl[0:TAIL, m % 2], pb[TAIL_G:TAIL_G + TAIL, w, 0:T], ACT.Gelu,
                                                     bias=b1_t[TAIL_G:TAIL_G + TAIL, ly, 1, m:m + 1])
                        e.then_inc(act_gelu, 1)
                if b is not None:
                    for j in range(UNITS + 2):
                        if j < UNITS:
                            heads = 2 if j < 4 else 4
                            keys = 512 // heads
                            act.wait_ge(dve_max, at(b, UNITS, j + 1))
                            if j >= 3 or later(b):
                                act.wait_ge(pe_pt, at(b, UNITS, j - 2))
                            for k in range(heads):
                                e = nc.scalar.activation(p_t[:, j % 3, k * keys:k * keys + keys],
                                                         pb[:, j % 3, k * keys:k * keys + keys], ACT.Exp,
                                                         bias=s_nm[:, j, k:k + 1], scale=1.0,
                                                         accum_out=s_sum[:, j, k:k + 1])
                            e.then_inc(act_exp, 1)
                        if j >= 2:
                            u = j - 2
                            act.wait_ge(pe_pt, at(b, UNITS, u + 1))
                            if u >= 2 or later(b):
                                act.wait_ge(pe_av, at(b, UNITS, u - 1))
                            nc.scalar.activation(pt_t[:, u % 2], pb[:, 3 + u % 2], ACT.Copy).then_inc(act_pt, 1)
                    for k in range(2):
                        act.wait_ge(pe_av, at(b, UNITS, UNITS))
                        nc.scalar.activation(o_hi[:, 2 * k:2 * k + 2].rearrange("p c t -> p (c t)"), pb[:, 5 + k],
                                             ACT.Copy).then_inc(act_ohi, 1)
                if a is not None:
                    for k in range(4):
                        act.wait_ge(pe_qkt, at(a, 4, k + 1))
                        nc.scalar.activation(qk_t[:, k // 2, 2 * (k % 2):2 * (k % 2) + 2].rearrange("p c t -> p (c t)"),
                                             pb[:, k], ACT.Copy).then_inc(act_qkt, 1)
                    if not (isinstance(a, int) and a == ITEMS - 1):
                        x_hi(plus(a, 1))

            def between(g):
                if g == 0:
                    x_hi(0)
                elif g == SEQS:
                    act.wait_ge(raw_a_in, 80)
                    act.wait_ge(pe_qkv, 6 * SEQS)
                    split_hi("qkv1", raw_a[:].rearrange("p (c n) -> p c n", c=KC), wqkv_hi[:])
                elif g == SEQS + 1:
                    act.wait_ge(raw_b_in, 64)
                    act.wait_ge(pe_wo, SEQS)
                    split_hi("wo1", raw_b[:, 0:IC * D].rearrange("p (c n) -> p c n", c=IC), wo_hi[:])
                elif g == SEQS + 2:
                    act.wait_ge(pe_w2, SEQS)
                    split_hi("w21", raw_b[:, IC * D:].rearrange("p (c n) -> p c n", c=FC), w2_hi[:])
                    act.wait_ge(raw_a_in, 96)
                    act.wait_ge(pe_w1, FC * SEQS)
                    split_hi("w11", raw_a[:, 0:KC * W1C * P].rearrange("p (c m n) -> p c m n", c=KC, n=P), w1_hi[:])

            l_iterations(act, run_l, between)

        @block.vector
        def _(dve):
            def split_lo(name, src, hi, lo):
                dve.wait_ge(w_hi, WEIGHT[name])
                nc.vector.tensor_tensor(lo, src, hi.bitcast(F32), ALU.subtract).then_inc(w_lo, 1)

            def aggregate(mean_var, stats, s_stats, s_out, n):
                dve.wait_ge(s_stats, at(n, 1, 1))
                dve.sem_inc(stats_seen, 1)
                for t in range(NT):
                    e = nc.vector.bn_aggr(mean_var[:, t], stats[:, t])
                e.then_inc(s_out, 1)

            def x_stats(a, par):
                dve.wait_ge(x_load[par], of_parity(a))
                for t in range(NT):
                    e = nc.vector.bn_stats(x_st[:, 0, t], x_in[:, par, t])
                e.then_inc(x_bst, 1)
                aggregate(x_mv[:, 0], x_st[:, 0], x_bst, x_bmv, a)

            def x_normed(a, par):
                dve.wait_ge(x_rst, at(a, 1, 1))
                dve.wait_ge(x_bmv, at(a, 1, 1))
                if later(a):
                    dve.wait_ge(x_tr, at(plus(a, -1), 1, 1))
                for t in range(NT):
                    e = nc.vector.tensor_scalar(xn[:, t], x_in[:, par, t], x_mv[:, 0, t, 0:1], x_rs[:, 0, t:t + 1],
                                                ALU.subtract, ALU.mult)
                e.then_inc(x_norm, 1)

            def x_turned_lo(a):
                dve.wait_ge(x_thi, at(a, 1, 1))
                nc.vector.tensor_tensor(xn_lo[:].rearrange("p c t -> p (c t)"), pb[:, 0],
                                        xn_hi[:].rearrange("p c t -> p (c t)").bitcast(F32),
                                        ALU.subtract).then_inc(x_tlo, 1)

            def x_maxes(b, u):
                dve.wait_ge(x_s, at(b, XUNITS, u + 1))
                nc.vector.tensor_reduce(x_nm[:, u], pb[:, 2 + u % 2].rearrange("p (k n) -> p k n", k=4)[:, :, 0:CTX],
                                        AX.X, ALU.max, negate=True).then_inc(x_max, 1)

            def x_norm_probs(b, u):
                dve.wait_ge(x_exp, at(b, XUNITS, u + 1))
                nc.vector.reciprocal(x_inv[:, u], x_sum[:, u]).then_inc(x_rec, 1)
                dve.wait_ge(x_rec, at(b, XUNITS, u + 1))
                nc.vector.tensor_tensor(x_p[:, u], x_p[:, u], x_inv[:, u].unsqueeze(2).broadcast_to([P, 4, CTX]),
                                        ALU.mult).then_inc(x_pn, 1)

            dve.wait_ge(zero_made, 1)
            split_lo("xq", raw_a[:, 0:KC * INNER].rearrange("p (c n) -> p c n", c=KC), xq_hi[:], xq_lo[:])
            split_lo("xo", raw_a[:, KC * INNER:KC * INNER + IC * D].rearrange("p (c n) -> p c n", c=IC), xo_hi[:], xo_lo[:])

            def run_x(g):
                a, b, par = x_roles(g)
                ahead = not isinstance(g, int) or g + 1 < SEQS
                if isinstance(g, int) and g == 0:
                    x_stats(0, 0)
                    x_normed(0, 0)
                    x_turned_lo(0)
                if b is not None:
                    x_maxes(b, 0)
                    x_maxes(b, 1)
                if ahead:
                    x_stats(plus(a, 1), 1 - par)
                if b is not None:
                    x_norm_probs(b, 0)
                    x_norm_probs(b, 1)
                if ahead:
                    x_normed(plus(a, 1), 1 - par)
                if b is not None:
                    x_maxes(b, 2)
                    x_norm_probs(b, 2)
                    x_maxes(b, 3)
                    x_norm_probs(b, 3)
                    for k in range(2):
                        dve.wait_ge(x_ohi, at(b, 2, k + 1))
                        hi = xo_hi_t[:, 2 * k:2 * k + 2].rearrange("p c t -> p (c t)")
                        nc.vector.tensor_tensor(xo_lo_t[:, 2 * k:2 * k + 2].rearrange("p c t -> p (c t)"), pb[:, 6 + k],
                                                hi.bitcast(F32), ALU.subtract).then_inc(x_olo, 1)
                if ahead:
                    x_turned_lo(plus(a, 1))
                if b is not None:
                    dve.wait_ge(x_wo, at(b, 1, 1))
                    dve.wait_ge(x_bias, at(b, 1, 1))
                    if later(b):
                        dve.wait_ge(x1_store, at(plus(b, -1), 16, 16))
                    nc.vector.tensor_tensor(x1_x[:].rearrange("p t d -> p (t d)"), pb[:, 4],
                                            x_b[:, 1 - par].rearrange("p t d -> p (t d)"), ALU.add).then_inc(x_res1, 1)
                    dve.wait_ge(x_res1, at(b, 1, 1))
                    for t in range(NT):
                        e = nc.vector.bn_stats(x_st[:, 1, t], x1_x[:, t])
                    e.then_inc(y_bst, 1)
                    aggregate(x_mv[:, 1], x_st[:, 1], y_bst, y_bmv, b)
                    dve.wait_ge(y_rst, at(b, 1, 1))
                    dve.wait_ge(y_bmv, at(b, 1, 1))
                    if later(b):
                        dve.wait_ge(y_store, at(plus(b, -1), 16, 16))
                    for t in range(NT):
                        e = nc.vector.tensor_scalar(y_x[:, t], x1_x[:, t], x_mv[:, 1, t, 0:1], x_rs[:, 1, t:t + 1],
                                                    ALU.subtract, ALU.mult)
                    e.then_inc(y_norm, 1)
                if isinstance(g, int) and g == 0:
                    dve.wait_ge(const_in, CONSTS)
                    nc.vector.tensor_copy(id_b[:], id_f[:]).then_inc(const_made, 1)
                    nc.vector.tensor_copy(mask_b[:], mask_raw[:]).then_inc(const_made, 1)
                    for layer in range(LAYERS):
                        for j, tab in enumerate((cos_t, sin_t)):
                            nc.vector.tensor_tensor(
                                tab[:, layer].rearrange("p t j d -> p t (j d)"),
                                rope_raw[:, j].rearrange("p t j d -> p t (j d)"),
                                sc_t[:, layer, j].rearrange("p j d -> p (j d)").unsqueeze(1).broadcast_to([P, NT, 2 * DH]),
                                ALU.mult).then_inc(const_made, 1)
                    split_lo("wo0", raw_b[:, 0:IC * D].rearrange("p (c n) -> p c n", c=IC), wo_hi[:], wo_lo[:])
                    split_lo("w20", raw_b[:, IC * D:].rearrange("p (c n) -> p c n", c=FC), w2_hi[:], w2_lo[:])
                if isinstance(g, int) and g == SEQS - 1:
                    split_lo("qkv0", raw_a[:].rearrange("p (c n) -> p c n", c=KC), wqkv_hi[:], wqkv_lo[:])
                if isinstance(g, int) and g == SEQS:
                    split_lo("w10", raw_a[:, 0:KC * W1C * P].rearrange("p (c m n) -> p c (m n)", c=KC, n=P),
                             w1_hi[:].rearrange("p c m n -> p c (m n)"), w1_lo[:].rearrange("p c m n -> p c (m n)"))

            x_iterations(dve, run_x)

            dve.wait_ge(stage_l, 1)
            dve.wait_ge(zero_made, 2)

            def x_lo(n):
                dve.wait_ge(act_xhi, at(n, 1, 1))
                nc.vector.tensor_tensor(shifted(xt_lo), pb[:, 4].rearrange("p (c t) -> p c t", c=KC),
                                        shifted(xt_hi).bitcast(F32), ALU.subtract).then_inc(dve_xlo, 1)

            def norm_h(c):
                dve.wait_ge(pe_wo, at(c, 1, 1))
                dve.wait_ge(res_load, at(c, 16, 16))
                if later(c):
                    dve.wait_ge(pool_x1b, at(plus(c, -1), 1, 1))
                nc.vector.tensor_tensor(x1[:, :, 0:3:2], pb[:, 7].rearrange("p (t c n) -> p t c n", t=NT, c=KC),
                                        x_res[:].rearrange("p t (c n) -> p t c n", c=KC), ALU.add).then_inc(dve_x1, 1)
                dve.wait_ge(shift, at(c, 48, 48))
                for t in range(NT):
                    e = nc.vector.bn_stats(l_st[:, t], x1[:, t, 0:2].rearrange("p c n -> p (c n)"))
                e.then_inc(dve_bst, 1)
                aggregate(l_mv, l_st, dve_bst, dve_bmv, c)
                dve.wait_ge(pool_rst, at(c, 1, 1))
                dve.wait_ge(dve_bmv, at(c, 1, 1))
                for t in range(NT):
                    e = nc.vector.tensor_scalar(h_n[:, t], x1[:, t, 0:2].rearrange("p c n -> p (c n)"), l_mv[:, t, 0:1],
                                                l_rs[:, t:t + 1], ALU.subtract, ALU.mult)
                e.then_inc(dve_h, 1)

            def squares(a, t):
                dve.wait_ge(act_sq, at(a, NT, t + 1))
                nc.vector.tensor_reduce(n_sq[:, t], r_sin[:, t].rearrange("p (h d) -> p h d", d=DH), AX.X,
                                        ALU.add).then_inc(dve_ss, 1)

            def rotate(a, t, layer):
                ly = layer_of(a, layer)
                qk = pb[:, 3 * t:3 * t + 2]
                nc.vector.tensor_tensor(
                    r_cos[:, t].rearrange("p (j h d) -> p j h d", j=2, d=DH),
                    qk.rearrange("p j (h d) -> p j h d", d=DH),
                    cos_t[:, ly, t].unsqueeze(2).broadcast_to([P, 2, HEADS, DH]), ALU.mult)
                dve.wait_ge(dve_ss, at(a, NT, t + 1))
                nc.vector.tensor_scalar(n_cl[:, t], n_sq[:, t], NORM_MIN_SQ, None, ALU.max).then_inc(dve_cl, 1)
                half = DH // 2
                for s in range(2):
                    o = r_sin[:, t].rearrange("p (j h d) -> p j h d", j=2, d=DH)[:, :, :, s * half:s * half + half]
                    i = qk.rearrange("p j (h d) -> p j h d", d=DH)[:, :, :, half - s * half:DH - s * half]
                    w = sin_t[:, ly, t, :, s * half:s * half + half].unsqueeze(2).broadcast_to([P, 2, HEADS, half])
                    e = nc.vector.tensor_tensor(o, i, w, ALU.mult)
                e.then_inc(dve_rope, 1)

            def run_l(g, layer=None):
                a, b, c, par = l_roles(g)
                if c is not None:
                    norm_h(c)
                if a is not None:
                    squares(a, 0)
                    rotate(a, 0, layer)
                    squares(a, 1)
                if c is not None:
                    dve.wait_ge(act_h, at(c, KC, KC))
                    flat = lambda t: t[:].rearrange("p c t -> p (c t)")
                    nc.vector.tensor_copy(flat(h_hi), flat(h_f)).then_inc(dve_hhi, 1)
                    dve.wait_ge(dve_hhi, at(c, 1, 1))
                    nc.vector.tensor_tensor(flat(h_lo), flat(h_f), flat(h_hi).bitcast(F32), ALU.subtract).then_inc(dve_hlo, 1)
                if a is not None:
                    rotate(a, 1, layer)
                if c is not None:
                    ly = layer_of(c, layer)
                    for m in range(FC + 1):
                        if m < FC:
                            w = [6, 7, 2, 5, 6, 7][m]
                            rows = P if m < FC - 1 else TAIL
                            dve.wait_ge(act_gelu, at(c, FC, m + 1))
                            if m >= 2 or later(c):
                                dve.wait_ge(pool_hglo, at(c, FC, m - 1))
                            nc.vector.scalar_tensor_tensor(out=hg[0:rows, m % 2], in0=pb[0:rows, w, 0:T],
                                                           scalar=b1_t[0:rows, ly, 0, m:m + 1], in1=gl[0:rows, m % 2],
                                                           op0=ALU.add, op1=ALU.mult).then_inc(dve_hg, 1)
                        if m >= 1:
                            k = m - 1
                            rows = P if k < FC - 1 else TAIL
                            dve.wait_ge(dve_hg, at(c, FC, k + 1))
                            nc.vector.tensor_copy(hg_hi[0:rows, k], hg[0:rows, k % 2]).then_inc(dve_hghi, 1)
                if b is not None:
                    for j in range(UNITS + 1):
                        if j < UNITS:
                            heads = 2 if j < 4 else 4
                            dve.wait_ge(pe_s, at(b, UNITS, j + 1))
                            nc.vector.tensor_reduce(s_nm[:, j, 0:heads], pb[:, j % 3].rearrange("p (k n) -> p k n", k=heads),
                                                    AX.X, ALU.max, negate=True).then_inc(dve_max, 1)
                        if j >= 1:
                            u = j - 1
                            heads = 2 if u < 4 else 4
                            dve.wait_ge(act_exp, at(b, UNITS, u + 1))
                            nc.vector.reciprocal(s_inv[:, u, 0:heads], s_sum[:, u, 0:heads]).then_inc(dve_rec, 1)
                            dve.wait_ge(dve_rec, at(b, UNITS, u + 1))
                            pu = p_t[:, u % 3].rearrange("p (k n) -> p k n", k=heads)
                            nc.vector.tensor_tensor(pu, pu, s_inv[:, u, 0:heads].unsqueeze(2).broadcast_to(
                                [P, heads, 512 // heads]), ALU.mult).then_inc(dve_pn, 1)
                if c is not None:
                    dve.wait_ge(pe_w2, at(c, 1, 1))
                    if layer_of(c, layer) == LAYERS - 1:
                        dve.wait_ge(pool_x1o, at(plus(c, -SEQS), 1, 1))
                    else:
                        dve.wait_ge(pool_x1b, at(c, 1, 1))
                    if not isinstance(c, int) or c >= 2:
                        dve.wait_ge(x2_store, at(plus(c, -2), 16, 16))
                    nc.vector.tensor_tensor(x2[:, par].rearrange("p t d -> p (t d)"), pb[:, 7],
                                            x1b[:].rearrange("p t d -> p (t d)"), ALU.add).then_inc(dve_x2, 1)
                if b is not None:
                    for k in range(2):
                        dve.wait_ge(act_ohi, at(b, 2, k + 1))
                        hi = o_hi[:, 2 * k:2 * k + 2].rearrange("p c t -> p (c t)")
                        nc.vector.tensor_tensor(o_lo[:, 2 * k:2 * k + 2].rearrange("p c t -> p (c t)"), pb[:, 5 + k],
                                                hi.bitcast(F32), ALU.subtract).then_inc(dve_olo, 1)
                if a is not None and not (isinstance(a, int) and a == ITEMS - 1):
                    x_lo(plus(a, 1))

            def between(g):
                if g == 0:
                    dve.wait_ge(const_made, 2 + 2 * LAYERS)
                    x_lo(0)
                elif g == SEQS:
                    split_lo("qkv1", raw_a[:].rearrange("p (c n) -> p c n", c=KC), wqkv_hi[:], wqkv_lo[:])
                elif g == SEQS + 1:
                    split_lo("wo1", raw_b[:, 0:IC * D].rearrange("p (c n) -> p c n", c=IC), wo_hi[:], wo_lo[:])
                elif g == SEQS + 2:
                    split_lo("w21", raw_b[:, IC * D:].rearrange("p (c n) -> p c n", c=FC), w2_hi[:], w2_lo[:])
                    split_lo("w11", raw_a[:, 0:KC * W1C * P].rearrange("p (c m n) -> p c (m n)", c=KC, n=P),
                             w1_hi[:].rearrange("p c m n -> p c (m n)"), w1_lo[:].rearrange("p c m n -> p c (m n)"))

            l_iterations(dve, run_l, between)

        @block.gpsimd
        def _(pool):
            nc.gpsimd.memset(half_neg[:], -0.5)
            nc.gpsimd.memset(eps_t[:], EPS)
            nc.gpsimd.memset(c_in[:], 0.0).then_inc(zero_made, 1)

            def deviation(var, eps_out, out, n, s_in, s_in_v, s_eps, s_out):
                pool.wait_ge(s_in, s_in_v)
                nc.gpsimd.tensor_tensor(eps_out, var, eps_t[:], ALU.add).then_inc(s_eps, 1)
                pool.wait_ge(s_eps, at(n, 1, 1))
                nc.gpsimd.tensor_tensor(out, eps_out, half_neg[:, 0:NT], ALU.pow).then_inc(s_out, 1)

            def x_bias_rows(a, par):
                pool.wait_ge(x_load[par], of_parity(a))
                if not isinstance(a, int) or a >= 2:
                    pool.wait_ge(x_res1, at(plus(a, -2), 1, 1))
                nc.gpsimd.tensor_tensor(x_b[:, par], x_in[:, par], bo_t[:].unsqueeze(1).broadcast_to([P, NT, D]),
                                        ALU.add).then_inc(x_bias, 1)

            def run_x(g):
                a, b, par = x_roles(g)
                ahead = not isinstance(g, int) or g + 1 < SEQS
                if isinstance(g, int) and g == 0:
                    deviation(x_mv[:, 0, :, 1], x_ve[:, 0], x_rs[:, 0], 0, x_bmv, 1, x_eps, x_rst)
                    pool.wait_ge(const_in, CONSTS)
                    x_bias_rows(0, 0)
                if ahead:
                    n = plus(a, 1)
                    deviation(x_mv[:, 0, :, 1], x_ve[:, 0], x_rs[:, 0], n, x_bmv, at(n, 1, 1), x_eps, x_rst)
                    x_bias_rows(n, 1 - par)
                if b is not None:
                    deviation(x_mv[:, 1, :, 1], x_ve[:, 1], x_rs[:, 1], b, y_bmv, at(b, 1, 1), y_eps, y_rst)

            x_iterations(pool, run_x)

            pool.wait_ge(stage_l, 1)
            nc.gpsimd.memset(xt_hi[:, T:T + 1].bitcast(F32), 0.0)
            nc.gpsimd.memset(xt_lo[:, T:T + 1].bitcast(F32), 0.0)
            nc.gpsimd.memset(x1[0:1, 0, 1], 0.0)
            nc.gpsimd.memset(hg_hi[:, FC - 1].bitcast(F32), 0.0)
            nc.gpsimd.memset(hg_lo[:, FC - 1].bitcast(F32), 0.0).then_inc(zero_made, 1)

            def norm_qk(a, t):
                pool.wait_ge(dve_cl, at(a, NT, t + 1))
                nc.gpsimd.tensor_tensor(n_inv[:, t], n_cl[:, t], half_neg[:], ALU.pow).then_inc(pool_inv, 1)
                pool.wait_ge(dve_rope, at(a, NT, t + 1))
                nc.gpsimd.tensor_tensor(r_cos[:, t], r_cos[:, t], r_sin[:, t], ALU.add).then_inc(pool_sum, 1)
                pool.wait_ge(pool_inv, at(a, NT, t + 1))
                pool.wait_ge(pool_sum, at(a, NT, t + 1))
                rows = r_cos[:, t].rearrange("p (h d) -> p h d", d=DH)
                nc.gpsimd.tensor_tensor(rows, rows, n_inv[:, t].unsqueeze(2).broadcast_to([P, 2 * HEADS, DH]),
                                        ALU.mult).then_inc(pool_qk, 1)

            def run_l(g, layer=None):
                a, b, c, par = l_roles(g)
                if c is not None:
                    ly = layer_of(c, layer)
                    pool.wait_ge(dve_x1, at(c, 1, 1))
                    if later(c):
                        pool.wait_ge(dve_x2, at(plus(c, -1), 1, 1))
                    nc.gpsimd.tensor_tensor(x1b[:].rearrange("p t (c n) -> p t c n", c=KC), x1[:, :, 0:3:2],
                                            b2_t[:, ly].rearrange("p (c n) -> p c n", c=KC).unsqueeze(1).broadcast_to(
                                                [P, NT, KC, P]), ALU.add).then_inc(pool_x1b, 1)
                    deviation(l_mv[:, :, 1], l_ve[:], l_rs[:], c, dve_bmv, at(c, 1, 1), pool_eps, pool_rst)
                    if ly == LAYERS - 1:
                        pool.wait_ge(pool_x1b, at(c, 1, 1))
                        pool.wait_ge(orig_load, at(plus(c, -SEQS), 16, 16))
                        nc.gpsimd.tensor_tensor(x1b[:], x1b[:], x_orig[:], ALU.add).then_inc(pool_x1o, 1)
                if a is not None:
                    norm_qk(a, 0)
                if c is not None:
                    for m in range(FC):
                        rows = P if m < FC - 1 else TAIL
                        pool.wait_ge(dve_hghi, at(c, FC, m + 1))
                        nc.gpsimd.tensor_tensor(hg_lo[0:rows, m], hg[0:rows, m % 2], hg_hi[0:rows, m].bitcast(F32),
                                                ALU.subtract).then_inc(pool_hglo, 1)
                if a is not None:
                    norm_qk(a, 1)

            l_iterations(pool, run_l, lambda g: None)


def kernel(x, ctx_768, L0_xattn_Wq, L0_xattn_Wk, L0_xattn_Wv, L0_xattn_Wo, L0_xattn_bo, L0_ffn_wqkv, L0_ffn_q_scale,
           L0_ffn_k_scale, L0_ffn_wo, L0_ffn_ln_g, L0_ffn_ln_b, L0_ffn_w1, L0_ffn_b1, L0_ffn_w2, L0_ffn_b2):
    import concourse.bacc as bacc
    from concourse.bass_utils import run_bass_kernel_spmd

    def rows_padded(w, rows):
        w = np.asarray(w)
        p = np.zeros(w.shape[:-2] + (rows,) + w.shape[-1:], w.dtype)
        p[..., :w.shape[-2], :] = w
        return p

    w1 = np.asarray(L0_ffn_w1)
    b1 = np.asarray(L0_ffn_b1)
    w1_p = np.zeros((LAYERS, D, W1C, P), w1.dtype)
    b1_p = np.zeros((LAYERS, P, 2, FC), b1.dtype)
    for m in range(FC):
        n = P if m < FC - 1 else TAIL
        for part in range(2):
            src = slice(part * HID + m * P, part * HID + m * P + n)
            chunk, to = (2 * m + part, 0) if m < FC - 1 else (W1C - 1, part * TAIL_G)
            w1_p[:, :, chunk, to:to + n] = w1[:, :, src]
            b1_p[:, to:to + n, part, m] = b1[:, src]
    by_channel = lambda v: np.ascontiguousarray(np.asarray(v).reshape(LAYERS, KC, P).transpose(0, 2, 1))

    arrays = {
        "x": np.asarray(x), "ctx": np.asarray(ctx_768),
        "xwq": np.asarray(L0_xattn_Wq), "xwk": rows_padded(L0_xattn_Wk, 2 * P), "xwv": rows_padded(L0_xattn_Wv, 2 * P),
        "xwo": np.asarray(L0_xattn_Wo), "xbo": np.asarray(L0_xattn_bo),
        "wqkv": np.asarray(L0_ffn_wqkv), "qsc": np.asarray(L0_ffn_q_scale), "ksc": np.asarray(L0_ffn_k_scale),
        "wo": np.asarray(L0_ffn_wo), "lng": by_channel(L0_ffn_ln_g), "lnb": by_channel(L0_ffn_ln_b),
        "w1": w1_p.reshape(LAYERS, D, W1C * P), "b1": b1_p,
        "w2": rows_padded(L0_ffn_w2, FC * P), "b2": np.asarray(L0_ffn_b2),
        "rope": rope_tables(), "mask": masks(), "ident": np.eye(P, dtype=np.float32),
    }
    nc = bacc.Bacc("TRN2", target_bir_lowering=False, num_devices=1)
    args = []
    for name, a in arrays.items():
        arrays[name] = a = np.ascontiguousarray(a)
        args.append(nc.dram_tensor(name, a.shape, mybir.dt.from_np(a.dtype), kind="ExternalInput").ap())
    args.append(nc.dram_tensor("out", (SEQS, T, D), F32, kind="ExternalOutput").ap())
    build(nc, *args)
    r = run_bass_kernel_spmd(nc, [arrays], core_ids=[0])
    return r.results[0]["out"]
```

```python
from contextlib import ExitStack

import numpy as np

import concourse.bass as bass
from concourse import mybir

F32 = mybir.dt.float32
F32R = mybir.dt.float32r
BF16 = mybir.dt.bfloat16
ALU = mybir.AluOpType
ACT = mybir.ActivationFunctionType
AX = mybir.AxisListType

P = 128
SEQS, T, D = 16, 256, 256
NT = T // P
KC = D // P
HEADS, DH = 8, 64
INNER = HEADS * DH
IC = INNER // P
CTX, CD = 77, 192
LAYERS = 2
ITEMS = LAYERS * SEQS
HID = int(D * 4 * 2 / 3)
FC = -(-HID // P)
TAIL = HID - (FC - 1) * P
TAIL_G = 64
W1C = 2 * (FC - 1) + 1
QKV = 3 * INNER
EPS = 1e-5
NORM_MIN_SQ = 1e-24
QK_SCALE = 8.0
WINDOW = 128
MASKED = -1e30
UNITS = 6
XUNITS = 4

WEIGHT = {name: n + 1 for n, name in enumerate(
    ["xq", "xo", "wo0", "w20", "qkv0", "w10", "qkv1", "wo1", "w21", "w11"])}


def rope_tables():
    half = np.arange(0, DH, 2, dtype=np.float32)
    freq = np.arange(T, dtype=np.float32)[:, None] * (1.0 / 10000.0 ** (half / DH))[None, :]
    base = (half + 0.4 * DH) / (1.4 * DH)
    power = (np.arange(T, dtype=np.float32) - T // 2) / float(WINDOW // 2)
    scale = (base[None, :] ** power[:, None]).astype(np.float32)
    cos, sin = np.cos(freq.astype(np.float32)), np.sin(freq.astype(np.float32))
    q = scale * np.float32(QK_SCALE)
    k = np.float32(1.0) / scale
    out = np.empty((2, T, 2, DH), np.float32)
    for j, s in enumerate((q, k)):
        out[0, :, j] = np.concatenate([cos * s, cos * s], -1)
        out[1, :, j] = np.concatenate([-sin * s, sin * s], -1)
    return np.ascontiguousarray(out.reshape(2, NT, P, 2, DH).transpose(2, 0, 1, 3, 4))


def masks():
    i, j = np.arange(P)[:, None], np.arange(P)[None, :]
    before = np.where(j < i, MASKED, 0.0)
    own = np.where(j > i, MASKED, 0.0)
    return np.concatenate([before, own, before, own, own, own, own, own], 1).astype(np.float32)


def at(n, per, k):
    if isinstance(n, int):
        return n * per + k
    i, c = n
    return i * (2 * per) + (c * per + k)


def of_parity(n):
    return 16 * (n // 2 + 1) if isinstance(n, int) else n[0] * 16 + 16 * (n[1] // 2 + 1)


def plus(n, d):
    return n + d if isinstance(n, int) else (n[0], n[1] + d)


def index(n):
    return n if isinstance(n, int) else n[0] * 2 + n[1]


def later(n):
    return not (isinstance(n, int) and n == 0)


def build(nc, x, ctx_in, xwq, xwk, xwv, xwo, xbo, wqkv, qsc, ksc, wo, lng, lnb, w1, b1, w2, b2, rope, mask, ident, out):
    ctx = ExitStack()
    with ctx:
        def sb(name, shape, dt=F32, where=ctx):
            return where.enter_context(nc.sbuf_tensor(name, shape, dt))

        def sem(name):
            return ctx.enter_context(nc.semaphore(name))

        y_dram = nc.dram_tensor("y_state", (SEQS, P, NT, D), F32, kind="Internal").ap()
        x1_dram = nc.dram_tensor("x1_state", (SEQS, P, NT, D), F32, kind="Internal").ap()

        pb = ctx.enter_context(nc.psum_tensor("pb", [P, 8, 512], F32))
        id_f = sb("id_f", [P, P])
        id_b = sb("id_b", [P, P], BF16)
        mask_b = sb("mask_b", [P, 2, 512], BF16)
        half_neg = sb("half_neg", [P, 2 * HEADS])
        eps_t = sb("eps_t", [P, NT])
        cos_t = sb("cos_t", [P, LAYERS, NT, 2, DH])
        sin_t = sb("sin_t", [P, LAYERS, NT, 2, DH])
        b2_t = sb("b2_t", [P, LAYERS, D])
        bo_t = sb("bo_t", [P, D])
        b1_t = sb("b1_t", [P, LAYERS, 2, FC])
        lng_t = sb("lng_t", [P, LAYERS, KC])
        lnb_t = sb("lnb_t", [P, LAYERS, KC])
        wqkv_hi = sb("wqkv_hi", [P, KC, QKV], F32R)
        wqkv_lo = sb("wqkv_lo", [P, KC, QKV], F32R)
        wo_hi = sb("wo_hi", [P, IC, D], F32R)
        wo_lo = sb("wo_lo", [P, IC, D], F32R)
        w1_hi = sb("w1_hi", [P, KC, W1C, P], F32R)
        w1_lo = sb("w1_lo", [P, KC, W1C, P], F32R)
        w2_hi = sb("w2_hi", [P, FC, D], F32R)
        w2_lo = sb("w2_lo", [P, FC, D], F32R)
        raw_a = sb("raw_a", [P, KC * QKV])
        raw_b = sb("raw_b", [P, (IC + FC) * D])

        X = ExitStack()
        rope_raw = sb("rope_raw", [P, 2, NT, 2, DH], where=X)
        sc_t = sb("sc_t", [P, LAYERS, 2, 2, DH], where=X)
        mask_raw = sb("mask_raw", [P, 2, 512], where=X)
        xq_hi = sb("xq_hi", [P, KC, INNER], F32R, X)
        xq_lo = sb("xq_lo", [P, KC, INNER], F32R, X)
        xo_hi = sb("xo_hi", [P, IC, D], F32R, X)
        xo_lo = sb("xo_lo", [P, IC, D], F32R, X)
        xk_w = sb("xk_w", [P, 2, INNER], where=X)
        xv_w = sb("xv_w", [P, 2, INNER], where=X)
        x_in = sb("x_in", [P, 2, NT, D], where=X)
        x_b = sb("x_b", [P, 2, NT, D], where=X)
        c_in = sb("c_in", [P, 2, D], where=X)
        xn = sb("xn", [P, NT, D], where=X)
        xn_hi = sb("xn_hi", [P, KC, T], F32R, X)
        xn_lo = sb("xn_lo", [P, KC, T], F32R, X)
        c_t = sb("c_t", [P, 2, CTX], where=X)
        xq_t = sb("xq_t", [P, 2, IC, T], where=X)
        xk_t = sb("xk_t", [P, 2, IC, CTX], where=X)
        x_v = sb("x_v", [P, 2, INNER], where=X)
        x_p = sb("x_p", [P, XUNITS, 4, CTX], where=X)
        x_pt = sb("x_pt", [P, XUNITS, 4, P], where=X)
        xo_hi_t = sb("xo_hi_t", [P, IC, T], F32R, X)
        xo_lo_t = sb("xo_lo_t", [P, IC, T], F32R, X)
        x1_x = sb("x1_x", [P, NT, D], where=X)
        y_x = sb("y_x", [P, NT, D], where=X)
        x_st = sb("x_st", [P, 2, NT, 6], where=X)
        x_mv = sb("x_mv", [P, 2, NT, 2], where=X)
        x_ve = sb("x_ve", [P, 2, NT], where=X)
        x_rs = sb("x_rs", [P, 2, NT], where=X)
        x_nm = sb("x_nm", [P, XUNITS, 4], where=X)
        x_sum = sb("x_sum", [P, XUNITS, 4], where=X)
        x_inv = sb("x_inv", [P, XUNITS, 4], where=X)
        X.close()

        L = ctx.enter_context(ExitStack())
        x_cur = sb("x_cur", [P, NT, D], where=L)
        x_res = sb("x_res", [P, NT, D], where=L)
        x_orig = sb("x_orig", [P, NT, D], where=L)
        xt_hi = sb("xt_hi", [P, 2 * T + 1], F32R, L)
        xt_lo = sb("xt_lo", [P, 2 * T + 1], F32R, L)
        r_cos = sb("r_cos", [P, NT, 2 * INNER], where=L)
        r_sin = sb("r_sin", [P, NT, 2 * INNER], where=L)
        n_sq = sb("n_sq", [P, NT, 2 * HEADS], where=L)
        n_cl = sb("n_cl", [P, NT, 2 * HEADS], where=L)
        n_inv = sb("n_inv", [P, NT, 2 * HEADS], where=L)
        qk_t = sb("qk_t", [P, 2, IC, T], where=L)
        v_t = sb("v_t", [P, 2, NT, INNER], where=L)
        p_t = sb("p_t", [P, 3, 512], where=L)
        pt_t = sb("pt_t", [P, 2, 512], where=L)
        s_nm = sb("s_nm", [P, UNITS, 4], where=L)
        s_sum = sb("s_sum", [P, UNITS, 4], where=L)
        s_inv = sb("s_inv", [P, UNITS, 4], where=L)
        o_hi = sb("o_hi", [P, IC, T], F32R, L)
        o_lo = sb("o_lo", [P, IC, T], F32R, L)
        x1 = sb("x1", [P, NT, 3, P], where=L)
        x1b = sb("x1b", [P, NT, D], where=L)
        l_st = sb("l_st", [P, NT, 6], where=L)
        l_mv = sb("l_mv", [P, NT, 2], where=L)
        l_ve = sb("l_ve", [P, NT], where=L)
        l_rs = sb("l_rs", [P, NT], where=L)
        h_n = sb("h_n", [P, NT, D], where=L)
        h_f = sb("h_f", [P, KC, T], where=L)
        h_hi = sb("h_hi", [P, KC, T], F32R, L)
        h_lo = sb("h_lo", [P, KC, T], F32R, L)
        gl = sb("gl", [P, 2, T], where=L)
        hg = sb("hg", [P, FC, T], where=L)
        hg_hi = sb("hg_hi", [P, FC, T], F32R, L)
        hg_lo = sb("hg_lo", [P, FC, T], F32R, L)
        x2 = sb("x2", [P, 2, NT, D], where=L)

        const_in = sem("const_in")
        raw_a_in, raw_b_in = sem("raw_a_in"), sem("raw_b_in")
        w_hi, w_lo = sem("w_hi"), sem("w_lo")
        const_made = sem("const_made")
        zero_made = sem("zero_made")
        x_load, c_load = [sem(f"x_load{u}") for u in range(2)], [sem(f"c_load{u}") for u in range(2)]
        x_bst, x_bmv = sem("x_bst"), sem("x_bmv")
        x_eps, x_rst = sem("x_eps"), sem("x_rst")
        x_norm = sem("x_norm")
        x_bias = sem("x_bias")
        x_tr, c_tr = sem("x_tr"), sem("c_tr")
        x_thi, x_tlo = sem("x_thi"), sem("x_tlo")
        c_cp = sem("c_cp")
        x_pq, x_pk, x_pv = sem("x_pq"), sem("x_pk"), sem("x_pv")
        x_cq, x_ck, x_cv = sem("x_cq"), sem("x_ck"), sem("x_cv")
        x_s, x_max, x_exp, x_rec, x_pn = sem("x_s"), sem("x_max"), sem("x_exp"), sem("x_rec"), sem("x_pn")
        x_ptr, x_ptc, x_av = sem("x_ptr"), sem("x_ptc"), sem("x_av")
        x_ohi, x_olo, x_wo = sem("x_ohi"), sem("x_olo"), sem("x_wo")
        x_res1, y_bst, y_bmv, y_eps, y_rst, y_norm = [sem(n) for n in (
            "x_res1", "y_bst", "y_bmv", "y_eps", "y_rst", "y_norm")]
        x1_store, y_store = sem("x1_store"), sem("y_store")
        stats_seen = sem("stats_seen")
        stage_l = sem("stage_l")
        cur_load, res_load, orig_load, shift, x2_store = [sem(n) for n in (
            "cur_load", "res_load", "orig_load", "shift", "x2_store")]
        pe_xt, act_xhi, dve_xlo = sem("pe_xt"), sem("act_xhi"), sem("dve_xlo")
        pe_qkv, act_sq, act_v = sem("pe_qkv"), sem("act_sq"), sem("act_v")
        dve_ss, dve_cl, dve_rope = sem("dve_ss"), sem("dve_cl"), sem("dve_rope")
        pool_inv, pool_sum, pool_qk = sem("pool_inv"), sem("pool_sum"), sem("pool_qk")
        pe_qkt, act_qkt = sem("pe_qkt"), sem("act_qkt")
        pe_s, dve_max, act_exp, dve_rec, dve_pn = sem("pe_s"), sem("dve_max"), sem("act_exp"), sem("dve_rec"), sem("dve_pn")
        pe_pt, act_pt, pe_av, act_ohi, dve_olo = sem("pe_pt"), sem("act_pt"), sem("pe_av"), sem("act_ohi"), sem("dve_olo")
        pe_wo, dve_x1, pool_x1b, pool_x1o = sem("pe_wo"), sem("dve_x1"), sem("pool_x1b"), sem("pool_x1o")
        dve_bst, dve_bmv, pool_eps, pool_rst, dve_h = [sem(n) for n in ("dve_bst", "dve_bmv", "pool_eps", "pool_rst", "dve_h")]
        pe_ht, act_h, dve_hhi, dve_hlo = sem("pe_ht"), sem("act_h"), sem("dve_hhi"), sem("dve_hlo")
        pe_w1, act_gelu, dve_hg, dve_hghi, pool_hglo = [sem(n) for n in ("pe_w1", "act_gelu", "dve_hg", "dve_hghi", "pool_hglo")]
        pe_w2, dve_x2 = sem("pe_w2"), sem("dve_x2")

        CONSTS = 0

        x_rows = x.rearrange("s (t p) d -> s p t d", p=P)
        out_rows = out.rearrange("s (t p) d -> s p t d", p=P)

        def one(t, n):
            return t[bass.ds(n, 1)].rearrange("o p t d -> p (o t) d")

        def x_iterations(eng, run):
            for g in range(3):
                run(g)
            with eng.Fori(1, SEQS // 2 - 1) as i:
                for u in range(2):
                    run((i, u + 1))
            for g in range(SEQS - 1, SEQS + 2):
                run(g)

        def x_roles(g):
            whole = isinstance(g, int)
            a = None if whole and g >= SEQS else g
            b = None if whole and not 1 <= g <= SEQS else plus(g, -1)
            d = None if whole and g < 2 else plus(g, -2)
            return a, b, d, (g if whole else g[1]) % 2

        def l_iterations(eng, run, between):
            for layer in range(LAYERS):
                first = layer * SEQS
                between(first)
                run(first)
                between(first + 1)
                run(first + 1)
                between(first + 2)
                peeled = 2 if layer else 4
                for g in range(first + 2, first + peeled):
                    run(g)
                ends = first + SEQS - (2 if layer else 0)
                with eng.Fori((first + peeled) // 2, ends // 2) as i:
                    for u in range(2):
                        run((i, u), layer)
            for g in range(ITEMS - 2, ITEMS + 2):
                run(g)

        def l_roles(g):
            a = g if not isinstance(g, int) or g < ITEMS else None
            b = plus(g, -1) if not isinstance(g, int) or 1 <= g <= ITEMS else None
            c = plus(g, -2) if not isinstance(g, int) or g >= 2 else None
            return a, b, c, (g if isinstance(g, int) else g[1]) % 2

        W1_BANK = [6, 7, 5, 6, 7, 5]

        def heads_of(u):
            return range(u // 2 * 4 + u % 2, u // 2 * 4 + 4, 2) if u < 4 else range(u % 2, HEADS, 2)

        def layer_of(n, layer):
            return n // SEQS if isinstance(n, int) else layer

        def seq_of(n, layer):
            return n % SEQS if isinstance(n, int) else n[0] * 2 + (n[1] - layer * SEQS)

        def shifted(t):
            whole = t[:]
            return bass.AP(tensor=whole.tensor, offset=whole.offset, ap=[list(whole.ap[0]), [T + 1, KC], [1, T]])

        block = ctx.enter_context(nc.Block())

        @block.sync
        def _(sp):
            nonlocal CONSTS
            sp.dma_start(id_f[:], ident).then_inc(const_in, 16)
            sp.dma_start(raw_a[:, 0:KC * INNER].rearrange("p (c n) -> p c n", c=KC),
                         xwq.rearrange("(c p) n -> p c n", p=P)).then_inc(raw_a_in, 16)
            sp.dma_start(raw_a[:, KC * INNER:KC * INNER + IC * D].rearrange("p (c n) -> p c n", c=IC),
                         xwo.rearrange("(c p) n -> p c n", p=P)).then_inc(raw_a_in, 16)

            def load_x(n):
                par = (n if isinstance(n, int) else n[1]) % 2
                sp.dma_start(x_in[:, par], one(x_rows, index(n))).then_inc(x_load[par], 16)
                sp.dma_start(c_in[0:CTX, par, 0:CD],
                             ctx_in[bass.ds(index(n), 1)].rearrange("o s d -> s (o d)")).then_inc(c_load[par], 16)

            sp.wait_ge(zero_made, 1)
            load_x(0)
            load_x(1)
            consts = [
                (xk_w[:], xwk.rearrange("(c p) n -> p c n", p=P)),
                (xv_w[:], xwv.rearrange("(c p) n -> p c n", p=P)),
                (bo_t[:], xbo.partition_broadcast(P)),
                (mask_raw[:], mask.rearrange("p (a n) -> p a n", a=2)),
                (rope_raw[:], rope),
            ]
            for layer in range(LAYERS):
                consts.append((b2_t[:, layer], b2[layer].partition_broadcast(P)))
                consts.append((b1_t[:, layer], b1[layer]))
                consts.append((lng_t[:, layer], lng[layer]))
                consts.append((lnb_t[:, layer], lnb[layer]))
                for j, s in enumerate((qsc, ksc)):
                    consts.append((sc_t[:, layer, 0, j], s[layer].partition_broadcast(P)))
                    for half in range(2):
                        consts.append((sc_t[:, layer, 1, j, half * 32:half * 32 + 32],
                                       s[layer, 32 - half * 32:64 - half * 32].partition_broadcast(P)))
            for dst, src in consts:
                sp.dma_start(dst, src).then_inc(const_in, 16)
            CONSTS = 16 * (len(consts) + 1)

            def load_b(layer):
                sp.dma_start(raw_b[:, 0:IC * D].rearrange("p (c n) -> p c n", c=IC),
                             wo[layer].rearrange("(c p) n -> p c n", p=P)).then_inc(raw_b_in, 16)
                sp.dma_start(raw_b[:, IC * D:(IC + FC) * D].rearrange("p (c n) -> p c n", c=FC),
                             w2[layer].rearrange("(c p) n -> p c n", p=P)).then_inc(raw_b_in, 16)

            def load_qkv(layer):
                sp.dma_start(raw_a[:].rearrange("p (c n) -> p c n", c=KC),
                             wqkv[layer].rearrange("(c p) n -> p c n", p=P)).then_inc(raw_a_in, 16)

            def load_w1(layer):
                sp.dma_start(raw_a[:, 0:KC * W1C * P].rearrange("p (c n) -> p c n", c=KC),
                             w1[layer].rearrange("(c p) n -> p c n", p=P)).then_inc(raw_a_in, 16)

            load_b(0)

            def run_x(g):
                a, b, d, par = x_roles(g)
                if d is not None:
                    sp.wait_ge(x_res1, at(d, 1, 1))
                    sp.dma_start(one(x1_dram, index(d)), x1_x[:]).then_inc(x1_store, 16)
                    sp.wait_ge(y_norm, at(d, 1, 1))
                    sp.dma_start(one(y_dram, index(d)), y_x[:]).then_inc(y_store, 16)
                if not isinstance(g, int) or g < SEQS - 2:
                    sp.wait_ge(x_norm, at(a, 1, 1))
                    sp.wait_ge(x_bias, at(a, 1, 1))
                    sp.wait_ge(c_tr, at(a, 1, 1))
                    load_x(plus(a, 2))
                if isinstance(g, int) and g == 0:
                    sp.wait_ge(w_lo, WEIGHT["xo"])
                    load_qkv(0)
                if isinstance(g, int) and g == SEQS - 1:
                    sp.wait_ge(w_lo, WEIGHT["qkv0"])
                    load_w1(0)
                    load_b(1)

            for g in range(3):
                run_x(g)
            with sp.Fori(1, SEQS // 2 - 2) as i:
                for u in range(2):
                    run_x((i, u + 1))
            for g in range(SEQS - 3, SEQS + 2):
                run_x(g)

            sp.wait_ge(x1_store, 16 * SEQS)
            sp.wait_ge(y_store, 16 * SEQS)
            sp.wait_ge(w_lo, WEIGHT["w10"])
            sp.sem_inc(stage_l, 1)
            sp.dma_start(x_cur[:], one(y_dram, 0)).then_inc(cur_load, 16)
            sp.dma_start(x_res[:], one(y_dram, 0)).then_inc(res_load, 16)
            load_qkv(1)

            def run_l(g, layer=None):
                a, b, c, par = l_roles(g)
                if c is not None:
                    sp.wait_ge(dve_x1, at(c, 1, 1))
                    for t in range(NT):
                        sp.dma_start(x1[1:P, t, 1], x1[0:P - 1, t, 2]).then_inc(shift, 16)
                    sp.dma_start(x1[0:1, 1, 1], x1[P - 1:P, 0, 2]).then_inc(shift, 16)
                    if b is not None:
                        sp.dma_start(x_res[:], one(y_dram, seq_of(b, layer))).then_inc(res_load, 16)
                    if layer_of(c, layer) == LAYERS - 1:
                        sp.dma_start(x_orig[:], one(x1_dram, seq_of(c, layer))).then_inc(orig_load, 16)
                if a is not None and not (isinstance(a, int) and a == ITEMS - 1):
                    sp.wait_ge(pe_xt, at(a, 1, 1))
                    sp.dma_start(x_cur[:], one(y_dram, seq_of(plus(a, 1), layer))).then_inc(cur_load, 16)
                if c is not None:
                    sp.wait_ge(dve_x2, at(c, 1, 1))
                    dst = out_rows if layer_of(c, layer) == LAYERS - 1 else y_dram
                    sp.dma_start(one(dst, seq_of(c, layer)), x2[:, par]).then_inc(x2_store, 16)

            def between(g):
                if g == SEQS:
                    sp.wait_ge(w_lo, WEIGHT["qkv1"])
                    load_w1(1)

            between(0)
            for g in range(4):
                run_l(g)
            with sp.Fori(2, SEQS // 2 - 1) as i:
                for u in range(2):
                    run_l((i, u), 0)
            run_l(SEQS - 2)
            run_l(SEQS - 1)
            between(SEQS)
            run_l(SEQS)
            run_l(SEQS + 1)
            with sp.Fori(SEQS // 2 + 1, SEQS - 1) as i:
                for u in range(2):
                    run_l((i, u), 1)
            for g in range(ITEMS - 2, ITEMS + 2):
                run_l(g)
            sp.wait_ge(x2_store, 16 * ITEMS)

        @block.tensor
        def _(pe):
            def bank(b):
                return pb[:, b]

            def split_product(dst, pairs, done):
                for n, (s_hi, s_lo, m_hi, m_lo) in enumerate(pairs):
                    for k, (s, m) in enumerate(((s_hi, m_hi), (s_hi, m_lo), (s_lo, m_hi))):
                        mm = pe.matmul(dst, s, m, start=(n == 0 and k == 0 and done[0]),
                                       stop=(n == len(pairs) - 1 and k == 2))
                return mm

            pe.wait_ge(const_in, CONSTS)

            def x_turn(a, par):
                pe.wait_ge(x_norm, at(a, 1, 1))
                for c in range(KC):
                    for t in range(NT):
                        mm = pe.transpose(pb[:, 0, c * T + t * P:c * T + t * P + P], xn[:, t, c * P:c * P + P], id_f[:])
                mm.then_inc(x_tr, 1)
                pe.wait_ge(c_load[par], of_parity(a))
                for c in range(2):
                    mm = pe.transpose(pb[:, 1, c * P:c * P + CTX], c_in[0:CTX, par, c * P:c * P + P],
                                      id_f[0:CTX, 0:CTX])
                mm.then_inc(c_tr, 1)

            def x_scores(b, par, u):
                t, odd = u // 2, u % 2
                if u == 0:
                    pe.wait_ge(x_cq, at(b, 2, 2))
                    pe.wait_ge(x_ck, at(b, 1, 1))
                if u >= 2:
                    pe.wait_ge(x_exp, at(b, XUNITS, u - 1))
                for k in range(4):
                    r = odd * DH
                    mm = pe.matmul(pb[:, 2 + u % 2, k * P:k * P + CTX], xq_t[r:r + DH, par, k, t * P:t * P + P],
                                   xk_t[r:r + DH, par, k, :], start=True, stop=True)
                mm.then_inc(x_s, 1)

            def x_probs(b, u):
                pe.wait_ge(x_pn, at(b, XUNITS, u + 1))
                if u >= 2:
                    pe.wait_ge(x_ptc, at(b, XUNITS, u - 1))
                for k in range(4):
                    mm = pe.transpose(pb[0:CTX, u % 2, k * P:k * P + P], x_p[:, u, k, :], id_f[:])
                mm.then_inc(x_ptr, 1)

            def x_values(b, par, u):
                t, odd = u // 2, u % 2
                if u == 0:
                    pe.wait_ge(x_cv, at(b, 1, 1))
                pe.wait_ge(x_ptc, at(b, XUNITS, u + 1))
                for k in range(4):
                    h = 2 * k + odd
                    r, col = odd * DH, (k % 2) * T + t * P
                    mm = pe.matmul(pb[r:r + DH, 6 + k // 2, col:col + P], x_v[0:CTX, par, h * DH:h * DH + DH],
                                   x_pt[0:CTX, u, k, :], start=True, stop=True)
                mm.then_inc(x_av, 1)

            def x_out(a, d):
                pe.wait_ge(x_ohi, at(d, 2, 2))
                pe.wait_ge(x_olo, at(d, 2, 2))
                if a is not None:
                    pe.wait_ge(c_cp, at(a, 1, 1))
                for t in range(NT):
                    rows = slice(t * P, t * P + P)
                    mm = split_product(pb[:, 1, t * D:t * D + D],
                                       [(xo_hi_t[:, c, rows], xo_lo_t[:, c, rows], xo_hi[:, c], xo_lo[:, c])
                                        for c in range(IC)], (True,))
                mm.then_inc(x_wo, 1)

            def x_queries(a):
                pe.wait_ge(x_thi, at(a, 1, 1))
                pe.wait_ge(x_tlo, at(a, 1, 1))
                for c in range(IC):
                    cols = slice(c * P, c * P + P)
                    mm = split_product(pb[:, 4 + c // 2, (c % 2) * T:(c % 2) * T + T],
                                       [(xq_hi[:, k, cols], xq_lo[:, k, cols], xn_hi[:, k], xn_lo[:, k])
                                        for k in range(KC)], (True,))
                    if c % 2:
                        mm.then_inc(x_pq, 1)

            def x_keys_values(a):
                pe.wait_ge(c_cp, at(a, 1, 1))
                for c in range(IC):
                    for k in range(2):
                        mm = pe.matmul(pb[:, 6, c * P:c * P + CTX], xk_w[:, k, c * P:c * P + P], c_t[:, k, :],
                                       start=(k == 0), stop=(k == 1))
                mm.then_inc(x_pk, 1)
                for k in range(2):
                    mm = pe.matmul(pb[0:CTX, 7, :], c_t[:, k, :], xv_w[:, k, :], start=(k == 0), stop=(k == 1))
                mm.then_inc(x_pv, 1)

            def run_x(g):
                a, b, d, par = x_roles(g)
                was = 1 - par
                if isinstance(g, int) and g == 0:
                    x_turn(0, 0)
                    pe.wait_ge(w_lo, WEIGHT["xo"])
                if b is not None:
                    x_scores(b, was, 0)
                    x_scores(b, was, 1)
                if d is not None:
                    x_out(a, d)
                if a is not None:
                    x_queries(a)
                if b is not None:
                    x_scores(b, was, 2)
                    x_scores(b, was, 3)
                    x_probs(b, 0)
                    if d is not None:
                        pe.wait_ge(x_res1, at(d, 1, 1))
                    x_probs(b, 1)
                if a is not None:
                    x_keys_values(a)
                if b is not None:
                    x_probs(b, 2)
                    x_probs(b, 3)
                    if a is not None:
                        pe.wait_ge(x_ck, at(a, 1, 1))
                        pe.wait_ge(x_cv, at(a, 1, 1))
                    for u in range(XUNITS):
                        x_values(b, was, u)
                if a is not None and not (isinstance(a, int) and a == SEQS - 1):
                    x_turn(plus(a, 1), 1 - par)

            x_iterations(pe, run_x)

            pe.wait_ge(stage_l, 1)
            QKV_BANK = {(0, 0): 0, (0, 1): 1, (1, 0): 3, (1, 1): 4, (0, 2): 2, (1, 2): 5}

            def turn_x(n):
                pe.wait_ge(cur_load, at(n, 16, 16))
                for c in range(KC):
                    for t in range(NT):
                        mm = pe.transpose(pb[:, 4, c * T + t * P:c * T + t * P + P], x_cur[:, t, c * P:c * P + P], id_f[:])
                mm.then_inc(pe_xt, 1)

            def project(a, t, part):
                b = QKV_BANK[t, part]
                if part < 2 and b < 4 and later(a):
                    pe.wait_ge(act_qkt, at(plus(a, -1), 4, b + 1))
                if part == 2 and b == 2 and later(a):
                    pe.wait_ge(act_qkt, at(plus(a, -1), 4, 3))
                cols = slice(part * INNER, part * INNER + INNER)
                mm = split_product(bank(b), [(xt_hi[:, c * T + t * P:c * T + t * P + P],
                                              xt_lo[:, c * T + t * P:c * T + t * P + P],
                                              wqkv_hi[:, c, cols], wqkv_lo[:, c, cols]) for c in range(KC)], (True,))
                mm.then_inc(pe_qkv, 1)

            def turn_h(c):
                pe.wait_ge(dve_h, at(c, 1, 1))
                for k in range(KC):
                    for t in range(NT):
                        mm = pe.transpose(pb[:, 7, k * T + t * P:k * T + t * P + P], h_n[:, t, k * P:k * P + P], id_f[:])
                mm.then_inc(pe_ht, 1)

            def hidden(a, c, m):
                if m == 0:
                    pe.wait_ge(dve_hhi, at(c, 1, 1))
                    pe.wait_ge(dve_hlo, at(c, 1, 1))
                if m == 2 and a is not None:
                    pe.wait_ge(act_v, at(a, NT, NT))
                if m >= 3:
                    pe.wait_ge(dve_hg, at(c, FC, m - 2))
                for part in range(2 if m < FC - 1 else 1):
                    n = 2 * m + part
                    mm = split_product(pb[:, W1_BANK[m], part * T:part * T + T],
                                       [(w1_hi[:, k, n], w1_lo[:, k, n], h_hi[:, k], h_lo[:, k]) for k in range(KC)],
                                       (True,))
                mm.then_inc(pe_w1, 1)

            def scores(a, b, c, u):
                if u == 0:
                    pe.wait_ge(act_qkt, at(b, 4, 4))
                    if a is not None:
                        pe.wait_ge(dve_rope, at(a, NT, 1))
                if u == 2 and a is not None:
                    pe.wait_ge(act_v, at(a, NT, 1))
                if u >= 3:
                    pe.wait_ge(act_exp, at(b, UNITS, u - 2))
                win1 = u < 4
                pe.matmul(bank(u % 3), id_b[:], mask_b[:, 0 if win1 else 1], start=True, stop=False, skip_group_check=True)
                keys = T if win1 else P
                for k, h in enumerate(heads_of(u)):
                    ch, r = h // 2, (h % 2) * DH
                    q_cols = slice(P, T) if win1 else slice(0, P)
                    mm = pe.matmul(pb[:, u % 3, k * keys:k * keys + keys], qk_t[r:r + DH, 0, ch, q_cols],
                                   qk_t[r:r + DH, 1, ch, 0:keys], start=False, stop=True, skip_group_check=True)
                mm.then_inc(pe_s, 1)

            def turn_p(a, b, u):
                pe.wait_ge(dve_pn, at(b, UNITS, u + 1))
                if u == 0 and a is not None:
                    pe.wait_ge(dve_rope, at(a, NT, 2))
                if u >= 2:
                    pe.wait_ge(act_pt, at(b, UNITS, u - 1))
                for k in range(4):
                    mm = pe.transpose(pb[:, 3 + u % 2, k * P:k * P + P], p_t[:, u % 3, k * P:k * P + P], id_f[:])
                mm.then_inc(pe_pt, 1)

            def weigh(a, b, c, par, u):
                pe.wait_ge(act_pt, at(b, UNITS, u + 1))
                if u == 0:
                    pe.wait_ge(act_v, at(b, NT, NT))
                    if c is not None:
                        pe.wait_ge(dve_hg, at(c, FC, FC))
                    elif a is not None:
                        pe.wait_ge(act_v, at(a, NT, NT))
                if u < 4:
                    for k, h in enumerate(heads_of(u)):
                        r, col = (h % 2) * DH, (h // 2 % 2) * T + P
                        for t in range(NT):
                            mm = pe.matmul(pb[r:r + DH, 5 + h // 4, col:col + P],
                                           v_t[:, par, t, h * DH:h * DH + DH],
                                           pt_t[:, u % 2, (2 * k + t) * P:(2 * k + t) * P + P],
                                           start=(t == 0), stop=(t == NT - 1))
                else:
                    for k, h in enumerate(heads_of(u)):
                        r, col = (h % 2) * DH, (h // 2 % 2) * T
                        mm = pe.matmul(pb[r:r + DH, 5 + h // 4, col:col + P], v_t[:, par, 0, h * DH:h * DH + DH],
                                       pt_t[:, u % 2, k * P:k * P + P], start=True, stop=True)
                mm.then_inc(pe_av, 1)

            def feed(c, n):
                t, k = n // FC, n % FC
                if n == 0:
                    pe.wait_ge(dve_hg, at(c, FC, FC))
                if t == 0:
                    pe.wait_ge(dve_hghi, at(c, FC, k + 1))
                    pe.wait_ge(pool_hglo, at(c, FC, k + 1))
                rows = slice(t * P, t * P + P)
                for j, (s, m) in enumerate(((hg_hi, w2_hi), (hg_hi, w2_lo), (hg_lo, w2_hi))):
                    mm = pe.matmul(pb[:, 7, t * D:t * D + D], s[:, k, rows], m[:, k],
                                   start=(k == 0 and j == 0), stop=(k == FC - 1 and j == 2))
                if n == NT * FC - 1:
                    mm.then_inc(pe_w2, 1)

            def run_l(g, layer=None):
                a, b, c, par = l_roles(g)
                if a is not None:
                    pe.wait_ge(act_xhi, at(a, 1, 1))
                    pe.wait_ge(dve_xlo, at(a, 1, 1))
                    for t in range(NT):
                        for part in range(2):
                            project(a, t, part)
                    for t in range(NT):
                        project(a, t, 2)
                if c is not None:
                    turn_h(c)
                if b is not None:
                    for u in range(3):
                        scores(a, b, c, u)
                if c is not None:
                    for m in range(FC):
                        hidden(a, c, m)
                for j in range(UNITS + 2):
                    if b is not None:
                        if j < 3:
                            scores(a, b, c, j + 3)
                        if j < UNITS:
                            turn_p(a, b, j)
                    if c is not None and 2 <= j:
                        feed(c, 2 * j - 4)
                        feed(c, 2 * j - 3)
                    if b is not None and j >= 2:
                        weigh(a, b, c, 1 - par, j - 2)
                if a is not None:
                    for k in range(4):
                        if k == 0:
                            pe.wait_ge(pool_qk, at(a, NT, NT))
                        if k == 2 and b is None:
                            pe.wait_ge(act_v, at(a, NT, 1))
                        for j in range(2):
                            for t in range(NT):
                                col = (2 * k + j) * P
                                mm = pe.transpose(pb[:, k, j * T + t * P:j * T + t * P + P],
                                                  r_cos[:, t, col:col + P], id_f[:])
                        mm.then_inc(pe_qkt, 1)
                    if not (isinstance(a, int) and a == ITEMS - 1):
                        turn_x(plus(a, 1))
                if b is not None:
                    pe.wait_ge(act_ohi, at(b, 2, 2))
                    pe.wait_ge(dve_olo, at(b, 2, 2))
                    if isinstance(b, int) and b == SEQS:
                        pe.wait_ge(w_lo, WEIGHT["wo1"])
                    if c is not None:
                        pe.wait_ge(dve_x2, at(c, 1, 1))
                    for t in range(NT):
                        rows = slice(t * P, t * P + P)
                        mm = split_product(pb[:, 7, t * D:t * D + D],
                                           [(o_hi[:, k, rows], o_lo[:, k, rows], wo_hi[:, k], wo_lo[:, k])
                                            for k in range(IC)], (True,))
                    mm.then_inc(pe_wo, 1)

            def between(g):
                if g == 0:
                    turn_x(0)
                    pe.wait_ge(w_lo, WEIGHT["w10"])
                elif g == SEQS:
                    pe.wait_ge(w_lo, WEIGHT["qkv1"])
                elif g == SEQS + 2:
                    pe.wait_ge(w_lo, WEIGHT["w11"])

            l_iterations(pe, run_l, between)

        @block.scalar
        def _(act):
            def split_hi(name, src, dst):
                nc.scalar.activation(dst, src, ACT.Copy).then_inc(w_hi, 1)

            act.wait_ge(raw_a_in, 32)
            split_hi("xq", raw_a[:, 0:KC * INNER].rearrange("p (c n) -> p c n", c=KC), xq_hi[:])
            split_hi("xo", raw_a[:, KC * INNER:KC * INNER + IC * D].rearrange("p (c n) -> p c n", c=IC), xo_hi[:])

            def x_turned(a):
                act.wait_ge(x_tr, at(a, 1, 1))
                nc.scalar.activation(xn_hi[:].rearrange("p c t -> p (c t)"), pb[:, 0], ACT.Copy).then_inc(x_thi, 1)
                act.wait_ge(c_tr, at(a, 1, 1))
                nc.scalar.activation(c_t[:], pb[:, 1, 0:2 * P].rearrange("p (c n) -> p c n", c=2)[:, :, 0:CTX],
                                     ACT.Copy).then_inc(c_cp, 1)

            def x_exps(b, u):
                act.wait_ge(x_max, at(b, XUNITS, u + 1))
                if later(b):
                    act.wait_ge(x_ptr, at(plus(b, -1), XUNITS, u + 1))
                for k in range(4):
                    e = nc.scalar.activation(x_p[:, u, k, :], pb[:, 2 + u % 2, k * P:k * P + CTX], ACT.Exp,
                                             bias=x_nm[:, u, k:k + 1], scale=1.0, accum_out=x_sum[:, u, k:k + 1])
                e.then_inc(x_exp, 1)

            def x_probs_copy(b, u):
                act.wait_ge(x_ptr, at(b, XUNITS, u + 1))
                nc.scalar.activation(x_pt[0:CTX, u].rearrange("p k n -> p (k n)"), pb[0:CTX, u % 2],
                                     ACT.Copy).then_inc(x_ptc, 1)

            def run_x(g):
                a, b, d, par = x_roles(g)
                if isinstance(g, int) and g == 0:
                    x_turned(0)
                if b is not None:
                    x_exps(b, 0)
                    x_exps(b, 1)
                if a is not None:
                    for k in range(2):
                        act.wait_ge(x_pq, at(a, 2, k + 1))
                        nc.scalar.activation(xq_t[:, par, 2 * k:2 * k + 2].rearrange("p c t -> p (c t)"), pb[:, 4 + k],
                                             ACT.Copy, scale=DH ** -0.5).then_inc(x_cq, 1)
                if b is not None:
                    x_exps(b, 2)
                    x_probs_copy(b, 0)
                    x_exps(b, 3)
                    x_probs_copy(b, 1)
                if a is not None:
                    act.wait_ge(x_pk, at(a, 1, 1))
                    nc.scalar.activation(xk_t[:, par], pb[:, 6].rearrange("p (c n) -> p c n", c=IC)[:, :, 0:CTX],
                                         ACT.Copy).then_inc(x_ck, 1)
                    act.wait_ge(x_pv, at(a, 1, 1))
                    nc.scalar.activation(x_v[0:CTX, par], pb[0:CTX, 7], ACT.Copy).then_inc(x_cv, 1)
                if b is not None:
                    x_probs_copy(b, 2)
                    x_probs_copy(b, 3)
                    act.wait_ge(x_av, at(b, XUNITS, XUNITS))
                    for k in range(2):
                        nc.scalar.activation(xo_hi_t[:, 2 * k:2 * k + 2].rearrange("p c t -> p (c t)"), pb[:, 6 + k],
                                             ACT.Copy).then_inc(x_ohi, 1)
                if a is not None and not (isinstance(a, int) and a == SEQS - 1):
                    x_turned(plus(a, 1))
                if isinstance(g, int) and g == 0:
                    act.wait_ge(raw_b_in, 32)
                    split_hi("wo0", raw_b[:, 0:IC * D].rearrange("p (c n) -> p c n", c=IC), wo_hi[:])
                    split_hi("w20", raw_b[:, IC * D:].rearrange("p (c n) -> p c n", c=FC), w2_hi[:])
                if isinstance(g, int) and g == SEQS - 1:
                    act.wait_ge(raw_a_in, 48)
                    split_hi("qkv0", raw_a[:].rearrange("p (c n) -> p c n", c=KC), wqkv_hi[:])
                if isinstance(g, int) and g == SEQS + 1:
                    act.wait_ge(raw_a_in, 64)
                    split_hi("w10", raw_a[:, 0:KC * W1C * P].rearrange("p (c m n) -> p c m n", c=KC, n=P), w1_hi[:])

            x_iterations(act, run_x)

            act.wait_ge(stage_l, 1)
            act.wait_ge(zero_made, 2)

            def x_hi(n):
                act.wait_ge(pe_xt, at(n, 1, 1))
                dst = shifted(xt_hi)
                nc.scalar.activation(dst, pb[:, 4].rearrange("p (c t) -> p c t", c=KC), ACT.Copy).then_inc(act_xhi, 1)

            def exps(b, j):
                heads = 2 if j < 4 else 4
                keys = 512 // heads
                act.wait_ge(dve_max, at(b, UNITS, j + 1))
                if j >= 3 or later(b):
                    act.wait_ge(pe_pt, at(b, UNITS, j - 2))
                for k in range(heads):
                    e = nc.scalar.activation(p_t[:, j % 3, k * keys:k * keys + keys], pb[:, j % 3, k * keys:k * keys + keys],
                                             ACT.Exp, bias=s_nm[:, j, k:k + 1], scale=1.0, accum_out=s_sum[:, j, k:k + 1])
                e.then_inc(act_exp, 1)

            def run_l(g, layer=None):
                a, b, c, par = l_roles(g)
                if a is not None:
                    for t in range(NT):
                        act.wait_ge(pe_qkv, at(a, 6, 2 * t + 2))
                        if later(a):
                            act.wait_ge(pool_qk, at(plus(a, -1), NT, t + 1))
                        nc.scalar.activation(r_sin[:, t].rearrange("p (j n) -> p j n", j=2), pb[:, 3 * t:3 * t + 2],
                                             ACT.Square).then_inc(act_sq, 1)
                if a is not None:
                    for t in range(NT):
                        act.wait_ge(pe_qkv, at(a, 6, 5 + t))
                        nc.scalar.activation(v_t[:, par, t], pb[:, 2 + 3 * t], ACT.Copy).then_inc(act_v, 1)
                if c is not None:
                    act.wait_ge(pe_ht, at(c, 1, 1))
                    ly = layer_of(c, layer)
                    for k in range(KC):
                        nc.scalar.activation(h_f[:, k], pb[:, 7, k * T:k * T + T], ACT.Identity,
                                             bias=lnb_t[:, ly, k:k + 1], scale=lng_t[:, ly, k:k + 1]).then_inc(act_h, 1)
                if b is not None:
                    for u in range(3):
                        exps(b, u)
                if c is not None:
                    ly = layer_of(c, layer)
                    for m in range(FC):
                        act.wait_ge(pe_w1, at(c, FC, m + 1))
                        if m >= 2 or later(c):
                            act.wait_ge(dve_hg, at(c, FC, m - 1))
                        w = W1_BANK[m]
                        if m < FC - 1:
                            e = nc.scalar.activation(gl[:, m % 2], pb[:, w, T:2 * T], ACT.Gelu,
                                                     bias=b1_t[:, ly, 1, m:m + 1])
                        else:
                            e = nc.scalar.activation(gl[0:TAIL, m % 2], pb[TAIL_G:TAIL_G + TAIL, w, 0:T], ACT.Gelu,
                                                     bias=b1_t[TAIL_G:TAIL_G + TAIL, ly, 1, m:m + 1])
                        e.then_inc(act_gelu, 1)
                if b is not None:
                    for j in range(UNITS):
                        if j < 3:
                            exps(b, j + 3)
                        act.wait_ge(pe_pt, at(b, UNITS, j + 1))
                        if j >= 2 or later(b):
                            act.wait_ge(pe_av, at(b, UNITS, j - 1))
                        nc.scalar.activation(pt_t[:, j % 2], pb[:, 3 + j % 2], ACT.Copy).then_inc(act_pt, 1)
                    act.wait_ge(pe_av, at(b, UNITS, UNITS))
                    for k in range(2):
                        nc.scalar.activation(o_hi[:, 2 * k:2 * k + 2].rearrange("p c t -> p (c t)"), pb[:, 5 + k],
                                             ACT.Copy).then_inc(act_ohi, 1)
                if a is not None:
                    for k in range(4):
                        act.wait_ge(pe_qkt, at(a, 4, k + 1))
                        nc.scalar.activation(qk_t[:, k // 2, 2 * (k % 2):2 * (k % 2) + 2].rearrange("p c t -> p (c t)"),
                                             pb[:, k], ACT.Copy).then_inc(act_qkt, 1)
                    if not (isinstance(a, int) and a == ITEMS - 1):
                        x_hi(plus(a, 1))

            def between(g):
                if g == 0:
                    x_hi(0)
                elif g == SEQS:
                    act.wait_ge(raw_a_in, 80)
                    act.wait_ge(pe_qkv, 6 * SEQS)
                    split_hi("qkv1", raw_a[:].rearrange("p (c n) -> p c n", c=KC), wqkv_hi[:])
                elif g == SEQS + 1:
                    act.wait_ge(raw_b_in, 64)
                    act.wait_ge(pe_wo, SEQS)
                    split_hi("wo1", raw_b[:, 0:IC * D].rearrange("p (c n) -> p c n", c=IC), wo_hi[:])
                elif g == SEQS + 2:
                    act.wait_ge(pe_w2, SEQS)
                    split_hi("w21", raw_b[:, IC * D:].rearrange("p (c n) -> p c n", c=FC), w2_hi[:])
                    act.wait_ge(raw_a_in, 96)
                    act.wait_ge(pe_w1, FC * SEQS)
                    split_hi("w11", raw_a[:, 0:KC * W1C * P].rearrange("p (c m n) -> p c m n", c=KC, n=P), w1_hi[:])

            l_iterations(act, run_l, between)

        @block.vector
        def _(dve):
            def split_lo(name, src, hi, lo):
                dve.wait_ge(w_hi, WEIGHT[name])
                nc.vector.tensor_tensor(lo, src, hi.bitcast(F32), ALU.subtract).then_inc(w_lo, 1)

            def aggregate(mean_var, stats, s_stats, s_out, n):
                dve.wait_ge(s_stats, at(n, 1, 1))
                dve.sem_inc(stats_seen, 1)
                for t in range(NT):
                    e = nc.vector.bn_aggr(mean_var[:, t], stats[:, t])
                e.then_inc(s_out, 1)

            def x_stats(a, par):
                dve.wait_ge(x_load[par], of_parity(a))
                for t in range(NT):
                    e = nc.vector.bn_stats(x_st[:, 0, t], x_in[:, par, t])
                e.then_inc(x_bst, 1)
                aggregate(x_mv[:, 0], x_st[:, 0], x_bst, x_bmv, a)

            def x_normed(a, par):
                dve.wait_ge(x_rst, at(a, 1, 1))
                dve.wait_ge(x_bmv, at(a, 1, 1))
                if later(a):
                    dve.wait_ge(x_tr, at(plus(a, -1), 1, 1))
                for t in range(NT):
                    e = nc.vector.tensor_scalar(xn[:, t], x_in[:, par, t], x_mv[:, 0, t, 0:1], x_rs[:, 0, t:t + 1],
                                                ALU.subtract, ALU.mult)
                e.then_inc(x_norm, 1)

            def x_turned_lo(a):
                dve.wait_ge(x_thi, at(a, 1, 1))
                nc.vector.tensor_tensor(xn_lo[:].rearrange("p c t -> p (c t)"), pb[:, 0],
                                        xn_hi[:].rearrange("p c t -> p (c t)").bitcast(F32),
                                        ALU.subtract).then_inc(x_tlo, 1)

            def x_maxes(b, u):
                dve.wait_ge(x_s, at(b, XUNITS, u + 1))
                nc.vector.tensor_reduce(x_nm[:, u], pb[:, 2 + u % 2].rearrange("p (k n) -> p k n", k=4)[:, :, 0:CTX],
                                        AX.X, ALU.max, negate=True).then_inc(x_max, 1)

            def x_norm_probs(b, u):
                dve.wait_ge(x_exp, at(b, XUNITS, u + 1))
                nc.vector.reciprocal(x_inv[:, u], x_sum[:, u]).then_inc(x_rec, 1)
                dve.wait_ge(x_rec, at(b, XUNITS, u + 1))
                nc.vector.tensor_tensor(x_p[:, u], x_p[:, u], x_inv[:, u].unsqueeze(2).broadcast_to([P, 4, CTX]),
                                        ALU.mult).then_inc(x_pn, 1)

            dve.wait_ge(zero_made, 1)
            split_lo("xq", raw_a[:, 0:KC * INNER].rearrange("p (c n) -> p c n", c=KC), xq_hi[:], xq_lo[:])
            split_lo("xo", raw_a[:, KC * INNER:KC * INNER + IC * D].rearrange("p (c n) -> p c n", c=IC), xo_hi[:], xo_lo[:])

            def run_x(g):
                a, b, d, par = x_roles(g)
                ahead = a is not None and not (isinstance(a, int) and a == SEQS - 1)
                if isinstance(g, int) and g == 0:
                    x_stats(0, 0)
                    x_normed(0, 0)
                    x_turned_lo(0)
                if b is not None:
                    x_maxes(b, 0)
                    x_maxes(b, 1)
                    x_norm_probs(b, 0)
                    x_norm_probs(b, 1)
                if d is not None:
                    dve.wait_ge(x_wo, at(d, 1, 1))
                    dve.wait_ge(x_bias, at(d, 1, 1))
                    if later(d):
                        dve.wait_ge(x1_store, at(plus(d, -1), 16, 16))
                    nc.vector.tensor_tensor(x1_x[:].rearrange("p t d -> p (t d)"), pb[:, 1],
                                            x_b[:, par].rearrange("p t d -> p (t d)"), ALU.add).then_inc(x_res1, 1)
                    dve.wait_ge(x_res1, at(d, 1, 1))
                    for t in range(NT):
                        e = nc.vector.bn_stats(x_st[:, 1, t], x1_x[:, t])
                    e.then_inc(y_bst, 1)
                    aggregate(x_mv[:, 1], x_st[:, 1], y_bst, y_bmv, d)
                if ahead:
                    x_stats(plus(a, 1), 1 - par)
                if b is not None:
                    x_maxes(b, 2)
                    x_maxes(b, 3)
                if d is not None:
                    dve.wait_ge(y_rst, at(d, 1, 1))
                    dve.wait_ge(y_bmv, at(d, 1, 1))
                    if later(d):
                        dve.wait_ge(y_store, at(plus(d, -1), 16, 16))
                    for t in range(NT):
                        e = nc.vector.tensor_scalar(y_x[:, t], x1_x[:, t], x_mv[:, 1, t, 0:1], x_rs[:, 1, t:t + 1],
                                                    ALU.subtract, ALU.mult)
                    e.then_inc(y_norm, 1)
                if b is not None:
                    x_norm_probs(b, 2)
                if ahead:
                    x_normed(plus(a, 1), 1 - par)
                if b is not None:
                    x_norm_probs(b, 3)
                    for k in range(2):
                        dve.wait_ge(x_ohi, at(b, 2, k + 1))
                        hi = xo_hi_t[:, 2 * k:2 * k + 2].rearrange("p c t -> p (c t)")
                        nc.vector.tensor_tensor(xo_lo_t[:, 2 * k:2 * k + 2].rearrange("p c t -> p (c t)"), pb[:, 6 + k],
                                                hi.bitcast(F32), ALU.subtract).then_inc(x_olo, 1)
                if ahead:
                    x_turned_lo(plus(a, 1))
                if isinstance(g, int) and g == 0:
                    dve.wait_ge(const_in, CONSTS)
                    nc.vector.tensor_copy(id_b[:], id_f[:]).then_inc(const_made, 1)
                    nc.vector.tensor_copy(mask_b[:], mask_raw[:]).then_inc(const_made, 1)
                    for layer in range(LAYERS):
                        for j, tab in enumerate((cos_t, sin_t)):
                            nc.vector.tensor_tensor(
                                tab[:, layer].rearrange("p t j d -> p t (j d)"),
                                rope_raw[:, j].rearrange("p t j d -> p t (j d)"),
                                sc_t[:, layer, j].rearrange("p j d -> p (j d)").unsqueeze(1).broadcast_to([P, NT, 2 * DH]),
                                ALU.mult).then_inc(const_made, 1)
                    split_lo("wo0", raw_b[:, 0:IC * D].rearrange("p (c n) -> p c n", c=IC), wo_hi[:], wo_lo[:])
                    split_lo("w20", raw_b[:, IC * D:].rearrange("p (c n) -> p c n", c=FC), w2_hi[:], w2_lo[:])
                if isinstance(g, int) and g == SEQS - 1:
                    split_lo("qkv0", raw_a[:].rearrange("p (c n) -> p c n", c=KC), wqkv_hi[:], wqkv_lo[:])
                if isinstance(g, int) and g == SEQS + 1:
                    split_lo("w10", raw_a[:, 0:KC * W1C * P].rearrange("p (c m n) -> p c (m n)", c=KC, n=P),
                             w1_hi[:].rearrange("p c m n -> p c (m n)"), w1_lo[:].rearrange("p c m n -> p c (m n)"))

            x_iterations(dve, run_x)

            dve.wait_ge(stage_l, 1)
            dve.wait_ge(zero_made, 2)

            def x_lo(n):
                dve.wait_ge(act_xhi, at(n, 1, 1))
                nc.vector.tensor_tensor(shifted(xt_lo), pb[:, 4].rearrange("p (c t) -> p c t", c=KC),
                                        shifted(xt_hi).bitcast(F32), ALU.subtract).then_inc(dve_xlo, 1)

            def residual(c):
                dve.wait_ge(pe_wo, at(c, 1, 1))
                dve.wait_ge(res_load, at(c, 16, 16))
                if later(c):
                    dve.wait_ge(pool_x1b, at(plus(c, -1), 1, 1))
                nc.vector.tensor_tensor(x1[:, :, 0:3:2], pb[:, 7].rearrange("p (t c n) -> p t c n", t=NT, c=KC),
                                        x_res[:].rearrange("p t (c n) -> p t c n", c=KC), ALU.add).then_inc(dve_x1, 1)

            def stats_h(c):
                dve.wait_ge(shift, at(c, 48, 48))
                for t in range(NT):
                    e = nc.vector.bn_stats(l_st[:, t], x1[:, t, 0:2].rearrange("p c n -> p (c n)"))
                e.then_inc(dve_bst, 1)
                aggregate(l_mv, l_st, dve_bst, dve_bmv, c)

            def norm_h(c):
                dve.wait_ge(pool_rst, at(c, 1, 1))
                dve.wait_ge(dve_bmv, at(c, 1, 1))
                for t in range(NT):
                    e = nc.vector.tensor_scalar(h_n[:, t], x1[:, t, 0:2].rearrange("p c n -> p (c n)"), l_mv[:, t, 0:1],
                                                l_rs[:, t:t + 1], ALU.subtract, ALU.mult)
                e.then_inc(dve_h, 1)

            def split_h(c):
                dve.wait_ge(act_h, at(c, KC, KC))
                flat = lambda t: t[:].rearrange("p c t -> p (c t)")
                nc.vector.tensor_copy(flat(h_hi), flat(h_f)).then_inc(dve_hhi, 1)
                dve.wait_ge(dve_hhi, at(c, 1, 1))
                nc.vector.tensor_tensor(flat(h_lo), flat(h_f), flat(h_hi).bitcast(F32), ALU.subtract).then_inc(dve_hlo, 1)

            def squares(a, t):
                dve.wait_ge(act_sq, at(a, NT, t + 1))
                nc.vector.tensor_reduce(n_sq[:, t], r_sin[:, t].rearrange("p (h d) -> p h d", d=DH), AX.X,
                                        ALU.add).then_inc(dve_ss, 1)

            def rotate_cos(a, t, layer):
                ly = layer_of(a, layer)
                nc.vector.tensor_tensor(
                    r_cos[:, t].rearrange("p (j h d) -> p j h d", j=2, d=DH),
                    pb[:, 3 * t:3 * t + 2].rearrange("p j (h d) -> p j h d", d=DH),
                    cos_t[:, ly, t].unsqueeze(2).broadcast_to([P, 2, HEADS, DH]), ALU.mult)

            def rotate_sin(a, t, layer):
                ly = layer_of(a, layer)
                dve.wait_ge(dve_ss, at(a, NT, t + 1))
                nc.vector.tensor_scalar(n_cl[:, t], n_sq[:, t], NORM_MIN_SQ, None, ALU.max).then_inc(dve_cl, 1)
                half = DH // 2
                qk = pb[:, 3 * t:3 * t + 2].rearrange("p j (h d) -> p j h d", d=DH)
                for s in range(2):
                    o = r_sin[:, t].rearrange("p (j h d) -> p j h d", j=2, d=DH)[:, :, :, s * half:s * half + half]
                    i = qk[:, :, :, half - s * half:DH - s * half]
                    w = sin_t[:, ly, t, :, s * half:s * half + half].unsqueeze(2).broadcast_to([P, 2, HEADS, half])
                    e = nc.vector.tensor_tensor(o, i, w, ALU.mult)
                e.then_inc(dve_rope, 1)

            def maxes(b, j):
                heads = 2 if j < 4 else 4
                dve.wait_ge(pe_s, at(b, UNITS, j + 1))
                nc.vector.tensor_reduce(s_nm[:, j, 0:heads], pb[:, j % 3].rearrange("p (k n) -> p k n", k=heads),
                                        AX.X, ALU.max, negate=True).then_inc(dve_max, 1)

            def norm_probs(b, u):
                heads = 2 if u < 4 else 4
                dve.wait_ge(act_exp, at(b, UNITS, u + 1))
                nc.vector.reciprocal(s_inv[:, u, 0:heads], s_sum[:, u, 0:heads]).then_inc(dve_rec, 1)
                dve.wait_ge(dve_rec, at(b, UNITS, u + 1))
                pu = p_t[:, u % 3].rearrange("p (k n) -> p k n", k=heads)
                nc.vector.tensor_tensor(pu, pu, s_inv[:, u, 0:heads].unsqueeze(2).broadcast_to(
                    [P, heads, 512 // heads]), ALU.mult).then_inc(dve_pn, 1)

            def gate(c, m, layer):
                ly = layer_of(c, layer)
                rows = P if m < FC - 1 else TAIL
                dve.wait_ge(act_gelu, at(c, FC, m + 1))
                if m == 0 and later(c):
                    dve.wait_ge(pool_hglo, at(plus(c, -1), FC, FC))
                nc.vector.scalar_tensor_tensor(out=hg[0:rows, m], in0=pb[0:rows, W1_BANK[m], 0:T],
                                               scalar=b1_t[0:rows, ly, 0, m:m + 1], in1=gl[0:rows, m % 2],
                                               op0=ALU.add, op1=ALU.mult).then_inc(dve_hg, 1)

            def gate_hi(c, m):
                rows = P if m < FC - 1 else TAIL
                dve.wait_ge(dve_hg, at(c, FC, m + 1))
                nc.vector.tensor_copy(hg_hi[0:rows, m], hg[0:rows, m]).then_inc(dve_hghi, 1)

            def run_l(g, layer=None):
                a, b, c, par = l_roles(g)
                if c is not None:
                    residual(c)
                if a is not None:
                    squares(a, 0)
                if c is not None:
                    stats_h(c)
                if a is not None:
                    rotate_cos(a, 0, layer)
                if c is not None:
                    norm_h(c)
                if a is not None:
                    rotate_sin(a, 0, layer)
                    squares(a, 1)
                if b is not None:
                    maxes(b, 0)
                if c is not None:
                    split_h(c)
                if b is not None:
                    maxes(b, 1)
                    maxes(b, 2)
                if a is not None:
                    rotate_cos(a, 1, layer)
                    rotate_sin(a, 1, layer)
                for m in range(FC + 1):
                    if b is not None and m < 3:
                        norm_probs(b, m)
                    if c is not None and m < FC:
                        gate(c, m, layer)
                    if c is not None and m >= 1:
                        gate_hi(c, m - 1)
                if b is not None:
                    for j in range(3, UNITS + 1):
                        if j < UNITS:
                            maxes(b, j)
                        if j >= 4:
                            norm_probs(b, j - 1)
                if c is not None:
                    dve.wait_ge(pe_w2, at(c, 1, 1))
                    if layer_of(c, layer) == LAYERS - 1:
                        dve.wait_ge(pool_x1o, at(plus(c, -SEQS), 1, 1))
                    else:
                        dve.wait_ge(pool_x1b, at(c, 1, 1))
                    if not isinstance(c, int) or c >= 2:
                        dve.wait_ge(x2_store, at(plus(c, -2), 16, 16))
                    nc.vector.tensor_tensor(x2[:, par].rearrange("p t d -> p (t d)"), pb[:, 7],
                                            x1b[:].rearrange("p t d -> p (t d)"), ALU.add).then_inc(dve_x2, 1)
                if b is not None:
                    for k in range(2):
                        dve.wait_ge(act_ohi, at(b, 2, k + 1))
                        hi = o_hi[:, 2 * k:2 * k + 2].rearrange("p c t -> p (c t)")
                        nc.vector.tensor_tensor(o_lo[:, 2 * k:2 * k + 2].rearrange("p c t -> p (c t)"), pb[:, 5 + k],
                                                hi.bitcast(F32), ALU.subtract).then_inc(dve_olo, 1)
                if a is not None and not (isinstance(a, int) and a == ITEMS - 1):
                    x_lo(plus(a, 1))

            def between(g):
                if g == 0:
                    dve.wait_ge(const_made, 2 + 2 * LAYERS)
                    x_lo(0)
                elif g == SEQS:
                    split_lo("qkv1", raw_a[:].rearrange("p (c n) -> p c n", c=KC), wqkv_hi[:], wqkv_lo[:])
                elif g == SEQS + 1:
                    split_lo("wo1", raw_b[:, 0:IC * D].rearrange("p (c n) -> p c n", c=IC), wo_hi[:], wo_lo[:])
                elif g == SEQS + 2:
                    split_lo("w21", raw_b[:, IC * D:].rearrange("p (c n) -> p c n", c=FC), w2_hi[:], w2_lo[:])
                    split_lo("w11", raw_a[:, 0:KC * W1C * P].rearrange("p (c m n) -> p c (m n)", c=KC, n=P),
                             w1_hi[:].rearrange("p c m n -> p c (m n)"), w1_lo[:].rearrange("p c m n -> p c (m n)"))

            l_iterations(dve, run_l, between)

        @block.gpsimd
        def _(pool):
            nc.gpsimd.memset(half_neg[:], -0.5)
            nc.gpsimd.memset(eps_t[:], EPS)
            nc.gpsimd.memset(c_in[:], 0.0).then_inc(zero_made, 1)

            def deviation(var, eps_out, out, n, s_in, s_in_v, s_eps, s_out):
                pool.wait_ge(s_in, s_in_v)
                nc.gpsimd.tensor_tensor(eps_out, var, eps_t[:], ALU.add).then_inc(s_eps, 1)
                pool.wait_ge(s_eps, at(n, 1, 1))
                nc.gpsimd.tensor_tensor(out, eps_out, half_neg[:, 0:NT], ALU.pow).then_inc(s_out, 1)

            def x_bias_rows(a, par):
                pool.wait_ge(x_load[par], of_parity(a))
                nc.gpsimd.tensor_tensor(x_b[:, par], x_in[:, par], bo_t[:].unsqueeze(1).broadcast_to([P, NT, D]),
                                        ALU.add).then_inc(x_bias, 1)

            def run_x(g):
                a, b, d, par = x_roles(g)
                ahead = a is not None and not (isinstance(a, int) and a == SEQS - 1)
                if isinstance(g, int) and g == 0:
                    deviation(x_mv[:, 0, :, 1], x_ve[:, 0], x_rs[:, 0], 0, x_bmv, 1, x_eps, x_rst)
                    pool.wait_ge(const_in, CONSTS)
                    x_bias_rows(0, 0)
                    x_bias_rows(1, 1)
                if d is not None:
                    deviation(x_mv[:, 1, :, 1], x_ve[:, 1], x_rs[:, 1], d, y_bmv, at(d, 1, 1), y_eps, y_rst)
                if ahead:
                    n = plus(a, 1)
                    deviation(x_mv[:, 0, :, 1], x_ve[:, 0], x_rs[:, 0], n, x_bmv, at(n, 1, 1), x_eps, x_rst)
                if d is not None and not (isinstance(d, int) and d >= SEQS - 2):
                    x_bias_rows(plus(d, 2), par)

            x_iterations(pool, run_x)

            pool.wait_ge(stage_l, 1)
            nc.gpsimd.memset(xt_hi[:, T:T + 1].bitcast(F32), 0.0)
            nc.gpsimd.memset(xt_lo[:, T:T + 1].bitcast(F32), 0.0)
            nc.gpsimd.memset(x1[0:1, 0, 1], 0.0)
            nc.gpsimd.memset(hg_hi[:, FC - 1].bitcast(F32), 0.0)
            nc.gpsimd.memset(hg_lo[:, FC - 1].bitcast(F32), 0.0).then_inc(zero_made, 1)

            def inverse_norms(a, t):
                pool.wait_ge(dve_cl, at(a, NT, t + 1))
                nc.gpsimd.tensor_tensor(n_inv[:, t], n_cl[:, t], half_neg[:], ALU.pow).then_inc(pool_inv, 1)

            def norm_qk(a, t):
                pool.wait_ge(dve_rope, at(a, NT, t + 1))
                nc.gpsimd.tensor_tensor(r_cos[:, t], r_cos[:, t], r_sin[:, t], ALU.add).then_inc(pool_sum, 1)
                pool.wait_ge(pool_inv, at(a, NT, t + 1))
                pool.wait_ge(pool_sum, at(a, NT, t + 1))
                rows = r_cos[:, t].rearrange("p (h d) -> p h d", d=DH)
                nc.gpsimd.tensor_tensor(rows, rows, n_inv[:, t].unsqueeze(2).broadcast_to([P, 2 * HEADS, DH]),
                                        ALU.mult).then_inc(pool_qk, 1)

            def run_l(g, layer=None):
                a, b, c, par = l_roles(g)
                if c is not None:
                    ly = layer_of(c, layer)
                    pool.wait_ge(dve_x1, at(c, 1, 1))
                    if later(c):
                        pool.wait_ge(dve_x2, at(plus(c, -1), 1, 1))
                    nc.gpsimd.tensor_tensor(x1b[:].rearrange("p t (c n) -> p t c n", c=KC), x1[:, :, 0:3:2],
                                            b2_t[:, ly].rearrange("p (c n) -> p c n", c=KC).unsqueeze(1).broadcast_to(
                                                [P, NT, KC, P]), ALU.add).then_inc(pool_x1b, 1)
                    deviation(l_mv[:, :, 1], l_ve[:], l_rs[:], c, dve_bmv, at(c, 1, 1), pool_eps, pool_rst)
                if a is not None:
                    inverse_norms(a, 0)
                    norm_qk(a, 0)
                    inverse_norms(a, 1)
                if c is not None:
                    if ly == LAYERS - 1:
                        pool.wait_ge(pool_x1b, at(c, 1, 1))
                        pool.wait_ge(orig_load, at(plus(c, -SEQS), 16, 16))
                        nc.gpsimd.tensor_tensor(x1b[:], x1b[:], x_orig[:], ALU.add).then_inc(pool_x1o, 1)
                    for m in range(FC):
                        rows = P if m < FC - 1 else TAIL
                        pool.wait_ge(dve_hghi, at(c, FC, m + 1))
                        nc.gpsimd.tensor_tensor(hg_lo[0:rows, m], hg[0:rows, m], hg_hi[0:rows, m].bitcast(F32),
                                                ALU.subtract).then_inc(pool_hglo, 1)
                if a is not None:
                    norm_qk(a, 1)

            l_iterations(pool, run_l, lambda g: None)


def kernel(x, ctx_768, L0_xattn_Wq, L0_xattn_Wk, L0_xattn_Wv, L0_xattn_Wo, L0_xattn_bo, L0_ffn_wqkv, L0_ffn_q_scale,
           L0_ffn_k_scale, L0_ffn_wo, L0_ffn_ln_g, L0_ffn_ln_b, L0_ffn_w1, L0_ffn_b1, L0_ffn_w2, L0_ffn_b2):
    import concourse.bacc as bacc
    from concourse.bass_utils import run_bass_kernel_spmd

    def rows_padded(w, rows):
        w = np.asarray(w)
        p = np.zeros(w.shape[:-2] + (rows,) + w.shape[-1:], w.dtype)
        p[..., :w.shape[-2], :] = w
        return p

    w1 = np.asarray(L0_ffn_w1)
    b1 = np.asarray(L0_ffn_b1)
    w1_p = np.zeros((LAYERS, D, W1C, P), w1.dtype)
    b1_p = np.zeros((LAYERS, P, 2, FC), b1.dtype)
    for m in range(FC):
        n = P if m < FC - 1 else TAIL
        for part in range(2):
            src = slice(part * HID + m * P, part * HID + m * P + n)
            chunk, to = (2 * m + part, 0) if m < FC - 1 else (W1C - 1, part * TAIL_G)
            w1_p[:, :, chunk, to:to + n] = w1[:, :, src]
            b1_p[:, to:to + n, part, m] = b1[:, src]
    by_channel = lambda v: np.ascontiguousarray(np.asarray(v).reshape(LAYERS, KC, P).transpose(0, 2, 1))

    arrays = {
        "x": np.asarray(x), "ctx": np.asarray(ctx_768),
        "xwq": np.asarray(L0_xattn_Wq), "xwk": rows_padded(L0_xattn_Wk, 2 * P), "xwv": rows_padded(L0_xattn_Wv, 2 * P),
        "xwo": np.asarray(L0_xattn_Wo), "xbo": np.asarray(L0_xattn_bo),
        "wqkv": np.asarray(L0_ffn_wqkv), "qsc": np.asarray(L0_ffn_q_scale), "ksc": np.asarray(L0_ffn_k_scale),
        "wo": np.asarray(L0_ffn_wo), "lng": by_channel(L0_ffn_ln_g), "lnb": by_channel(L0_ffn_ln_b),
        "w1": w1_p.reshape(LAYERS, D, W1C * P), "b1": b1_p,
        "w2": rows_padded(L0_ffn_w2, FC * P), "b2": np.asarray(L0_ffn_b2),
        "rope": rope_tables(), "mask": masks(), "ident": np.eye(P, dtype=np.float32),
    }
    nc = bacc.Bacc("TRN2", target_bir_lowering=False, num_devices=1)
    args = []
    for name, a in arrays.items():
        arrays[name] = a = np.ascontiguousarray(a)
        args.append(nc.dram_tensor(name, a.shape, mybir.dt.from_np(a.dtype), kind="ExternalInput").ap())
    args.append(nc.dram_tensor("out", (SEQS, T, D), F32, kind="ExternalOutput").ap())
    build(nc, *args)
    r = run_bass_kernel_spmd(nc, [arrays], core_ids=[0])
    return r.results[0]["out"]
```

```python
from contextlib import ExitStack

import numpy as np

import concourse.bass as bass
from concourse import mybir

F32 = mybir.dt.float32
F32R = mybir.dt.float32r
ALU = mybir.AluOpType
ACT = mybir.ActivationFunctionType
AX = mybir.AxisListType

P = 128
SEQS, T, D = 16, 256, 256
NT = T // P
KC = D // P
HEADS, DH = 8, 64
INNER = HEADS * DH
IC = INNER // P
CTX, CD = 77, 192
LAYERS = 2
ITEMS = LAYERS * SEQS
HID = int(D * 4 * 2 / 3)
FC = -(-HID // P)
TAIL = HID - (FC - 1) * P
TAIL_G = 64
W1C = 2 * (FC - 1) + 1
QKV = 3 * INNER
EPS = 1e-5
NORM_MIN_SQ = 1e-24
QK_SCALE = 8.0
WINDOW = 128
MASKED = -1e30
FAR = 3e38
UNITS = 6
XUNITS = 4

WEIGHT = {name: n + 1 for n, name in enumerate(
    ["xq", "xo", "wo0", "w20", "qkv0", "w10", "qkv1", "wo1", "w11", "w21"])}


def rope_tables():
    half = np.arange(0, DH, 2, dtype=np.float32)
    freq = np.arange(T, dtype=np.float32)[:, None] * (1.0 / 10000.0 ** (half / DH))[None, :]
    base = (half + 0.4 * DH) / (1.4 * DH)
    power = (np.arange(T, dtype=np.float32) - T // 2) / float(WINDOW // 2)
    scale = (base[None, :] ** power[:, None]).astype(np.float32)
    cos, sin = np.cos(freq.astype(np.float32)), np.sin(freq.astype(np.float32))
    q = scale * np.float32(QK_SCALE)
    k = np.float32(1.0) / scale
    out = np.empty((2, T, 2, DH), np.float32)
    for j, s in enumerate((q, k)):
        out[0, :, j] = np.concatenate([cos * s, cos * s], -1)
        out[1, :, j] = np.concatenate([-sin * s, sin * s], -1)
    return np.ascontiguousarray(out.reshape(2, NT, P, 2, DH).transpose(2, 0, 1, 3, 4))


def masks():
    i, j = np.arange(P)[:, None], np.arange(P)[None, :]
    return np.stack([np.where(j < i, MASKED, 0.0), np.where(j > i, MASKED, 0.0)], 1).astype(np.float32)


def at(n, per, k):
    if isinstance(n, int):
        return n * per + k
    i, c = n
    return i * (2 * per) + (c * per + k)


def of_parity(n):
    return 16 * (n // 2 + 1) if isinstance(n, int) else n[0] * 16 + 16 * (n[1] // 2 + 1)


def plus(n, d):
    return n + d if isinstance(n, int) else (n[0], n[1] + d)


def index(n):
    return n if isinstance(n, int) else n[0] * 2 + n[1]


def later(n):
    return not (isinstance(n, int) and n == 0)


def build(nc, x, ctx_in, xwq, xwk, xwv, xwo, xbo, wqkv, qsc, ksc, wo, lng, lnb, w1, b1, w2, b2, rope, mask, ident, out):
    ctx = ExitStack()
    with ctx:
        def sb(name, shape, dt=F32, where=ctx):
            return where.enter_context(nc.sbuf_tensor(name, shape, dt))

        def sem(name):
            return ctx.enter_context(nc.semaphore(name))

        y_dram = nc.dram_tensor("y_state", (SEQS, P, NT, D), F32, kind="Internal").ap()
        x1_dram = nc.dram_tensor("x1_state", (SEQS, P, NT, D), F32, kind="Internal").ap()

        pb = ctx.enter_context(nc.psum_tensor("pb", [P, 8, 512], F32))
        id_f = sb("id_f", [P, P])
        mask_t = sb("mask_t", [P, 2, P])
        half_neg = sb("half_neg", [P, 2 * HEADS])
        eps_t = sb("eps_t", [P, NT])
        cos_t = sb("cos_t", [P, LAYERS, NT, 2, DH])
        sin_t = sb("sin_t", [P, LAYERS, NT, 2, DH])
        b2_t = sb("b2_t", [P, LAYERS, D])
        bo_t = sb("bo_t", [P, D])
        b1_t = sb("b1_t", [P, LAYERS, 2, FC])
        lng_t = sb("lng_t", [P, LAYERS, KC])
        lnb_t = sb("lnb_t", [P, LAYERS, KC])
        wqkv_hi = sb("wqkv_hi", [P, KC, QKV], F32R)
        wqkv_lo = sb("wqkv_lo", [P, KC, QKV], F32R)
        wo_hi = sb("wo_hi", [P, IC, D], F32R)
        wo_lo = sb("wo_lo", [P, IC, D], F32R)
        w1_hi = sb("w1_hi", [P, KC, W1C, P], F32R)
        w1_lo = sb("w1_lo", [P, KC, W1C, P], F32R)
        w2_hi = sb("w2_hi", [P, FC, D], F32R)
        w2_lo = sb("w2_lo", [P, FC, D], F32R)
        raw_a = sb("raw_a", [P, KC * QKV])
        raw_b = sb("raw_b", [P, (IC + FC) * D])

        x1_x = sb("x1_x", [P, NT, D])
        y_x = sb("y_x", [P, NT, D])
        x_st = sb("x_st", [P, 2, NT, 6])
        x_mv = sb("x_mv", [P, 2, NT, 2])
        x_ve = sb("x_ve", [P, 2, NT])
        x_rs = sb("x_rs", [P, 2, NT])

        X = ExitStack()
        rope_raw = sb("rope_raw", [P, 2, NT, 2, DH], where=X)
        sc_t = sb("sc_t", [P, LAYERS, 2, 2, DH], where=X)
        xq_hi = sb("xq_hi", [P, KC, INNER], F32R, X)
        xq_lo = sb("xq_lo", [P, KC, INNER], F32R, X)
        xk_w = sb("xk_w", [P, 2, INNER], where=X)
        xv_w = sb("xv_w", [P, 2, INNER], where=X)
        x_in = sb("x_in", [P, 2, NT, D], where=X)
        c_in = sb("c_in", [P, 2, D], where=X)
        xn = sb("xn", [P, NT, D], where=X)
        xn_hi = sb("xn_hi", [P, KC, T], F32R, X)
        xn_lo = sb("xn_lo", [P, KC, T], F32R, X)
        c_t = sb("c_t", [P, 2, CTX], where=X)
        xq_t = sb("xq_t", [P, 2, IC, T], where=X)
        xk_t = sb("xk_t", [P, 2, IC, CTX], where=X)
        x_v = sb("x_v", [P, 2, INNER], where=X)
        x_p = sb("x_p", [P, XUNITS, 4, CTX], where=X)
        x_pt = sb("x_pt", [P, XUNITS, 4, P], where=X)
        x_nm = sb("x_nm", [P, XUNITS, 4], where=X)
        x_sum = sb("x_sum", [P, XUNITS, 4], where=X)
        x_inv = sb("x_inv", [P, XUNITS, 4], where=X)
        xo_hi = sb("xo_hi", [P, IC, D], F32R, X)
        xo_lo = sb("xo_lo", [P, IC, D], F32R, X)
        xo_hi_t = sb("xo_hi_t", [P, IC, T], F32R, X)
        xo_lo_t = sb("xo_lo_t", [P, IC, T], F32R, X)
        x_b = sb("x_b", [P, 2, NT, D], where=X)
        X.close()

        L = ctx.enter_context(ExitStack())
        r_cos = sb("r_cos", [P, NT, 2 * INNER], where=L)
        r_sin = sb("r_sin", [P, NT, 2 * INNER], where=L)
        n_sq = sb("n_sq", [P, NT, 2 * HEADS], where=L)
        n_cl = sb("n_cl", [P, NT, 2 * HEADS], where=L)
        n_inv = sb("n_inv", [P, NT, 2 * HEADS], where=L)
        qk_t = sb("qk_t", [P, 2, IC, T], where=L)
        v_t = sb("v_t", [P, 2, NT, INNER], where=L)
        p_t = sb("p_t", [P, 3, 512], where=L)
        pt_t = sb("pt_t", [P, 2, 512], where=L)
        s_nm = sb("s_nm", [P, UNITS, 4], where=L)
        s_sum = sb("s_sum", [P, UNITS, 4], where=L)
        s_inv = sb("s_inv", [P, UNITS, 4], where=L)
        o_hi = sb("o_hi", [P, IC, T], F32R, L)
        o_lo = sb("o_lo", [P, IC, T], F32R, L)
        x1 = sb("x1", [P, NT, 3, P], where=L)
        x1b = sb("x1b", [P, NT, D], where=L)
        l_st = sb("l_st", [P, NT, 6], where=L)
        l_mv = sb("l_mv", [P, NT, 2], where=L)
        l_ve = sb("l_ve", [P, NT], where=L)
        l_rs = sb("l_rs", [P, NT], where=L)
        h_n = sb("h_n", [P, NT, D], where=L)
        h_f = sb("h_f", [P, KC, T], where=L)
        h_hi = sb("h_hi", [P, KC, T], F32R, L)
        h_lo = sb("h_lo", [P, KC, T], F32R, L)
        gl = sb("gl", [P, 3, T], where=L)
        hg = sb("hg", [P, FC, T], where=L)
        hg_hi = sb("hg_hi", [P, FC, T], F32R, L)
        hg_lo = sb("hg_lo", [P, FC, T], F32R, L)
        x2 = sb("x2", [P, 2, NT, D], where=L)

        qk_sq = sb("qk_sq", [P, NT, 2 * INNER], where=L)
        x_cur = sb("x_cur", [P, NT, D], where=L)
        x_res = sb("x_res", [P, NT, D], where=L)
        x_orig = sb("x_orig", [P, NT, D], where=L)
        xt_hi = sb("xt_hi", [P, 2 * T + 1], F32R, L)
        xt_lo = sb("xt_lo", [P, 2 * T + 1], F32R, L)

        id_in, const_in = sem("id_in"), sem("const_in")
        raw_a_in, raw_b_in = sem("raw_a_in"), sem("raw_b_in")
        w_hi, w_lo = sem("w_hi"), sem("w_lo")
        const_made = sem("const_made")
        zero_made = sem("zero_made")
        x_load, c_load = [sem(f"x_load{u}") for u in range(2)], [sem(f"c_load{u}") for u in range(2)]
        x_bst, x_bmv = sem("x_bst"), sem("x_bmv")
        x_eps, x_rst = sem("x_eps"), sem("x_rst")
        x_norm = sem("x_norm")
        x_bias = sem("x_bias")
        x_tr, c_tr = sem("x_tr"), sem("c_tr")
        x_thi, x_tlo = sem("x_thi"), sem("x_tlo")
        c_cp = sem("c_cp")
        x_pq, x_pk, x_pv = sem("x_pq"), sem("x_pk"), sem("x_pv")
        x_cq, x_ck, x_cv = sem("x_cq"), sem("x_ck"), sem("x_cv")
        x_s, x_max, x_exp, x_rec, x_pn = sem("x_s"), sem("x_max"), sem("x_exp"), sem("x_rec"), sem("x_pn")
        x_ptr, x_ptc, x_av = sem("x_ptr"), sem("x_ptc"), sem("x_av")
        x_ohi, x_olo, x_wo = sem("x_ohi"), sem("x_olo"), sem("x_wo")
        x_res1, y_bst, y_bmv, y_eps, y_rst, y_norm = [sem(n) for n in (
            "x_res1", "y_bst", "y_bmv", "y_eps", "y_rst", "y_norm")]
        x1_store, y_store = sem("x1_store"), sem("y_store")
        stats_seen, scores_seen = sem("stats_seen"), sem("scores_seen")
        cur_load, res_load, orig_load, shift, x2_store = [sem(n) for n in (
            "cur_load", "res_load", "orig_load", "shift", "x2_store")]
        pe_xt, act_xhi, dve_xlo = sem("pe_xt"), sem("act_xhi"), sem("dve_xlo")
        pe_qkv, act_sq, act_v = sem("pe_qkv"), sem("act_sq"), sem("act_v")
        dve_ss, dve_cl, dve_rope = sem("dve_ss"), sem("dve_cl"), sem("dve_rope")
        pool_inv, pool_sum, pool_qk = sem("pool_inv"), sem("pool_sum"), sem("pool_qk")
        pe_qkt, act_qkt = sem("pe_qkt"), sem("act_qkt")
        pe_s, dve_max, act_exp, dve_rec, dve_pn = sem("pe_s"), sem("dve_max"), sem("act_exp"), sem("dve_rec"), sem("dve_pn")
        pe_pt, act_pt, pe_av, act_ohi, dve_olo = sem("pe_pt"), sem("act_pt"), sem("pe_av"), sem("act_ohi"), sem("dve_olo")
        pe_wo, dve_x1, pool_x1b = sem("pe_wo"), sem("dve_x1"), sem("pool_x1b")
        dve_bst, dve_bmv, pool_eps, pool_rst, dve_h = [sem(n) for n in ("dve_bst", "dve_bmv", "pool_eps", "pool_rst", "dve_h")]
        pe_ht, act_h, dve_hhi, dve_hlo = sem("pe_ht"), sem("act_h"), sem("dve_hhi"), sem("dve_hlo")
        pe_w1, act_gelu, dve_hg, dve_hghi, pool_hglo = [sem(n) for n in ("pe_w1", "act_gelu", "dve_hg", "dve_hghi", "pool_hglo")]
        pe_w2, dve_x2, dve_out = sem("pe_w2"), sem("dve_x2"), sem("dve_out")

        CONSTS = 0

        x_rows = x.rearrange("s (t p) d -> s p t d", p=P)
        out_rows = out.rearrange("s (t p) d -> s p t d", p=P)

        def one(t, n):
            return t[bass.ds(n, 1)].rearrange("o p t d -> p (o t) d")

        def x_iterations(eng, run):
            for g in range(3):
                run(g)
            with eng.Fori(1, SEQS // 2 - 1) as i:
                for u in range(2):
                    run((i, u + 1))
            for g in range(SEQS - 1, SEQS + 2):
                run(g)

        def x_roles(g):
            whole = isinstance(g, int)
            a = None if whole and g >= SEQS else g
            b = None if whole and not 1 <= g <= SEQS else plus(g, -1)
            d = None if whole and g < 2 else plus(g, -2)
            return a, b, d, (g if whole else g[1]) % 2

        def l_iterations(eng, run, between):
            for layer in range(LAYERS):
                first = layer * SEQS
                between(first)
                run(first)
                between(first + 1)
                run(first + 1)
                between(first + 2)
                run(first + 2)
                run(first + 3)
                with eng.Fori(first // 2 + 2, (first + SEQS) // 2 - 1) as i:
                    for u in range(2):
                        run((i, u), layer)
                for g in range(first + SEQS - 2, first + SEQS):
                    run(g)
            run(ITEMS)
            run(ITEMS + 1)

        def l_roles(g):
            a = g if not isinstance(g, int) or g < ITEMS else None
            b = plus(g, -1) if not isinstance(g, int) or 1 <= g <= ITEMS else None
            c = plus(g, -2) if not isinstance(g, int) or g >= 2 else None
            return a, b, c, (g if isinstance(g, int) else g[1]) % 2

        QK_PARTS = [(0, slice(0, 1)), (0, slice(1, 2)), (1, slice(0, 2))]
        W1_BANK = [6, 7, 5, 4, 6, 7]
        S_BANK = [2, 0, 1, 2, 0, 1]

        def heads_of(u):
            return range(u // 2 * 4 + u % 2, u // 2 * 4 + 4, 2) if u < 4 else range(u % 2, HEADS, 2)

        def layer_of(n, layer):
            return n // SEQS if isinstance(n, int) else layer

        def seq_of(n, layer):
            return n % SEQS if isinstance(n, int) else n[0] * 2 + (n[1] - layer * SEQS)

        def shifted(t):
            whole = t[:]
            return bass.AP(tensor=whole.tensor, offset=whole.offset, ap=[list(whole.ap[0]), [T + 1, KC], [1, T]])

        block = ctx.enter_context(nc.Block())

        @block.sync
        def _(sp):
            nonlocal CONSTS
            def load_x(n):
                par = (n if isinstance(n, int) else n[1]) % 2
                sp.dma_start(x_in[:, par], one(x_rows, index(n))).then_inc(x_load[par], 16)
                sp.dma_start(c_in[0:CTX, par, 0:CD],
                             ctx_in[bass.ds(index(n), 1)].rearrange("o s d -> s (o d)")).then_inc(c_load[par], 16)

            sp.wait_ge(zero_made, 1)
            load_x(0)
            sp.dma_start(id_f[:], ident).then_inc(id_in, 16)
            sp.dma_start(raw_a[:, 0:KC * INNER].rearrange("p (c n) -> p c n", c=KC),
                         xwq.rearrange("(c p) n -> p c n", p=P)).then_inc(raw_a_in, 16)
            sp.dma_start(raw_a[:, KC * INNER:KC * INNER + IC * D].rearrange("p (c n) -> p c n", c=IC),
                         xwo.rearrange("(c p) n -> p c n", p=P)).then_inc(raw_a_in, 16)

            load_x(1)
            consts = [
                (xk_w[:], xwk.rearrange("(c p) n -> p c n", p=P)),
                (xv_w[:], xwv.rearrange("(c p) n -> p c n", p=P)),
                (bo_t[:], xbo.partition_broadcast(P)),
                (mask_t[:], mask),
                (rope_raw[:], rope),
            ]
            for layer in range(LAYERS):
                consts.append((b2_t[:, layer], b2[layer].partition_broadcast(P)))
                consts.append((b1_t[:, layer], b1[layer]))
                consts.append((lng_t[:, layer], lng[layer]))
                consts.append((lnb_t[:, layer], lnb[layer]))
                for j, s in enumerate((qsc, ksc)):
                    consts.append((sc_t[:, layer, 0, j], s[layer].partition_broadcast(P)))
                    for half in range(2):
                        consts.append((sc_t[:, layer, 1, j, half * 32:half * 32 + 32],
                                       s[layer, 32 - half * 32:64 - half * 32].partition_broadcast(P)))
            for dst, src in consts:
                sp.dma_start(dst, src).then_inc(const_in, 16)
            CONSTS = 16 * len(consts)

            def load_b(layer):
                sp.dma_start(raw_b[:, 0:IC * D].rearrange("p (c n) -> p c n", c=IC),
                             wo[layer].rearrange("(c p) n -> p c n", p=P)).then_inc(raw_b_in, 16)
                sp.dma_start(raw_b[:, IC * D:(IC + FC) * D].rearrange("p (c n) -> p c n", c=FC),
                             w2[layer].rearrange("(c p) n -> p c n", p=P)).then_inc(raw_b_in, 16)

            def load_qkv(layer):
                sp.dma_start(raw_a[:].rearrange("p (c n) -> p c n", c=KC),
                             wqkv[layer].rearrange("(c p) n -> p c n", p=P)).then_inc(raw_a_in, 16)

            def load_w1(layer):
                sp.dma_start(raw_a[:, 0:KC * W1C * P].rearrange("p (c n) -> p c n", c=KC),
                             w1[layer].rearrange("(c p) n -> p c n", p=P)).then_inc(raw_a_in, 16)

            load_b(0)

            def run_x(g):
                a, b, d, par = x_roles(g)
                if d is not None:
                    sp.wait_ge(x_res1, at(d, 1, 1))
                    sp.dma_start(one(x1_dram, index(d)), x1_x[:]).then_inc(x1_store, 16)
                    sp.wait_ge(y_norm, at(d, 1, 1))
                    sp.dma_start(one(y_dram, index(d)), y_x[:]).then_inc(y_store, 16)
                if not isinstance(g, int) or g < SEQS - 2:
                    sp.wait_ge(x_norm, at(a, 1, 1))
                    sp.wait_ge(x_bias, at(a, 1, 1))
                    sp.wait_ge(c_tr, at(a, 1, 1))
                    load_x(plus(a, 2))
                if isinstance(g, int) and g == 0:
                    sp.wait_ge(w_lo, WEIGHT["xo"])
                    load_qkv(0)
                if isinstance(g, int) and g == 1:
                    sp.wait_ge(w_lo, WEIGHT["qkv0"])
                    load_w1(0)
                    load_b(1)
                if isinstance(g, int) and g == SEQS - 1:
                    sp.wait_ge(y_store, 16 * (SEQS - 2))
                    sp.dma_start(x_cur[:], one(y_dram, 0)).then_inc(cur_load, 16)
                    sp.dma_start(x_res[:], one(y_dram, 0)).then_inc(res_load, 16)
                    sp.wait_ge(w_lo, WEIGHT["w10"])
                    load_qkv(1)

            for g in range(3):
                run_x(g)
            with sp.Fori(1, SEQS // 2 - 2) as i:
                for u in range(2):
                    run_x((i, u + 1))
            for g in range(SEQS - 3, SEQS + 2):
                run_x(g)

            sp.wait_ge(x1_store, 16 * SEQS)
            sp.wait_ge(y_store, 16 * SEQS)

            def run_l(g, layer=None):
                a, b, c, par = l_roles(g)
                if c is not None:
                    sp.wait_ge(dve_x1, at(c, 1, 1))
                    sp.dma_start(x1[1:P, :, 1], x1[0:P - 1, :, 2]).then_inc(shift, 16)
                    sp.dma_start(x1[0:1, 1, 1], x1[P - 1:P, 0, 2]).then_inc(shift, 16)
                    if b is not None:
                        sp.dma_start(x_res[:], one(y_dram, seq_of(b, layer))).then_inc(res_load, 16)
                    if layer_of(c, layer) == LAYERS - 1:
                        sp.dma_start(x_orig[:], one(x1_dram, seq_of(c, layer))).then_inc(orig_load, 16)
                if a is not None and not (isinstance(a, int) and a == ITEMS - 1):
                    sp.wait_ge(pe_xt, at(a, 1, 1))
                    sp.dma_start(x_cur[:], one(y_dram, seq_of(plus(a, 1), layer))).then_inc(cur_load, 16)
                if c is not None:
                    if layer_of(c, layer) == LAYERS - 1:
                        sp.wait_ge(dve_out, at(plus(c, -SEQS), 1, 1))
                        dst = out_rows
                    else:
                        sp.wait_ge(dve_x2, at(c, 1, 1))
                        dst = y_dram
                    sp.dma_start(one(dst, seq_of(c, layer)), x2[:, par]).then_inc(x2_store, 16)

            def between(g):
                if g == SEQS:
                    sp.wait_ge(w_lo, WEIGHT["qkv1"])
                    load_w1(1)

            between(0)
            for g in range(4):
                run_l(g)
            with sp.Fori(2, SEQS // 2 - 1) as i:
                for u in range(2):
                    run_l((i, u), 0)
            run_l(SEQS - 2)
            run_l(SEQS - 1)
            between(SEQS)
            run_l(SEQS)
            run_l(SEQS + 1)
            with sp.Fori(SEQS // 2 + 1, SEQS - 1) as i:
                for u in range(2):
                    run_l((i, u), 1)
            for g in range(ITEMS - 2, ITEMS + 2):
                run_l(g)
            sp.wait_ge(x2_store, 16 * ITEMS)

        @block.tensor
        def _(pe):
            def bank(b):
                return pb[:, b]

            def split_product(dst, pairs):
                for n, (s_hi, s_lo, m_hi, m_lo) in enumerate(pairs):
                    for k, (s, m) in enumerate(((s_hi, m_hi), (s_hi, m_lo), (s_lo, m_hi))):
                        mm = pe.matmul(dst, s, m, start=(n == 0 and k == 0),
                                       stop=(n == len(pairs) - 1 and k == 2))
                return mm

            def turn_x(n):
                pe.wait_ge(cur_load, at(n, 16, 16))
                for c in range(KC):
                    for t in range(NT):
                        mm = pe.transpose(pb[:, 4, c * T + t * P:c * T + t * P + P], x_cur[:, t, c * P:c * P + P], id_f[:])
                mm.then_inc(pe_xt, 1)

            pe.wait_ge(id_in, 16)

            def x_turn(a, par):
                pe.wait_ge(x_norm, at(a, 1, 1))
                for c in range(KC):
                    for t in range(NT):
                        mm = pe.transpose(pb[:, 0, c * T + t * P:c * T + t * P + P], xn[:, t, c * P:c * P + P], id_f[:])
                mm.then_inc(x_tr, 1)
                pe.wait_ge(c_load[par], of_parity(a))
                for c in range(2):
                    mm = pe.transpose(pb[:, 1, c * P:c * P + CTX], c_in[0:CTX, par, c * P:c * P + P],
                                      id_f[0:CTX, 0:CTX])
                mm.then_inc(c_tr, 1)

            def x_scores(b, par, u):
                t, odd = u // 2, u % 2
                if u == 0:
                    pe.wait_ge(x_cq, at(b, 2, 2))
                    pe.wait_ge(x_ck, at(b, 1, 1))
                if u >= 2:
                    pe.wait_ge(x_exp, at(b, XUNITS, u - 1))
                for k in range(4):
                    r = odd * DH
                    mm = pe.matmul(pb[:, 2 + u % 2, k * P:k * P + CTX], xq_t[r:r + DH, par, k, t * P:t * P + P],
                                   xk_t[r:r + DH, par, k, :], start=True, stop=True)
                mm.then_inc(x_s, 1)

            def x_probs(b, u):
                pe.wait_ge(x_pn, at(b, XUNITS, u + 1))
                if u >= 2:
                    pe.wait_ge(x_ptc, at(b, XUNITS, u - 1))
                for k in range(4):
                    mm = pe.transpose(pb[0:CTX, u % 2, k * P:k * P + P], x_p[:, u, k, :], id_f[:])
                mm.then_inc(x_ptr, 1)

            def x_values(b, par, u):
                t, odd = u // 2, u % 2
                if u == 0:
                    pe.wait_ge(x_cv, at(b, 1, 1))
                pe.wait_ge(x_ptc, at(b, XUNITS, u + 1))
                for k in range(4):
                    h = 2 * k + odd
                    r, col = odd * DH, (k % 2) * T + t * P
                    mm = pe.matmul(pb[r:r + DH, 6 + k // 2, col:col + P], x_v[0:CTX, par, h * DH:h * DH + DH],
                                   x_pt[0:CTX, u, k, :], start=True, stop=True)
                mm.then_inc(x_av, 1)

            def x_out(a, d):
                if isinstance(d, int) and d == 0:
                    pe.wait_ge(w_lo, WEIGHT["xo"])
                pe.wait_ge(x_ohi, at(d, 2, 2))
                pe.wait_ge(x_olo, at(d, 2, 2))
                if a is not None:
                    pe.wait_ge(c_cp, at(a, 1, 1))
                for t in range(NT):
                    rows = slice(t * P, t * P + P)
                    mm = split_product(pb[:, 1, t * D:t * D + D],
                                       [(xo_hi_t[:, c, rows], xo_lo_t[:, c, rows], xo_hi[:, c], xo_lo[:, c])
                                        for c in range(IC)])
                mm.then_inc(x_wo, 1)

            def x_queries(a):
                pe.wait_ge(x_thi, at(a, 1, 1))
                pe.wait_ge(x_tlo, at(a, 1, 1))
                for c in range(IC):
                    cols = slice(c * P, c * P + P)
                    mm = split_product(pb[:, 4 + c // 2, (c % 2) * T:(c % 2) * T + T],
                                       [(xq_hi[:, k, cols], xq_lo[:, k, cols], xn_hi[:, k], xn_lo[:, k])
                                        for k in range(KC)])
                    if c % 2:
                        mm.then_inc(x_pq, 1)

            def x_keys_values(a):
                if isinstance(a, int) and a == 0:
                    pe.wait_ge(const_in, CONSTS)
                pe.wait_ge(c_cp, at(a, 1, 1))
                for c in range(IC):
                    for k in range(2):
                        mm = pe.matmul(pb[:, 6, c * P:c * P + CTX], xk_w[:, k, c * P:c * P + P], c_t[:, k, :],
                                       start=(k == 0), stop=(k == 1))
                mm.then_inc(x_pk, 1)
                for k in range(2):
                    mm = pe.matmul(pb[0:CTX, 7, :], c_t[:, k, :], xv_w[:, k, :], start=(k == 0), stop=(k == 1))
                mm.then_inc(x_pv, 1)

            def run_x(g):
                a, b, d, par = x_roles(g)
                was = 1 - par
                if isinstance(g, int) and g == 0:
                    x_turn(0, 0)
                    pe.wait_ge(w_lo, WEIGHT["xq"])
                if b is not None:
                    x_scores(b, was, 0)
                    x_scores(b, was, 1)
                if isinstance(g, int) and g == SEQS + 1:
                    turn_x(0)
                if d is not None:
                    x_out(a, d)
                if a is not None:
                    x_queries(a)
                if b is not None:
                    x_scores(b, was, 2)
                    x_scores(b, was, 3)
                    x_probs(b, 0)
                    if d is not None:
                        pe.wait_ge(x_res1, at(d, 1, 1))
                    x_probs(b, 1)
                if a is not None:
                    x_keys_values(a)
                if b is not None:
                    x_probs(b, 2)
                    x_probs(b, 3)
                    if a is not None:
                        pe.wait_ge(x_ck, at(a, 1, 1))
                        pe.wait_ge(x_cv, at(a, 1, 1))
                    for u in range(XUNITS):
                        x_values(b, was, u)
                if a is not None and not (isinstance(a, int) and a == SEQS - 1):
                    x_turn(plus(a, 1), 1 - par)

            x_iterations(pe, run_x)

            QKV_BANK = {(0, 0): 0, (0, 1): 1, (1, 0): 3, (1, 1): 4, (0, 2): 2, (1, 2): 5}

            def project(a, t, part):
                b = QKV_BANK[t, part]
                if isinstance(a, int) and a == 0 and b == 1:
                    pe.wait_ge(x_res1, SEQS)
                if part < 2 and b < 4 and later(a):
                    pe.wait_ge(act_qkt, at(plus(a, -1), 4, b + 1))
                if part == 2 and b == 2 and later(a):
                    pe.wait_ge(act_qkt, at(plus(a, -1), 4, 3))
                cols = slice(part * INNER, part * INNER + INNER)
                mm = split_product(bank(b), [(xt_hi[:, c * T + t * P:c * T + t * P + P],
                                              xt_lo[:, c * T + t * P:c * T + t * P + P],
                                              wqkv_hi[:, c, cols], wqkv_lo[:, c, cols]) for c in range(KC)])
                mm.then_inc(pe_qkv, 1)

            def turn_h(c):
                pe.wait_ge(dve_h, at(c, 1, 1))
                for k in range(KC):
                    for t in range(NT):
                        mm = pe.transpose(pb[:, 7, k * T + t * P:k * T + t * P + P], h_n[:, t, k * P:k * P + P], id_f[:])
                mm.then_inc(pe_ht, 1)

            def hidden(a, c, m):
                if m == 0:
                    if isinstance(c, int) and c == SEQS:
                        pe.wait_ge(w_lo, WEIGHT["w11"])
                    pe.wait_ge(dve_hhi, at(c, 1, 1))
                    pe.wait_ge(dve_hlo, at(c, 1, 1))
                if m == 2 and a is not None:
                    pe.wait_ge(act_v, at(a, NT, NT))
                if m == 3 and a is not None:
                    pe.wait_ge(dve_rope, at(a, NT, NT))
                if m >= 4:
                    pe.wait_ge(dve_hg, at(c, FC, m - 3))
                for part in range(2 if m < FC - 1 else 1):
                    n = 2 * m + part
                    mm = split_product(pb[:, W1_BANK[m], part * T:part * T + T],
                                       [(w1_hi[:, k, n], w1_lo[:, k, n], h_hi[:, k], h_lo[:, k]) for k in range(KC)])
                mm.then_inc(pe_w1, 1)

            def scores(a, b, c, u):
                if u == 0:
                    pe.wait_ge(act_qkt, at(b, 4, 4))
                    if a is not None:
                        pe.wait_ge(act_v, at(a, NT, 1))
                if u == 1 and a is not None:
                    pe.wait_ge(dve_rope, at(a, NT, 1))
                if u >= 3:
                    pe.wait_ge(dve_max, at(b, UNITS, u - 2))
                win1 = u < 4
                keys = T if win1 else P
                for k, h in enumerate(heads_of(u)):
                    ch, r = h // 2, (h % 2) * DH
                    q_cols = slice(P, T) if win1 else slice(0, P)
                    mm = pe.matmul(pb[:, S_BANK[u], k * keys:k * keys + keys], qk_t[r:r + DH, 0, ch, q_cols],
                                   qk_t[r:r + DH, 1, ch, 0:keys], start=True, stop=True)
                mm.then_inc(pe_s, 1)

            def turn_p(a, b, c, u):
                pe.wait_ge(dve_pn, at(b, UNITS, u + 1))
                if u == 0 and a is not None:
                    pe.wait_ge(dve_rope, at(a, NT, 2))
                if u == 1 and c is not None:
                    pe.wait_ge(dve_hg, at(c, FC, 4))
                if u >= 2:
                    pe.wait_ge(act_pt, at(b, UNITS, u - 1))
                for k in range(4):
                    mm = pe.transpose(pb[:, 3 + u % 2, k * P:k * P + P], p_t[:, u % 3, k * P:k * P + P], id_f[:])
                mm.then_inc(pe_pt, 1)

            def weigh(a, b, c, par, u):
                pe.wait_ge(act_pt, at(b, UNITS, u + 1))
                if u == 0:
                    pe.wait_ge(act_v, at(b, NT, NT))
                    if c is not None:
                        pe.wait_ge(dve_hg, at(c, FC, FC))
                    elif a is not None:
                        pe.wait_ge(act_v, at(a, NT, NT))
                if u < 4:
                    for k, h in enumerate(heads_of(u)):
                        r, col = (h % 2) * DH, (h // 2 % 2) * T + P
                        for t in range(NT):
                            mm = pe.matmul(pb[r:r + DH, 5 + h // 4, col:col + P],
                                           v_t[:, par, t, h * DH:h * DH + DH],
                                           pt_t[:, u % 2, (2 * k + t) * P:(2 * k + t) * P + P],
                                           start=(t == 0), stop=(t == NT - 1))
                else:
                    for k, h in enumerate(heads_of(u)):
                        r, col = (h % 2) * DH, (h // 2 % 2) * T
                        mm = pe.matmul(pb[r:r + DH, 5 + h // 4, col:col + P], v_t[:, par, 0, h * DH:h * DH + DH],
                                       pt_t[:, u % 2, k * P:k * P + P], start=True, stop=True)
                mm.then_inc(pe_av, 1)

            def feed(c, n):
                t, k = n // FC, n % FC
                if n == 0:
                    if isinstance(c, int) and c == SEQS:
                        pe.wait_ge(w_lo, WEIGHT["w21"])
                    pe.wait_ge(dve_hg, at(c, FC, FC))
                if t == 0:
                    pe.wait_ge(dve_hghi, at(c, FC, k + 1))
                    pe.wait_ge(pool_hglo, at(c, FC, k + 1))
                rows = slice(t * P, t * P + P)
                for j, (s, m) in enumerate(((hg_hi, w2_hi), (hg_hi, w2_lo), (hg_lo, w2_hi))):
                    mm = pe.matmul(pb[:, 7, t * D:t * D + D], s[:, k, rows], m[:, k],
                                   start=(k == 0 and j == 0), stop=(k == FC - 1 and j == 2))
                if n == NT * FC - 1:
                    mm.then_inc(pe_w2, 1)

            def run_l(g, layer=None):
                a, b, c, par = l_roles(g)
                if a is not None:
                    pe.wait_ge(act_xhi, at(a, 1, 1))
                    pe.wait_ge(dve_xlo, at(a, 1, 1))
                    for t in range(NT):
                        for part in range(2):
                            project(a, t, part)
                    for t in range(NT):
                        project(a, t, 2)
                if c is not None:
                    turn_h(c)
                if b is not None:
                    for u in range(3):
                        scores(a, b, c, u)
                if c is not None:
                    for m in range(FC):
                        hidden(a, c, m)
                if b is not None:
                    turn_p(a, b, c, 0)
                    scores(a, b, c, 3)
                    turn_p(a, b, c, 1)
                    scores(a, b, c, 4)
                    scores(a, b, c, 5)
                for j in range(UNITS):
                    if c is not None:
                        feed(c, 2 * j)
                        feed(c, 2 * j + 1)
                    if b is not None:
                        if j < 3 or j == 4:
                            weigh(a, b, c, 1 - par, min(j, 3))
                        if j == 0:
                            turn_p(a, b, c, 2)
                        if 2 <= j < 5:
                            turn_p(a, b, c, j + 1)
                if b is not None:
                    weigh(a, b, c, 1 - par, 4)
                    weigh(a, b, c, 1 - par, 5)
                if a is not None:
                    for k in range(4):
                        if k == 0:
                            pe.wait_ge(pool_qk, at(a, NT, NT))
                        if k == 2 and b is None:
                            pe.wait_ge(act_v, at(a, NT, 1))
                        for j in range(2):
                            for t in range(NT):
                                col = (2 * k + j) * P
                                mm = pe.transpose(pb[:, k, j * T + t * P:j * T + t * P + P],
                                                  r_cos[:, t, col:col + P], id_f[:])
                        mm.then_inc(pe_qkt, 1)
                    if not (isinstance(a, int) and a == ITEMS - 1):
                        turn_x(plus(a, 1))
                if b is not None:
                    pe.wait_ge(act_ohi, at(b, 2, 2))
                    pe.wait_ge(dve_olo, at(b, 2, 2))
                    if isinstance(b, int) and b == SEQS:
                        pe.wait_ge(w_lo, WEIGHT["wo1"])
                    if c is not None:
                        pe.wait_ge(dve_x2, at(c, 1, 1))
                    for t in range(NT):
                        rows = slice(t * P, t * P + P)
                        mm = split_product(pb[:, 7, t * D:t * D + D],
                                           [(o_hi[:, k, rows], o_lo[:, k, rows], wo_hi[:, k], wo_lo[:, k])
                                            for k in range(IC)])
                    mm.then_inc(pe_wo, 1)

            def between(g):
                if g == 0:
                    pe.wait_ge(w_lo, WEIGHT["w10"])
                elif g == SEQS:
                    pe.wait_ge(w_lo, WEIGHT["qkv1"])

            l_iterations(pe, run_l, between)

        @block.scalar
        def _(act):
            def split_hi(name, src, dst):
                nc.scalar.activation(dst, src, ACT.Copy).then_inc(w_hi, 1)

            act.wait_ge(raw_a_in, 32)
            split_hi("xq", raw_a[:, 0:KC * INNER].rearrange("p (c n) -> p c n", c=KC), xq_hi[:])
            split_hi("xo", raw_a[:, KC * INNER:KC * INNER + IC * D].rearrange("p (c n) -> p c n", c=IC), xo_hi[:])

            def split_third(g, m):
                if not isinstance(g, int) or not 1 <= g <= 2:
                    return
                if g == 1:
                    act.wait_ge(raw_a_in, 48)
                    cols = slice(m * INNER, m * INNER + INNER)
                    e = nc.scalar.activation(wqkv_hi[:, :, cols], raw_a[:].rearrange("p (c n) -> p c n", c=KC)[:, :, cols],
                                             ACT.Copy)
                else:
                    act.wait_ge(raw_a_in, 64)
                    chunks = slice(m * 4, min(m * 4 + 4, W1C))
                    e = nc.scalar.activation(w1_hi[:, :, chunks], raw_a[:, 0:KC * W1C * P].rearrange(
                        "p (c m n) -> p c m n", c=KC, n=P)[:, :, chunks], ACT.Copy)
                if m == 2:
                    e.then_inc(w_hi, 1)

            def x_turned(a):
                act.wait_ge(x_tr, at(a, 1, 1))
                nc.scalar.activation(xn_hi[:].rearrange("p c t -> p (c t)"), pb[:, 0], ACT.Copy).then_inc(x_thi, 1)
                act.wait_ge(c_tr, at(a, 1, 1))
                nc.scalar.activation(c_t[:], pb[:, 1, 0:2 * P].rearrange("p (c n) -> p c n", c=2)[:, :, 0:CTX],
                                     ACT.Copy).then_inc(c_cp, 1)

            def x_exps(b, u):
                act.wait_ge(x_max, at(b, XUNITS, u + 1))
                if later(b):
                    act.wait_ge(x_ptr, at(plus(b, -1), XUNITS, u + 1))
                for k in range(4):
                    e = nc.scalar.activation(x_p[:, u, k, :], pb[:, 2 + u % 2, k * P:k * P + CTX], ACT.Exp,
                                             bias=x_nm[:, u, k:k + 1], scale=1.0, accum_out=x_sum[:, u, k:k + 1])
                e.then_inc(x_exp, 1)

            def x_probs_copy(b, u):
                act.wait_ge(x_ptr, at(b, XUNITS, u + 1))
                nc.scalar.activation(x_pt[0:CTX, u].rearrange("p k n -> p (k n)"), pb[0:CTX, u % 2],
                                     ACT.Copy).then_inc(x_ptc, 1)

            def run_x(g):
                a, b, d, par = x_roles(g)
                if isinstance(g, int) and g == 0:
                    x_turned(0)
                if b is not None:
                    x_exps(b, 0)
                    x_exps(b, 1)
                split_third(g, 0)
                if a is not None:
                    for k in range(2):
                        act.wait_ge(x_pq, at(a, 2, k + 1))
                        nc.scalar.activation(xq_t[:, par, 2 * k:2 * k + 2].rearrange("p c t -> p (c t)"), pb[:, 4 + k],
                                             ACT.Copy, scale=DH ** -0.5).then_inc(x_cq, 1)
                split_third(g, 1)
                if b is not None:
                    x_exps(b, 2)
                    x_probs_copy(b, 0)
                split_third(g, 2)
                if b is not None:
                    x_exps(b, 3)
                    x_probs_copy(b, 1)
                if a is not None:
                    act.wait_ge(x_pk, at(a, 1, 1))
                    nc.scalar.activation(xk_t[:, par], pb[:, 6].rearrange("p (c n) -> p c n", c=IC)[:, :, 0:CTX],
                                         ACT.Copy).then_inc(x_ck, 1)
                    act.wait_ge(x_pv, at(a, 1, 1))
                    nc.scalar.activation(x_v[0:CTX, par], pb[0:CTX, 7], ACT.Copy).then_inc(x_cv, 1)
                if b is not None:
                    x_probs_copy(b, 2)
                    x_probs_copy(b, 3)
                    act.wait_ge(x_av, at(b, XUNITS, XUNITS))
                    for k in range(2):
                        nc.scalar.activation(xo_hi_t[:, 2 * k:2 * k + 2].rearrange("p c t -> p (c t)"), pb[:, 6 + k],
                                             ACT.Copy).then_inc(x_ohi, 1)
                if a is not None and not (isinstance(a, int) and a == SEQS - 1):
                    x_turned(plus(a, 1))
                if isinstance(g, int) and g == 0:
                    act.wait_ge(raw_b_in, 32)
                    split_hi("wo0", raw_b[:, 0:IC * D].rearrange("p (c n) -> p c n", c=IC), wo_hi[:])
                    split_hi("w20", raw_b[:, IC * D:].rearrange("p (c n) -> p c n", c=FC), w2_hi[:])

            x_iterations(act, run_x)


            def x_hi(n):
                act.wait_ge(pe_xt, at(n, 1, 1))
                dst = shifted(xt_hi)
                nc.scalar.activation(dst, pb[:, 4].rearrange("p (c t) -> p c t", c=KC), ACT.Copy).then_inc(act_xhi, 1)

            def gelu(c, m, layer):
                ly = layer_of(c, layer)
                act.wait_ge(pe_w1, at(c, FC, m + 1))
                if m >= 3 or later(c):
                    act.wait_ge(dve_hg, at(c, FC, m - 2))
                w = W1_BANK[m]
                if m < FC - 1:
                    e = nc.scalar.activation(gl[:, m % 3], pb[:, w, T:2 * T], ACT.Gelu, bias=b1_t[:, ly, 1, m:m + 1])
                else:
                    e = nc.scalar.activation(gl[0:TAIL, m % 3], pb[TAIL_G:TAIL_G + TAIL, w, 0:T], ACT.Gelu,
                                             bias=b1_t[TAIL_G:TAIL_G + TAIL, ly, 1, m:m + 1])
                e.then_inc(act_gelu, 1)

            def probs_copy(b, u):
                act.wait_ge(pe_pt, at(b, UNITS, u + 1))
                if u >= 2 or later(b):
                    act.wait_ge(pe_av, at(b, UNITS, u - 1))
                nc.scalar.activation(pt_t[:, u % 2], pb[:, 3 + u % 2], ACT.Copy).then_inc(act_pt, 1)

            def exps(b, j):
                heads = 2 if j < 4 else 4
                keys = 512 // heads
                act.wait_ge(dve_max, at(b, UNITS, j + 1))
                for k in range(heads):
                    pu = p_t[:, j % 3, k * keys:k * keys + keys]
                    e = nc.scalar.activation(pu, pu, ACT.Exp, bias=s_nm[:, j, k:k + 1], scale=-1.0,
                                             accum_out=s_sum[:, j, k:k + 1])
                e.then_inc(act_exp, 1)

            def run_l(g, layer=None):
                a, b, c, par = l_roles(g)
                if a is not None:
                    for n, (t, parts) in enumerate(QK_PARTS):
                        act.wait_ge(pe_qkv, at(a, 6, 2 * t + parts.stop))
                        if later(a):
                            act.wait_ge(dve_ss, at(plus(a, -1), NT, t + 1))
                        nc.scalar.activation(
                            qk_sq[:, t, parts.start * INNER:parts.stop * INNER].rearrange("p (j n) -> p j n", n=INNER),
                            pb[:, 3 * t + parts.start:3 * t + parts.stop], ACT.Square).then_inc(act_sq, 1)
                if a is not None:
                    for t in range(NT):
                        act.wait_ge(pe_qkv, at(a, 6, 5 + t))
                        nc.scalar.activation(v_t[:, par, t], pb[:, 2 + 3 * t], ACT.Copy).then_inc(act_v, 1)
                if c is not None:
                    act.wait_ge(pe_ht, at(c, 1, 1))
                    ly = layer_of(c, layer)
                    for k in range(KC):
                        nc.scalar.activation(h_f[:, k], pb[:, 7, k * T:k * T + T], ACT.Identity,
                                             bias=lnb_t[:, ly, k:k + 1], scale=lng_t[:, ly, k:k + 1]).then_inc(act_h, 1)
                if b is not None:
                    exps(b, 0)
                    exps(b, 1)
                if c is not None:
                    for m in range(FC):
                        gelu(c, m, layer)
                        if isinstance(g, int) and g == SEQS - 1 and m < 3:
                            act.wait_ge(raw_a_in, 80)
                            act.wait_ge(pe_qkv, 6 * SEQS)
                            cols = slice(m * INNER, m * INNER + INNER)
                            e = nc.scalar.activation(wqkv_hi[:, :, cols],
                                                     raw_a[:].rearrange("p (c n) -> p c n", c=KC)[:, :, cols], ACT.Copy)
                            if m == 2:
                                e.then_inc(w_hi, 1)
                        if isinstance(g, int) and g == SEQS + 1 and m == 0:
                            act.wait_ge(raw_b_in, 64)
                            act.wait_ge(pe_wo, SEQS)
                            split_hi("wo1", raw_b[:, 0:IC * D].rearrange("p (c n) -> p c n", c=IC), wo_hi[:])
                        if isinstance(g, int) and g == SEQS + 2 and m == 0:
                            act.wait_ge(pe_w2, SEQS)
                            split_hi("w21", raw_b[:, IC * D:].rearrange("p (c n) -> p c n", c=FC), w2_hi[:])
                if b is not None:
                    probs_copy(b, 0)
                    exps(b, 2)
                    probs_copy(b, 1)
                    exps(b, 3)
                    probs_copy(b, 2)
                    exps(b, 4)
                    exps(b, 5)
                    for u in range(3, UNITS):
                        probs_copy(b, u)
                    act.wait_ge(pe_av, at(b, UNITS, UNITS))
                    for k in range(2):
                        nc.scalar.activation(o_hi[:, 2 * k:2 * k + 2].rearrange("p c t -> p (c t)"), pb[:, 5 + k],
                                             ACT.Copy).then_inc(act_ohi, 1)
                if a is not None:
                    for k in range(4):
                        act.wait_ge(pe_qkt, at(a, 4, k + 1))
                        nc.scalar.activation(qk_t[:, k // 2, 2 * (k % 2):2 * (k % 2) + 2].rearrange("p c t -> p (c t)"),
                                             pb[:, k], ACT.Copy).then_inc(act_qkt, 1)
                    if not (isinstance(a, int) and a == ITEMS - 1):
                        x_hi(plus(a, 1))

            def between(g):
                if g == 0:
                    x_hi(0)
                elif g == SEQS + 2:
                    act.wait_ge(raw_a_in, 96)
                    act.wait_ge(pe_w1, FC * SEQS)
                    split_hi("w11", raw_a[:, 0:KC * W1C * P].rearrange("p (c m n) -> p c m n", c=KC, n=P), w1_hi[:])

            l_iterations(act, run_l, between)

        @block.vector
        def _(dve):
            def split_lo(name, src, hi, lo):
                dve.wait_ge(w_hi, WEIGHT[name])
                nc.vector.tensor_tensor(lo, src, hi.bitcast(F32), ALU.subtract).then_inc(w_lo, 1)

            def aggregate(mean_var, stats, s_stats, s_out, n):
                dve.wait_ge(s_stats, at(n, 1, 1))
                dve.sem_inc(stats_seen, 1)
                for t in range(NT):
                    e = nc.vector.bn_aggr(mean_var[:, t], stats[:, t])
                e.then_inc(s_out, 1)

            def x_lo(n):
                dve.wait_ge(act_xhi, at(n, 1, 1))
                nc.vector.tensor_tensor(shifted(xt_lo), pb[:, 4].rearrange("p (c t) -> p c t", c=KC),
                                        shifted(xt_hi).bitcast(F32), ALU.subtract).then_inc(dve_xlo, 1)

            def x_stats(a, par):
                dve.wait_ge(x_load[par], of_parity(a))
                for t in range(NT):
                    e = nc.vector.bn_stats(x_st[:, 0, t], x_in[:, par, t])
                e.then_inc(x_bst, 1)
                aggregate(x_mv[:, 0], x_st[:, 0], x_bst, x_bmv, a)

            def x_normed(a, par):
                dve.wait_ge(x_rst, at(a, 1, 1))
                dve.wait_ge(x_bmv, at(a, 1, 1))
                if later(a):
                    dve.wait_ge(x_tr, at(plus(a, -1), 1, 1))
                for t in range(NT):
                    e = nc.vector.tensor_scalar(xn[:, t], x_in[:, par, t], x_mv[:, 0, t, 0:1], x_rs[:, 0, t:t + 1],
                                                ALU.subtract, ALU.mult)
                e.then_inc(x_norm, 1)

            def x_turned_lo(a):
                dve.wait_ge(x_thi, at(a, 1, 1))
                nc.vector.tensor_tensor(xn_lo[:].rearrange("p c t -> p (c t)"), pb[:, 0],
                                        xn_hi[:].rearrange("p c t -> p (c t)").bitcast(F32),
                                        ALU.subtract).then_inc(x_tlo, 1)

            def x_maxes(b, u):
                dve.wait_ge(x_s, at(b, XUNITS, u + 1))
                nc.vector.tensor_reduce(x_nm[:, u], pb[:, 2 + u % 2].rearrange("p (k n) -> p k n", k=4)[:, :, 0:CTX],
                                        AX.X, ALU.max, negate=True).then_inc(x_max, 1)

            def x_norm_probs(b, u):
                dve.wait_ge(x_exp, at(b, XUNITS, u + 1))
                nc.vector.reciprocal(x_inv[:, u], x_sum[:, u]).then_inc(x_rec, 1)
                dve.wait_ge(x_rec, at(b, XUNITS, u + 1))
                nc.vector.tensor_tensor(x_p[:, u], x_p[:, u], x_inv[:, u].unsqueeze(2).broadcast_to([P, 4, CTX]),
                                        ALU.mult).then_inc(x_pn, 1)

            def run_x(g):
                a, b, d, par = x_roles(g)
                ahead = a is not None and not (isinstance(a, int) and a == SEQS - 1)
                if isinstance(g, int) and g == 0:
                    x_stats(0, 0)
                    x_normed(0, 0)
                    split_lo("xq", raw_a[:, 0:KC * INNER].rearrange("p (c n) -> p c n", c=KC), xq_hi[:], xq_lo[:])
                    x_turned_lo(0)
                    split_lo("xo", raw_a[:, KC * INNER:KC * INNER + IC * D].rearrange("p (c n) -> p c n", c=IC), xo_hi[:],
                             xo_lo[:])
                if b is not None:
                    x_maxes(b, 0)
                    x_maxes(b, 1)
                    x_norm_probs(b, 0)
                    x_norm_probs(b, 1)
                if isinstance(g, int) and g == SEQS + 1:
                    x_lo(0)
                if d is not None:
                    dve.wait_ge(x_wo, at(d, 1, 1))
                    dve.wait_ge(x_bias, at(d, 1, 1))
                    if later(d):
                        dve.wait_ge(x1_store, at(plus(d, -1), 16, 16))
                    nc.vector.tensor_tensor(x1_x[:].rearrange("p t d -> p (t d)"), pb[:, 1],
                                            x_b[:, par].rearrange("p t d -> p (t d)"), ALU.add).then_inc(x_res1, 1)
                    dve.wait_ge(x_res1, at(d, 1, 1))
                    for t in range(NT):
                        e = nc.vector.bn_stats(x_st[:, 1, t], x1_x[:, t])
                    e.then_inc(y_bst, 1)
                    aggregate(x_mv[:, 1], x_st[:, 1], y_bst, y_bmv, d)
                if ahead:
                    x_stats(plus(a, 1), 1 - par)
                if b is not None:
                    x_maxes(b, 2)
                    x_maxes(b, 3)
                if d is not None:
                    dve.wait_ge(y_rst, at(d, 1, 1))
                    dve.wait_ge(y_bmv, at(d, 1, 1))
                    if later(d):
                        dve.wait_ge(y_store, at(plus(d, -1), 16, 16))
                    for t in range(NT):
                        e = nc.vector.tensor_scalar(y_x[:, t], x1_x[:, t], x_mv[:, 1, t, 0:1], x_rs[:, 1, t:t + 1],
                                                    ALU.subtract, ALU.mult)
                    e.then_inc(y_norm, 1)
                if b is not None:
                    x_norm_probs(b, 2)
                if ahead:
                    x_normed(plus(a, 1), 1 - par)
                if b is not None:
                    x_norm_probs(b, 3)
                if isinstance(g, int) and g == 1:
                    split_lo("qkv0", raw_a[:].rearrange("p (c n) -> p c n", c=KC), wqkv_hi[:], wqkv_lo[:])
                if isinstance(g, int) and g == 2:
                    split_lo("w10", raw_a[:, 0:KC * W1C * P].rearrange("p (c m n) -> p c (m n)", c=KC, n=P),
                             w1_hi[:].rearrange("p c m n -> p c (m n)"), w1_lo[:].rearrange("p c m n -> p c (m n)"))
                if b is not None:
                    for k in range(2):
                        dve.wait_ge(x_ohi, at(b, 2, k + 1))
                        hi = xo_hi_t[:, 2 * k:2 * k + 2].rearrange("p c t -> p (c t)")
                        nc.vector.tensor_tensor(xo_lo_t[:, 2 * k:2 * k + 2].rearrange("p c t -> p (c t)"), pb[:, 6 + k],
                                                hi.bitcast(F32), ALU.subtract).then_inc(x_olo, 1)
                if ahead:
                    x_turned_lo(plus(a, 1))
                if isinstance(g, int) and g == 0:
                    dve.wait_ge(const_in, CONSTS)
                    for layer in range(LAYERS):
                        for j, tab in enumerate((cos_t, sin_t)):
                            nc.vector.tensor_tensor(
                                tab[:, layer].rearrange("p t j d -> p t (j d)"),
                                rope_raw[:, j].rearrange("p t j d -> p t (j d)"),
                                sc_t[:, layer, j].rearrange("p j d -> p (j d)").unsqueeze(1).broadcast_to([P, NT, 2 * DH]),
                                ALU.mult).then_inc(const_made, 1)
                    split_lo("wo0", raw_b[:, 0:IC * D].rearrange("p (c n) -> p c n", c=IC), wo_hi[:], wo_lo[:])
                    split_lo("w20", raw_b[:, IC * D:].rearrange("p (c n) -> p c n", c=FC), w2_hi[:], w2_lo[:])

            x_iterations(dve, run_x)


            def residual(c):
                dve.wait_ge(pe_wo, at(c, 1, 1))
                dve.wait_ge(res_load, at(c, 16, 16))
                if later(c):
                    dve.wait_ge(pool_x1b, at(plus(c, -1), 1, 1))
                nc.vector.tensor_tensor(x1[:, :, 0:3:2], pb[:, 7].rearrange("p (t c n) -> p t c n", t=NT, c=KC),
                                        x_res[:].rearrange("p t (c n) -> p t c n", c=KC), ALU.add).then_inc(dve_x1, 1)

            def stats_h(c):
                dve.wait_ge(shift, at(c, 32, 32))
                for t in range(NT):
                    e = nc.vector.bn_stats(l_st[:, t], x1[:, t, 0:2].rearrange("p c n -> p (c n)"))
                e.then_inc(dve_bst, 1)
                aggregate(l_mv, l_st, dve_bst, dve_bmv, c)

            def norm_h(c):
                dve.wait_ge(pool_rst, at(c, 1, 1))
                dve.wait_ge(dve_bmv, at(c, 1, 1))
                for t in range(NT):
                    e = nc.vector.tensor_scalar(h_n[:, t], x1[:, t, 0:2].rearrange("p c n -> p (c n)"), l_mv[:, t, 0:1],
                                                l_rs[:, t:t + 1], ALU.subtract, ALU.mult)
                e.then_inc(dve_h, 1)

            def split_h(c):
                dve.wait_ge(act_h, at(c, KC, KC))
                flat = lambda t: t[:].rearrange("p c t -> p (c t)")
                nc.vector.tensor_copy(flat(h_hi), flat(h_f)).then_inc(dve_hhi, 1)
                dve.wait_ge(dve_hhi, at(c, 1, 1))
                nc.vector.tensor_tensor(flat(h_lo), flat(h_f), flat(h_hi).bitcast(F32), ALU.subtract).then_inc(dve_hlo, 1)

            def squares(a, t):
                nc.vector.tensor_reduce(n_sq[:, t], qk_sq[:, t].rearrange("p (h d) -> p h d", d=DH), AX.X,
                                        ALU.add).then_inc(dve_ss, 1)
                dve.wait_ge(dve_ss, at(a, NT, t + 1))
                nc.vector.tensor_scalar(n_cl[:, t], n_sq[:, t], NORM_MIN_SQ, None, ALU.max).then_inc(dve_cl, 1)

            def rotate_cos(a, t, layer):
                ly = layer_of(a, layer)
                for n, (tile, parts) in enumerate(QK_PARTS):
                    if tile == t:
                        dve.wait_ge(act_sq, at(a, len(QK_PARTS), n + 1))
                        nc.vector.tensor_tensor(
                            r_cos[:, t, parts.start * INNER:parts.stop * INNER].rearrange(
                                "p (j h d) -> p j h d", h=HEADS, d=DH),
                            pb[:, 3 * t + parts.start:3 * t + parts.stop].rearrange("p j (h d) -> p j h d", d=DH),
                            cos_t[:, ly, t, parts].unsqueeze(2).broadcast_to([P, parts.stop - parts.start, HEADS, DH]),
                            ALU.mult)

            def rotate_sin(a, t, layer):
                ly = layer_of(a, layer)
                half = DH // 2
                qk = pb[:, 3 * t:3 * t + 2].rearrange("p j (h d) -> p j h d", d=DH)
                for s in range(2):
                    o = r_sin[:, t].rearrange("p (j h d) -> p j h d", j=2, d=DH)[:, :, :, s * half:s * half + half]
                    i = qk[:, :, :, half - s * half:DH - s * half]
                    w = sin_t[:, ly, t, :, s * half:s * half + half].unsqueeze(2).broadcast_to([P, 2, HEADS, half])
                    e = nc.vector.tensor_tensor(o, i, w, ALU.mult)
                e.then_inc(dve_rope, 1)

            def maxes(b, j):
                heads = 2 if j < 4 else 4
                keys = 512 // heads
                m = mask_t[:].rearrange("p a n -> p (a n)")[:, 2 * P - keys:]
                dve.wait_ge(pe_s, at(b, UNITS, j + 1))
                if j >= 3 or later(b):
                    dve.wait_ge(pe_pt, at(b, UNITS, j - 2))
                dve.sem_inc(scores_seen, 1)
                for k in range(heads):
                    e = nc.vector.tensor_tensor_reduce(p_t[:, j % 3, k * keys:k * keys + keys],
                                                       pb[:, S_BANK[j], k * keys:k * keys + keys], m, -1.0, FAR, ALU.add,
                                                       ALU.min, s_nm[:, j, k:k + 1])
                e.then_inc(dve_max, 1)

            def norm_probs(b, u):
                heads = 2 if u < 4 else 4
                dve.wait_ge(act_exp, at(b, UNITS, u + 1))
                nc.vector.reciprocal(s_inv[:, u, 0:heads], s_sum[:, u, 0:heads]).then_inc(dve_rec, 1)
                dve.wait_ge(dve_rec, at(b, UNITS, u + 1))
                pu = p_t[:, u % 3].rearrange("p (k n) -> p k n", k=heads)
                nc.vector.tensor_tensor(pu, pu, s_inv[:, u, 0:heads].unsqueeze(2).broadcast_to(
                    [P, heads, 512 // heads]), ALU.mult).then_inc(dve_pn, 1)

            def gate(c, m, layer):
                ly = layer_of(c, layer)
                rows = P if m < FC - 1 else TAIL
                dve.wait_ge(act_gelu, at(c, FC, m + 1))
                if m == 0 and later(c):
                    dve.wait_ge(pool_hglo, at(plus(c, -1), FC, FC))
                nc.vector.scalar_tensor_tensor(out=hg[0:rows, m], in0=pb[0:rows, W1_BANK[m], 0:T],
                                               scalar=b1_t[0:rows, ly, 0, m:m + 1], in1=gl[0:rows, m % 3],
                                               op0=ALU.add, op1=ALU.mult).then_inc(dve_hg, 1)

            def gate_hi(c, m):
                rows = P if m < FC - 1 else TAIL
                dve.wait_ge(dve_hg, at(c, FC, m + 1))
                nc.vector.tensor_copy(hg_hi[0:rows, m], hg[0:rows, m]).then_inc(dve_hghi, 1)

            def run_l(g, layer=None):
                a, b, c, par = l_roles(g)
                if c is not None:
                    residual(c)
                if isinstance(g, int) and g == SEQS + 2:
                    split_lo("w11", raw_a[:, 0:KC * W1C * P].rearrange("p (c m n) -> p c (m n)", c=KC, n=P),
                             w1_hi[:].rearrange("p c m n -> p c (m n)"), w1_lo[:].rearrange("p c m n -> p c (m n)"))
                if a is not None:
                    rotate_cos(a, 0, layer)
                if c is not None:
                    stats_h(c)
                if a is not None:
                    squares(a, 0)
                if c is not None:
                    norm_h(c)
                if a is not None:
                    rotate_sin(a, 0, layer)
                if c is not None:
                    split_h(c)
                if b is not None:
                    maxes(b, 0)
                    maxes(b, 1)
                if a is not None:
                    rotate_cos(a, 1, layer)
                    rotate_sin(a, 1, layer)
                if b is not None:
                    norm_probs(b, 0)
                for m in range(FC + 1):
                    if c is not None and m < FC:
                        gate(c, m, layer)
                    if c is not None and m >= 1:
                        gate_hi(c, m - 1)
                    if b is not None and m == 1:
                        norm_probs(b, 1)
                    if b is not None and m == 2:
                        maxes(b, 2)
                if isinstance(g, int) and g == SEQS + 2:
                    split_lo("w21", raw_b[:, IC * D:].rearrange("p (c n) -> p c n", c=FC), w2_hi[:], w2_lo[:])
                if b is not None:
                    maxes(b, 3)
                    norm_probs(b, 2)
                    maxes(b, 4)
                if a is not None:
                    squares(a, 1)
                if b is not None:
                    norm_probs(b, 3)
                    maxes(b, 5)
                    norm_probs(b, 4)
                    norm_probs(b, 5)
                if isinstance(g, int) and g == SEQS + 1:
                    split_lo("wo1", raw_b[:, 0:IC * D].rearrange("p (c n) -> p c n", c=IC), wo_hi[:], wo_lo[:])
                if isinstance(g, int) and g == SEQS - 1:
                    split_lo("qkv1", raw_a[:].rearrange("p (c n) -> p c n", c=KC), wqkv_hi[:], wqkv_lo[:])
                if c is not None:
                    dve.wait_ge(pe_w2, at(c, 1, 1))
                    dve.wait_ge(pool_x1b, at(c, 1, 1))
                    if not isinstance(c, int) or c >= 2:
                        dve.wait_ge(x2_store, at(plus(c, -2), 16, 16))
                    nc.vector.tensor_tensor(x2[:, par].rearrange("p t d -> p (t d)"), pb[:, 7],
                                            x1b[:].rearrange("p t d -> p (t d)"), ALU.add).then_inc(dve_x2, 1)
                    if layer_of(c, layer) == LAYERS - 1:
                        dve.wait_ge(dve_x2, at(c, 1, 1))
                        dve.wait_ge(orig_load, at(plus(c, -SEQS), 16, 16))
                        nc.vector.tensor_tensor(x2[:, par], x2[:, par], x_orig[:], ALU.add).then_inc(dve_out, 1)
                if b is not None:
                    for k in range(2):
                        dve.wait_ge(act_ohi, at(b, 2, k + 1))
                        hi = o_hi[:, 2 * k:2 * k + 2].rearrange("p c t -> p (c t)")
                        nc.vector.tensor_tensor(o_lo[:, 2 * k:2 * k + 2].rearrange("p c t -> p (c t)"), pb[:, 5 + k],
                                                hi.bitcast(F32), ALU.subtract).then_inc(dve_olo, 1)
                if a is not None and not (isinstance(a, int) and a == ITEMS - 1):
                    x_lo(plus(a, 1))

            def between(g):
                if g == 0:
                    dve.wait_ge(const_made, 2 * LAYERS)
                elif g == 2:
                    dve.wait_ge(zero_made, 2)

            l_iterations(dve, run_l, between)

        @block.gpsimd
        def _(pool):
            nc.gpsimd.memset(half_neg[:], -0.5)
            nc.gpsimd.memset(eps_t[:], EPS)
            nc.gpsimd.memset(xt_hi[:, T:T + 1].bitcast(F32), 0.0)
            nc.gpsimd.memset(xt_lo[:, T:T + 1].bitcast(F32), 0.0)
            nc.gpsimd.memset(c_in[:], 0.0).then_inc(zero_made, 1)

            def deviation(var, eps_out, out, n, s_in, s_in_v, s_eps, s_out):
                pool.wait_ge(s_in, s_in_v)
                nc.gpsimd.tensor_tensor(eps_out, var, eps_t[:], ALU.add).then_inc(s_eps, 1)
                pool.wait_ge(s_eps, at(n, 1, 1))
                nc.gpsimd.tensor_tensor(out, eps_out, half_neg[:, 0:NT], ALU.pow).then_inc(s_out, 1)

            def x_bias_rows(a, par):
                pool.wait_ge(x_load[par], of_parity(a))
                nc.gpsimd.tensor_tensor(x_b[:, par], x_in[:, par], bo_t[:].unsqueeze(1).broadcast_to([P, NT, D]),
                                        ALU.add).then_inc(x_bias, 1)

            def run_x(g):
                a, b, d, par = x_roles(g)
                ahead = a is not None and not (isinstance(a, int) and a == SEQS - 1)
                if isinstance(g, int) and g == 0:
                    deviation(x_mv[:, 0, :, 1], x_ve[:, 0], x_rs[:, 0], 0, x_bmv, 1, x_eps, x_rst)
                    pool.wait_ge(const_in, CONSTS)
                    x_bias_rows(0, 0)
                    x_bias_rows(1, 1)
                if d is not None:
                    deviation(x_mv[:, 1, :, 1], x_ve[:, 1], x_rs[:, 1], d, y_bmv, at(d, 1, 1), y_eps, y_rst)
                if ahead:
                    n = plus(a, 1)
                    deviation(x_mv[:, 0, :, 1], x_ve[:, 0], x_rs[:, 0], n, x_bmv, at(n, 1, 1), x_eps, x_rst)
                if d is not None and not (isinstance(d, int) and d >= SEQS - 2):
                    x_bias_rows(plus(d, 2), par)

            x_iterations(pool, run_x)

            nc.gpsimd.memset(x1[0:1, 0, 1], 0.0)
            nc.gpsimd.memset(hg_hi[:, FC - 1].bitcast(F32), 0.0)
            nc.gpsimd.memset(hg_lo[:, FC - 1].bitcast(F32), 0.0).then_inc(zero_made, 1)

            def inverse_norms(a, t):
                pool.wait_ge(dve_cl, at(a, NT, t + 1))
                nc.gpsimd.tensor_tensor(n_inv[:, t], n_cl[:, t], half_neg[:], ALU.pow).then_inc(pool_inv, 1)

            def add_parts(a, t):
                pool.wait_ge(dve_rope, at(a, NT, t + 1))
                nc.gpsimd.tensor_tensor(r_cos[:, t], r_cos[:, t], r_sin[:, t], ALU.add).then_inc(pool_sum, 1)

            def norm_qk(a, t):
                pool.wait_ge(pool_inv, at(a, NT, t + 1))
                pool.wait_ge(pool_sum, at(a, NT, t + 1))
                rows = r_cos[:, t].rearrange("p (h d) -> p h d", d=DH)
                nc.gpsimd.tensor_tensor(rows, rows, n_inv[:, t].unsqueeze(2).broadcast_to([P, 2 * HEADS, DH]),
                                        ALU.mult).then_inc(pool_qk, 1)

            def run_l(g, layer=None):
                a, b, c, par = l_roles(g)
                if c is not None:
                    ly = layer_of(c, layer)
                    pool.wait_ge(dve_x1, at(c, 1, 1))
                    if later(c):
                        pool.wait_ge(dve_x2, at(plus(c, -1), 1, 1))
                    nc.gpsimd.tensor_tensor(x1b[:].rearrange("p t (c n) -> p t c n", c=KC), x1[:, :, 0:3:2],
                                            b2_t[:, ly].rearrange("p (c n) -> p c n", c=KC).unsqueeze(1).broadcast_to(
                                                [P, NT, KC, P]), ALU.add).then_inc(pool_x1b, 1)
                    deviation(l_mv[:, :, 1], l_ve[:], l_rs[:], c, dve_bmv, at(c, 1, 1), pool_eps, pool_rst)
                if a is not None:
                    inverse_norms(a, 0)
                    add_parts(a, 0)
                    norm_qk(a, 0)
                    add_parts(a, 1)
                if c is not None:
                    for m in range(FC):
                        rows = P if m < FC - 1 else TAIL
                        pool.wait_ge(dve_hghi, at(c, FC, m + 1))
                        nc.gpsimd.tensor_tensor(hg_lo[0:rows, m], hg[0:rows, m], hg_hi[0:rows, m].bitcast(F32),
                                                ALU.subtract).then_inc(pool_hglo, 1)
                if a is not None:
                    inverse_norms(a, 1)
                    norm_qk(a, 1)

            l_iterations(pool, run_l, lambda g: None)


def kernel(x, ctx_768, L0_xattn_Wq, L0_xattn_Wk, L0_xattn_Wv, L0_xattn_Wo, L0_xattn_bo, L0_ffn_wqkv, L0_ffn_q_scale,
           L0_ffn_k_scale, L0_ffn_wo, L0_ffn_ln_g, L0_ffn_ln_b, L0_ffn_w1, L0_ffn_b1, L0_ffn_w2, L0_ffn_b2):
    import concourse.bacc as bacc
    from concourse.bass_utils import run_bass_kernel_spmd

    def rows_padded(w, rows):
        w = np.asarray(w)
        p = np.zeros(w.shape[:-2] + (rows,) + w.shape[-1:], w.dtype)
        p[..., :w.shape[-2], :] = w
        return p

    w1 = np.asarray(L0_ffn_w1)
    b1 = np.asarray(L0_ffn_b1)
    w1_p = np.zeros((LAYERS, D, W1C, P), w1.dtype)
    b1_p = np.zeros((LAYERS, P, 2, FC), b1.dtype)
    for m in range(FC):
        n = P if m < FC - 1 else TAIL
        for part in range(2):
            src = slice(part * HID + m * P, part * HID + m * P + n)
            chunk, to = (2 * m + part, 0) if m < FC - 1 else (W1C - 1, part * TAIL_G)
            w1_p[:, :, chunk, to:to + n] = w1[:, :, src]
            b1_p[:, to:to + n, part, m] = b1[:, src]
    by_channel = lambda v: np.ascontiguousarray(np.asarray(v).reshape(LAYERS, KC, P).transpose(0, 2, 1))

    arrays = {
        "x": np.asarray(x), "ctx": np.asarray(ctx_768),
        "xwq": np.asarray(L0_xattn_Wq), "xwk": rows_padded(L0_xattn_Wk, 2 * P), "xwv": rows_padded(L0_xattn_Wv, 2 * P),
        "xwo": np.asarray(L0_xattn_Wo), "xbo": np.asarray(L0_xattn_bo),
        "wqkv": np.asarray(L0_ffn_wqkv), "qsc": np.asarray(L0_ffn_q_scale), "ksc": np.asarray(L0_ffn_k_scale),
        "wo": np.asarray(L0_ffn_wo), "lng": by_channel(L0_ffn_ln_g), "lnb": by_channel(L0_ffn_ln_b),
        "w1": w1_p.reshape(LAYERS, D, W1C * P), "b1": b1_p,
        "w2": rows_padded(L0_ffn_w2, FC * P), "b2": np.asarray(L0_ffn_b2),
        "rope": rope_tables(), "mask": masks(), "ident": np.eye(P, dtype=np.float32),
    }
    nc = bacc.Bacc("TRN2", target_bir_lowering=False, num_devices=1)
    args = []
    for name, a in arrays.items():
        arrays[name] = a = np.ascontiguousarray(a)
        args.append(nc.dram_tensor(name, a.shape, mybir.dt.from_np(a.dtype), kind="ExternalInput").ap())
    args.append(nc.dram_tensor("out", (SEQS, T, D), F32, kind="ExternalOutput").ap())
    build(nc, *args)
    r = run_bass_kernel_spmd(nc, [arrays], core_ids=[0])
    return r.results[0]["out"]
```
